# Optimizing a Trainium2 kernel written in Bass

```python
import numpy as np
import jax
import jax.numpy as jnp

def _softmax(x, axis=-1):
    return jax.nn.softmax(x, axis=axis)

def _gelu(x):
    return jax.nn.gelu(x, approximate=True)

def _silu(x):
    return jax.nn.silu(x)

def _sigmoid(x):
    return jax.nn.sigmoid(x)

def _layernorm(x, axis=-1, eps=1e-05):
    m = jnp.mean(x, axis=axis, keepdims=True)
    v = jnp.var(x, axis=axis, keepdims=True)
    return (x - m) / jnp.sqrt(v + eps)

def _scatter_add(tgt, idx, src, axis=0):
    return tgt.at[idx].add(src)

def _segment_sum(src, seg, n):
    return jax.ops.segment_sum(src, seg, n)
kernel_name = 'mk_metaformer_d2_conv_nhwc256_r4_5b2418'

def setup_inputs(seed: int=0):
    np.random.seed(seed)
    _w = jnp.asarray

    def _rec_inputs():
        import jax
        import jax.numpy as jnp
        _gk = jax.random.key(seed)
        x = -0.0002023 + 1 * jax.random.normal(jax.random.fold_in(_gk, 1), (8, 56, 56, 64), jnp.float32)
        return x
    x = _rec_inputs()

    def _L0_conv_setup():
        import jax, jax.numpy as jnp
        import numpy as np
        GAMMA = 2.0
        EPS = 1e-12
        key = jax.random.key(seed)
        k1, k2 = jax.random.split(key)
        B, H, W_, C = (8, 56, 56, 64)
        x = jax.random.normal(k1, (B, H, W_, C), dtype=jnp.float32)
        W = jax.random.normal(k2, (C, C), dtype=jnp.float32) * 0.05
        return {'x': x, 'W': W}
    _L0_conv_all = _L0_conv_setup()
    _L0_conv_in = {k: v for k, v in _L0_conv_all.items() if k in ('W',)}
    del _L0_conv_all

    def _L0_ffn_setup():
        import jax, jax.numpy as jnp
        import numpy as np
        D_MODEL = 64
        N_EXPERTS = 16
        HIDDEN = 128
        SCALE = 0.02
        key = jax.random.key(seed)
        ks = jax.random.split(key, 5)
        x = jax.random.normal(ks[0], (4, 2048, D_MODEL), dtype=jnp.float32)
        gate_w = jax.random.normal(ks[1], (D_MODEL, N_EXPERTS), dtype=jnp.float32) * SCALE
        gate_b = jnp.zeros((N_EXPERTS,), dtype=jnp.float32)
        w1 = jax.random.normal(ks[2], (N_EXPERTS, D_MODEL, HIDDEN), dtype=jnp.float32) * SCALE
        w2 = jax.random.normal(ks[3], (N_EXPERTS, D_MODEL, HIDDEN), dtype=jnp.float32) * SCALE
        w3 = jax.random.normal(ks[4], (N_EXPERTS, HIDDEN, D_MODEL), dtype=jnp.float32) * SCALE
        return {'x': x, 'gate_w': gate_w, 'gate_b': gate_b, 'w1': w1, 'w2': w2, 'w3': w3}
    _L0_ffn_all = _L0_ffn_setup()
    _L0_ffn_in = {k: v for k, v in _L0_ffn_all.items() if k in ('gate_w', 'gate_b', 'w1', 'w2', 'w3')}
    del _L0_ffn_all

    def _L1_conv_setup():
        import jax, jax.numpy as jnp
        import numpy as np
        from jax import lax
        K_SIZE = 3
        STRIDE = 1
        PADDING = 1

        def _dcnv2(x, offset_w, offset_b, dcn_weight):
            k, stride, padding = (K_SIZE, STRIDE, PADDING)
            N, H, W, C = x.shape
            kk = k * k
            om = lax.conv_general_dilated(x, offset_w, window_strides=(stride, stride), padding='SAME', dimension_numbers=('NHWC', 'HWIO', 'NHWC')) + offset_b
            offset = om[..., :2 * kk]
            mask = jax.nn.sigmoid(om[..., 2 * kk:])
            oH = (H + 2 * padding - (k - 1)) // stride
            oW = (W + 2 * padding - (k - 1)) // stride
            pad_x = jnp.pad(x, ((0, 0), (padding, padding + 1), (padding, padding + 1), (0, 0)))
            base_y = jnp.arange(oH, dtype=x.dtype) * stride + padding
            base_x = jnp.arange(oW, dtype=x.dtype) * stride + padding
            kr = jnp.arange(k, dtype=x.dtype) - (k - 1) / 2.0
            inner_y = jnp.repeat(kr, k)
            inner_x = jnp.tile(kr, k)
            off_yx = offset.reshape(N, oH, oW, kk, 2)
            pos_y = base_y[None, :, None, None] + inner_y[None, None, None, :] + off_yx[..., 0]
            pos_x = base_x[None, None, :, None] + inner_x[None, None, None, :] + off_yx[..., 1]
            pos_y = jnp.clip(pos_y, 0.0, H + 2 * padding - 1.0)
            pos_x = jnp.clip(pos_x, 0.0, W + 2 * padding - 1.0)
            y1 = jnp.floor(pos_y)
            x1 = jnp.floor(pos_x)
            y1i = y1.astype(jnp.int32)
            x1i = x1.astype(jnp.int32)
            y2i = y1i + 1
            x2i = x1i + 1
            gather = jax.vmap(lambda px, yi, xi: px[yi, xi])
            v1 = gather(pad_x, y1i, x1i)
            v2 = gather(pad_x, y1i, x2i)
            v3 = gather(pad_x, y2i, x1i)
            v4 = gather(pad_x, y2i, x2i)
            lh = (pos_y - y1)[..., None]
            lw = (pos_x - x1)[..., None]
            hh = 1.0 - lh
            hw = 1.0 - lw
            value = (hh * hw * v1 + hh * lw * v2 + lh * hw * v3 + lh * lw * v4) * mask[..., None]
            value = jnp.transpose(value, (0, 1, 2, 4, 3)).reshape(N, oH, oW, C * kk)
            w = jnp.transpose(dcn_weight, (1, 2, 3, 0)).reshape(C * kk, -1)
            return jnp.einsum('nhwc,cf->nhwf', value, w)
        key = jax.random.key(seed)
        k1, k2, k3 = jax.random.split(key, 3)
        x = jax.random.normal(k1, (4, 16, 16, 64), dtype=jnp.float32)
        offset_w = jax.random.normal(k2, (3, 3, 64, 27), dtype=jnp.float32) * 0.01
        offset_b = jnp.zeros((1, 1, 1, 27), dtype=jnp.float32)
        dcn_weight = jax.random.normal(k3, (64, 64, 3, 3), dtype=jnp.float32) * 0.02
        return {'x': x, 'offset_w': offset_w, 'offset_b': offset_b, 'dcn_weight': dcn_weight}
    _L1_conv_all = _L1_conv_setup()
    _L1_conv_in = {k: v for k, v in _L1_conv_all.items() if k in ('offset_w', 'offset_b', 'dcn_weight')}
    del _L1_conv_all

    def _L1_ffn_setup():
        import jax, jax.numpy as jnp
        import numpy as np
        B, S, D = (8, 1024, 64)
        H = 4 * D
        CAPACITY = 0.5
        key = jax.random.key(seed)
        ks = jax.random.split(key, 6)
        x = jax.random.normal(ks[0], (B, S, D), dtype=jnp.float32)
        attention_mask = jnp.zeros((B, 1, 1, S), dtype=jnp.float32)
        wr = jax.random.normal(ks[1], (D, 1), dtype=jnp.float32) * 0.02
        br = jnp.zeros((1,), dtype=jnp.float32)
        w1 = jax.random.normal(ks[2], (D, H), dtype=jnp.float32) * 0.02
        b1 = jnp.zeros((H,), dtype=jnp.float32)
        w2 = jax.random.normal(ks[3], (H, D), dtype=jnp.float32) * 0.02
        b2 = jnp.zeros((D,), dtype=jnp.float32)
        return {'x': x, 'attention_mask': attention_mask, 'wr': wr, 'br': br, 'w1': w1, 'b1': b1, 'w2': w2, 'b2': b2}
    _L1_ffn_all = _L1_ffn_setup()
    _L1_ffn_in = {k: v for k, v in _L1_ffn_all.items() if k in ('attention_mask', 'wr', 'br', 'w1', 'b1', 'w2', 'b2')}
    del _L1_ffn_all
    return {'x': x, 'L0_conv_W': _L0_conv_in['W'], 'L0_ffn_gate_w': _L0_ffn_in['gate_w'], 'L0_ffn_gate_b': _L0_ffn_in['gate_b'], 'L0_ffn_w1': _L0_ffn_in['w1'], 'L0_ffn_w2': _L0_ffn_in['w2'], 'L0_ffn_w3': _L0_ffn_in['w3'], 'L1_conv_offset_w': _L1_conv_in['offset_w'], 'L1_conv_offset_b': _L1_conv_in['offset_b'], 'L1_conv_dcn_weight': _L1_conv_in['dcn_weight'], 'L1_ffn_attention_mask': _L1_ffn_in['attention_mask'], 'L1_ffn_wr': _L1_ffn_in['wr'], 'L1_ffn_br': _L1_ffn_in['br'], 'L1_ffn_w1': _L1_ffn_in['w1'], 'L1_ffn_b1': _L1_ffn_in['b1'], 'L1_ffn_w2': _L1_ffn_in['w2'], 'L1_ffn_b2': _L1_ffn_in['b2']}

def reference(x, L0_conv_W, L0_ffn_gate_w, L0_ffn_gate_b, L0_ffn_w1, L0_ffn_w2, L0_ffn_w3, L1_conv_offset_w, L1_conv_offset_b, L1_conv_dcn_weight, L1_ffn_attention_mask, L1_ffn_wr, L1_ffn_br, L1_ffn_w1, L1_ffn_b1, L1_ffn_w2, L1_ffn_b2):
    import jax
    import jax.numpy as jnp

    def _L0_conv_ref(x, W):
        import jax, jax.numpy as jnp
        import numpy as np
        GAMMA = 2.0
        EPS = 1e-12
        B, H, Wd, C = x.shape
        hw = H * Wd
        t = jnp.einsum('bhwc,cd->bhwd', x, W).reshape(B, hw, C)
        xf = x.reshape(B, hw, C)
        inv_norm = jax.lax.rsqrt(jnp.maximum(jnp.sum(xf * xf, axis=-1, keepdims=True), EPS))
        xn = xf * inv_norm
        sim = jnp.einsum('bic,bjc->bij', xn, xn)
        sim = jnp.power(jax.nn.relu(sim), GAMMA)
        y = jnp.einsum('bij,bjc->bic', sim, t)
        return y.reshape(B, H, Wd, C)

    def _L0_ffn_ref(x, gate_w, gate_b, w1, w2, w3):
        import jax, jax.numpy as jnp
        import numpy as np
        D_MODEL = 64
        N_EXPERTS = 16
        HIDDEN = 128
        SCALE = 0.02
        n_experts = w1.shape[0]
        logits = jnp.einsum('bsd,de->bse', x, gate_w) + gate_b
        probs = jax.nn.softmax(logits, axis=-1)
        top_probs, top_idx = jax.lax.top_k(probs, 2)
        top_probs = top_probs / jnp.sum(top_probs, axis=-1, keepdims=True)
        dispatch = jnp.sum(jax.nn.one_hot(top_idx, n_experts, dtype=x.dtype) * top_probs[..., None], axis=-2)
        h1 = jnp.einsum('bsd,edh->bseh', x, w1)
        h2 = jnp.einsum('bsd,edh->bseh', x, w2)
        hidden = jax.nn.silu(h1) * h2
        expert_out = jnp.einsum('bseh,eho->bseo', hidden, w3)
        return jnp.einsum('bseo,bse->bso', expert_out, dispatch)

    def _L1_conv_ref(x, offset_w, offset_b, dcn_weight):
        import jax, jax.numpy as jnp
        import numpy as np
        from jax import lax
        K_SIZE = 3
        STRIDE = 1
        PADDING = 1

        def _dcnv2(x, offset_w, offset_b, dcn_weight):
            k, stride, padding = (K_SIZE, STRIDE, PADDING)
            N, H, W, C = x.shape
            kk = k * k
            om = lax.conv_general_dilated(x, offset_w, window_strides=(stride, stride), padding='SAME', dimension_numbers=('NHWC', 'HWIO', 'NHWC')) + offset_b
            offset = om[..., :2 * kk]
            mask = jax.nn.sigmoid(om[..., 2 * kk:])
            oH = (H + 2 * padding - (k - 1)) // stride
            oW = (W + 2 * padding - (k - 1)) // stride
            pad_x = jnp.pad(x, ((0, 0), (padding, padding + 1), (padding, padding + 1), (0, 0)))
            base_y = jnp.arange(oH, dtype=x.dtype) * stride + padding
            base_x = jnp.arange(oW, dtype=x.dtype) * stride + padding
            kr = jnp.arange(k, dtype=x.dtype) - (k - 1) / 2.0
            inner_y = jnp.repeat(kr, k)
            inner_x = jnp.tile(kr, k)
            off_yx = offset.reshape(N, oH, oW, kk, 2)
            pos_y = base_y[None, :, None, None] + inner_y[None, None, None, :] + off_yx[..., 0]
            pos_x = base_x[None, None, :, None] + inner_x[None, None, None, :] + off_yx[..., 1]
            pos_y = jnp.clip(pos_y, 0.0, H + 2 * padding - 1.0)
            pos_x = jnp.clip(pos_x, 0.0, W + 2 * padding - 1.0)
            y1 = jnp.floor(pos_y)
            x1 = jnp.floor(pos_x)
            y1i = y1.astype(jnp.int32)
            x1i = x1.astype(jnp.int32)
            y2i = y1i + 1
            x2i = x1i + 1
            gather = jax.vmap(lambda px, yi, xi: px[yi, xi])
            v1 = gather(pad_x, y1i, x1i)
            v2 = gather(pad_x, y1i, x2i)
            v3 = gather(pad_x, y2i, x1i)
            v4 = gather(pad_x, y2i, x2i)
            lh = (pos_y - y1)[..., None]
            lw = (pos_x - x1)[..., None]
            hh = 1.0 - lh
            hw = 1.0 - lw
            value = (hh * hw * v1 + hh * lw * v2 + lh * hw * v3 + lh * lw * v4) * mask[..., None]
            value = jnp.transpose(value, (0, 1, 2, 4, 3)).reshape(N, oH, oW, C * kk)
            w = jnp.transpose(dcn_weight, (1, 2, 3, 0)).reshape(C * kk, -1)
            return jnp.einsum('nhwc,cf->nhwf', value, w)
        return _dcnv2(x, offset_w, offset_b, dcn_weight)

    def _L1_ffn_ref(x, attention_mask, wr, br, w1, b1, w2, b2):
        import jax, jax.numpy as jnp
        import numpy as np
        B, S, D = (8, 1024, 64)
        H = 4 * D
        CAPACITY = 0.5
        b, s, d = x.shape
        weights = (jnp.einsum('bsd,do->bso', x, wr) + br)[..., 0]
        k = max(1, int(CAPACITY * s))
        kk = k - 1 if k > 1 else 1
        _, idx = jax.lax.top_k(weights, k)
        sel_idx = idx[:, :kk]
        sel = jnp.take_along_axis(x, sel_idx[:, :, None], axis=1)
        h = jax.nn.gelu(jnp.einsum('bkd,dh->bkh', sel, w1) + b1)
        y = jnp.einsum('bkh,hd->bkd', h, w2) + b2
        w_sel = jnp.take_along_axis(weights, sel_idx, axis=1)
        y = y * w_sel[..., None]
        batch_idx = jnp.arange(b)[:, None]
        processed = jnp.zeros_like(x).at[batch_idx, sel_idx].set(y)
        return processed + x

    def _gn(v, G=32, eps=1e-05):
        B_, H_, W_, C_ = v.shape
        g = v.reshape(B_, H_, W_, G, C_ // G)
        m = jnp.mean(g, axis=(1, 2, 4), keepdims=True)
        s = jnp.var(g, axis=(1, 2, 4), keepdims=True)
        return ((g - m) / jnp.sqrt(s + eps)).reshape(v.shape)

    def _ln_c(v, eps=1e-06):
        m = jnp.mean(v, axis=-1, keepdims=True)
        s = jnp.var(v, axis=-1, keepdims=True)
        return (v - m) / jnp.sqrt(s + eps)

    def _ln_t(v, eps=1e-05):
        m = jnp.mean(v, axis=-1, keepdims=True)
        s = jnp.var(v, axis=-1, keepdims=True)
        return (v - m) / jnp.sqrt(s + eps)

    def _to_tokens(v):
        B_, H_, W_, C_ = v.shape
        return v.reshape(B_, H_ * W_, C_)

    def _from_tokens(t, like):
        return t.reshape(like.shape)
    x = x + _L0_conv_ref(_ln_c(x), L0_conv_W)
    t = _to_tokens(x)
    t = t + _L0_ffn_ref(_ln_t(t), L0_ffn_gate_w, L0_ffn_gate_b, L0_ffn_w1, L0_ffn_w2, L0_ffn_w3)
    x = _from_tokens(t, x)
    x = x + _L1_conv_ref(_ln_c(x), L1_conv_offset_w, L1_conv_offset_b, L1_conv_dcn_weight)
    t = _to_tokens(x)
    t = t + _L1_ffn_ref(_ln_t(t), L1_ffn_attention_mask, L1_ffn_wr, L1_ffn_br, L1_ffn_w1, L1_ffn_b1, L1_ffn_w2, L1_ffn_b2)
    x = _from_tokens(t, x)
    return x

_drawn_inputs = setup_inputs


def setup_inputs(seed=0):
    import zlib

    import numpy as np

    out = dict(_drawn_inputs(seed))
    spreads = {'L0_ffn_gate_b': (0.0, 0.8),
     'L1_conv_offset_b': (0.0, 0.482),
     'L1_ffn_b1': (0.0, 0.8),
     'L1_ffn_b2': (0.0, 0.8)}
    factors = {'L0_ffn_gate_w': 8.0,
     'L0_ffn_w1': 8.0,
     'L0_ffn_w2': 8.0,
     'L0_ffn_w3': 8.0,
     'L1_ffn_wr': 8.0,
     'L1_ffn_w1': 8.0,
     'L1_ffn_w2': 8.0}
    for name, (base, spread) in spreads.items():
        noise = np.random.default_rng([zlib.crc32(name.encode()), seed]).standard_normal(out[name].shape)
        drawn = base * np.exp(spread * noise) if base else spread * noise
        out[name] = jnp.asarray(drawn.astype(out[name].dtype))
    for name, factor in factors.items():
        out[name] = (out[name] * factor).astype(out[name].dtype)
    return out
```

```python
from contextlib import ExitStack

import numpy as np
import concourse.bass as bass
from concourse import mybir

ACT_STEPS = (1, 3, 4, 6, 7)


def metaformer_kernel(nc, x, conv_w, gate_w, gate_b, w1, w2, w3, off_w, off_b, dcn_w, wr, br, f1, fb1, f2, fb2,
                      ident_in, grid_in, rank_in, pick_in, tri_in, bits_in, out):
    f32, f16, i32, u32 = mybir.dt.float32, mybir.dt.float16, mybir.dt.int32, mybir.dt.uint32
    ALU, ACT, AX = mybir.AluOpType, mybir.ActivationFunctionType, mybir.AxisListType

    B, H, W, C = x.shape
    N = H * W
    TP = 2 * W
    T = N // TP
    E, HID = w1.shape[0], w1.shape[2]
    FH = f1.shape[1]
    TAPS = 9
    CT = 4
    CW = CT * TP
    NCH = T // CT
    IW = 392
    JB = 4
    SPB = 2 * JB
    BPH = T // JB
    SPH = SPB * BPH
    SPI = 2 * SPH
    OC = 32
    SIDE = W + 2
    XS = 256.0
    KTOP = int(0.5 * N) - 1
    LNC_EPS, LNT_EPS = 1e-6, 1e-5
    MOE1, MOE2, GATE, OFF, FFN1, ROUTE = range(6)
    NW = 6
    ACT_N = len(ACT_STEPS)
    DVE_STEPS = tuple(u for u in range(SPB) if u not in ACT_STEPS)
    DVE_N = len(DVE_STEPS)

    table = nc.dram_tensor("corner_table", [SIDE * SIDE, 4 * C], f32).ap()
    x3_dram = nc.dram_tensor("x3_scratch", [B, N, C], f32).ap()
    yw_dram = nc.dram_tensor("yw_scratch", [B, N, C], f32).ap()

    ctx = ExitStack()
    with ctx:
        def sb(name, shape, dt=f32):
            return ctx.enter_context(nc.sbuf_tensor(name, shape, dt))

        ident = sb("ident", [128, 128])
        ident2 = sb("ident2", [128, C])
        ident16 = sb("ident16", [TP, TP], f16)
        ones16 = sb("ones16", [TP, TP], f16)
        tri16 = sb("tri16", [TP, TP], f16)
        pick = sb("pick", [128, E * 128], f16)
        zero16 = sb("zero16", [128, IW], f16)
        grid = sb("grid", [TP, T, 2 * TAPS])
        rank = sb("rank", [TP, E])
        bits = sb("bits", [TP, 31], i32)
        w_mix = sb("w_mix", [C, C])
        w1h = sb("w1h", [128, E * HID], f16)
        w1l = sb("w1l", [128, E * HID], f16)
        w2h = sb("w2h", [128, E * HID], f16)
        w2l = sb("w2l", [128, E * HID], f16)
        w3s = sb("w3s", [HID, E, C])
        gateh = sb("gateh", [128, E], f16)
        gatel = sb("gatel", [128, E], f16)
        gbias = sb("gbias", [TP, E])
        offh = sb("offh", [128, TAPS * OC], f16)
        offl = sb("offl", [128, TAPS * OC], f16)
        obias = sb("obias", [TP, 27])
        dcn = sb("dcn", [128, 5, C])
        wrh = sb("wrh", [128, 2], f16)
        wrl = sb("wrl", [128, 2], f16)
        brc = sb("brc", [TP, 1])
        f1h = sb("f1h", [128, FH], f16)
        f1l = sb("f1l", [128, FH], f16)
        fb1c = sb("fb1c", [128, 2])
        f2s = sb("f2s", [128, 2, C])
        fb2r = sb("fb2r", [TP, C])
        amax = sb("amax", [128, NW])
        amin = sb("amin", [128, NW])
        amax_all = sb("amax_all", [128, NW])
        wscale = sb("wscale", [128, NW])
        descale = sb("descale", [128, NW])

        xin = sb("xin", [TP, T, C])
        xln = sb("xln", [TP, T, C])
        tmp = sb("tmp", [TP, T, C])
        x1 = sb("x1", [TP, T, C])
        xB = sb("xB", [TP, T, C])
        yw = sb("yw", [TP, T, C])
        st = sb("st", [TP, 8, T])
        split = sb("split", [TP, T, 4 * C], f16)
        xn_hl = sb("xn_hl", [128, N], f16)
        xn_hh = sb("xn_hh", [128, N], f16)
        xn_ll = sb("xn_ll", [128, N], f16)
        dT = xn_hh
        padded = sb("padded", [128, SIDE * SIDE], f16)
        pad_v = padded[:, :].rearrange("p (y x) -> p y x", x=SIDE)
        work = sb("work", [128, 8 * IW])
        relu = work[0:TP, 0:4 * IW].rearrange("p (q b n) -> p q b n", q=2, b=2)
        sq = work[0:TP, 4 * IW:8 * IW].rearrange("p (q b n) -> p q b n", q=2, b=2)
        silu = work[:, 0:2 * CW].rearrange("p (q n) -> p q n", q=2)
        hid = work[:, 2 * CW:6 * CW].rearrange("p (q n) -> p q n", q=4)
        xj = sb("xj", [TP, 2, JB, C])
        small = sb("small", [TP, 5, 2 * TAPS * T])
        z_cm = small[0:C, 0:4, :].rearrange("p a b -> p (a b)")[:, 0:4 * IW]
        smallc = sb("smallc", [TP, 8, T])
        disp = sb("disp", [TP, T, E])
        dsplit = sb("dsplit", [TP, T, 2 * E], f16)
        om = sb("om", [TP, T, OC])
        mask = sb("mask", [TP, T, TAPS])
        om_cm = sb("om_cm", [128, CW])
        om_c = (om_cm, silu[:, 0, :])
        corner_w = sb("corner_w", [TP, T * TAPS, 4])
        index = sb("index", [TP, T * TAPS], u32)
        pool_cell = sb("pool_cell", [TP, 5])
        index_now = sb("index_now", [TP, 2, TAPS], u32)
        G = sb("G", [128, 2, 4 * TAPS * C])
        stage, stage2 = G[:, 0, :], G[:, 1, :]
        val = sb("val", [TP, TAPS * C])
        val_cm = sb("val_cm", [128, 5 * TP])
        w_all = sb("w_all", [TP, B, T])
        key = small[:, 0, 0:B * T].rearrange("p (b t) -> p b t", b=B)
        hit = small[:, 1, 0:B * T].rearrange("p (b t) -> p b t", b=B)
        eqf = small[:, 2, 0:B * T].rearrange("p (b t) -> p b t", b=B)
        tot = small[:, 3, 0:B * T].rearrange("p (b t) -> p b t", b=B)
        pre = small[:, 4, 0:B * T].rearrange("p (b t) -> p b t", b=B)
        sel = sb("sel", [TP, B, T])
        eq16 = sb("eq16", [TP, B * T], f16)
        kf = sb("kf", [TP, 8, B])
        ki = sb("ki", [TP, 3, B], i32)
        cnt16 = sb("cnt16", [TP, B], f16)

        PS = [ctx.enter_context(nc.psum_tensor(f"PS{i}", [128, 2, 512], f32)) for i in range(4)]
        S = [PS[0][:, 0, :], PS[0][:, 1, :], PS[1][:, 0, :], PS[1][:, 1, :]]
        Y0, Y1, D0, D1 = PS[2][:, 0, :], PS[2][:, 1, :], PS[3][:, 0, :], PS[3][:, 1, :]

        s = {n: ctx.enter_context(nc.semaphore(n)) for n in """
            w_loaded w_staged w_taken amax_done amax_red stage_zero table_zeroed const_done
            x_loaded x1_added var_done std_done scaled h_cast split_done tr_done tr_cm
            sim_done relu_done sq_act sq_dve xj_ready z_done z_ready y_done
            logits_done sm_shift sm_exp disp_split disp_tr disp_cm
            up_done silu_done gate_done bcast_done hid_done ycm_done ycm_ready ytm_done x2_added
            geo_ln pad_ready om_done om_ready om_tr om_taken mask_in mask_out geo_done xb_copied
            table_written gath0 gath1 cell_done pool_step val_ready val_tr valcm_ready dcn_done x3_added
            route_done route_taken fup_done gelu_done fdown_done yw_done skip_added x3_stored yw_stored
            count_in count_done tie_in tie_done x3_back0 x3_back1 yw_back0 yw_back1 fin_ready out_stored0
            out_stored1""".split()}
        gath = (s["gath0"], s["gath1"])
        V, A, P, GP = nc.vector, nc.scalar, nc.tensor, nc.gpsimd
        block = ctx.enter_context(nc.Block())

        def bc(ap, axis, n):
            v = ap.unsqueeze(axis)
            shape = list(v.shape)
            shape[axis] = n
            return v.to_broadcast(shape)

        def tm_dram(t, k):
            return t[bass.ds(k, 1), :, :].rearrange("a (t p) c -> p (a t) c", p=TP)

        def round_of(k, which, backs=True):
            return 5 * k - (1 if backs else 0) * 0 + which

        @block.sync
        def _(sp):
            x_flat = x.rearrange("b h w c -> b (h w) c")

            def load_x(k):
                sp.dma_start(xin[:, :, :], tm_dram(x_flat, k)).then_inc(s["x_loaded"], 16)

            def write_table(k):
                sp.wait_ge(s["geo_ln"], k + 1)
                for slot, (dy, dx) in enumerate(((1, 1), (1, 0), (0, 1), (0, 0))):
                    tv = table.rearrange("(y x) (s c) -> x y s c", x=SIDE, c=C)
                    for r in range(2):
                        dst = tv[dx:dx + W, dy + r:dy + r + H, slot, :].rearrange("x (t two) c -> x t two c", two=2)[:, :, 0, :]
                        sp.dma_start(dst, xln[r * W:(r + 1) * W, :, :]).then_inc(s["table_written"], 16)

            def back_stores(b):
                sp.wait_ge(s["skip_added"], b + 1)
                sp.dma_start(tm_dram(x3_dram, b), xB[:, :, :]).then_inc(s["x3_stored"], 16)
                sp.wait_ge(s["yw_done"], (b + 1) * NCH)
                sp.dma_start(tm_dram(yw_dram, b), yw[:, :, :]).then_inc(s["yw_stored"], 16)

            load_x(0)
            loads = [(ident[:, :], ident_in), (ident2[0:C, :], ident_in[0:C, 0:C]), (ident2[C:128, :], ident_in[0:C, 0:C]),
                     (grid[:, :, :], grid_in), (rank[:, :], rank_in), (w_mix[:, :], conv_w),
                     (w3s[:, :, :], w3.rearrange("e h c -> h e c")),
                     (gbias[:, :], gate_b.to_broadcast([TP, E])), (obias[:, :], off_b.to_broadcast([TP, 27])),
                     (dcn[:, 0:4, :], dcn_w[0:512, :].rearrange("(n k) c -> k n c", k=128)),
                     (dcn[0:C, 4, :], dcn_w[512:576, :]),
                     (brc[:, :], br.to_broadcast([TP, 1])), (fb1c[:, :], fb1.rearrange("(m p) o -> p (m o)", p=128)),
                     (f2s[:, :, :], f2.rearrange("(m k) c -> k m c", m=2)),
                     (fb2r[:, :], fb2.to_broadcast([TP, C]))]
            with nc.allow_non_contiguous_dma(reason="small constants"):
                for dst, src in loads:
                    sp.dma_start(dst, src).then_inc(s["w_loaded"], 16)
            for w, dst in ((w1, stage), (w2, stage2)):
                for h in range(2):
                    sp.dma_start(dst[h * C:(h + 1) * C, 0:E * HID].rearrange("c (e h) -> c e h", e=E),
                                 w.rearrange("e c h -> c e h")).then_inc(s["w_staged"], 16)
            sp.wait_ge(s["w_taken"], 1)
            with nc.allow_non_contiguous_dma(reason="small weights"):
                for h in range(2):
                    r = slice(h * C, (h + 1) * C)
                    for dst, src in ((stage[r, 0:E], gate_w), (stage[r, 768:769], wr), (stage[r, 1024:1024 + FH], f1),
                                     (stage[r, 64:64 + TAPS * OC].rearrange("c (t o) -> c t o", o=OC)[:, :, 0:27],
                                      off_w.rearrange("(t c) o -> c t o", c=C))):
                        sp.dma_start(dst, src).then_inc(s["w_staged"], 16)
            sp.dma_start(stage2[0:TP, 0:TP], tri_in).then_inc(s["w_staged"], 16)
            sp.dma_start(stage2[0:TP, 128:159], bits_in).then_inc(s["w_staged"], 16)
            sp.wait_ge(s["w_taken"], 2)
            sp.dma_start(stage2[0:2 * E, 0:E * 128], pick_in).then_inc(s["w_staged"], 16)
            sp.wait_ge(s["stage_zero"], 1)
            tz = table.rearrange("e n -> (e n)").rearrange("(p n) -> p n", p=128)
            pieces = range(0, tz.shape[1], 1682)
            for a in pieces:
                sp.dma_start(tz[:, a:a + 1682], stage[:, 0:1682]).then_inc(s["table_zeroed"], 16)
            sp.wait_ge(s["table_zeroed"], 16 * len(pieces))

            def image(k, has_back, has_next):
                if has_next:
                    sp.wait_ge(s["x1_added"], 4 * (k + 1))
                    load_x(k + 1)
                if has_back:
                    back_stores(k - 1)
                write_table(k)

            image(0, False, True)
            with sp.Fori(1, B - 1) as k:
                image(k, True, True)
            image(B - 1, True, False)
            back_stores(B - 1)
            sp.wait_ge(s["x3_stored"], 16 * B)
            sp.wait_ge(s["yw_stored"], 16 * B)
            for k in range(B):
                q = k % 2
                if k >= 2:
                    sp.wait_ge(s[f"out_stored{q}"], 16 * (k // 2))
                sp.dma_start((x1, xin)[q][:, :, :], tm_dram(x3_dram, k)).then_inc(s[f"x3_back{q}"], 16)
                sp.dma_start((tmp, xln)[q][:, :, :], tm_dram(yw_dram, k)).then_inc(s[f"yw_back{q}"], 16)

        @block.gpsimd
        def _(pool):
            for n in range(2):
                pool.wait_ge(s["amax_done"], n + 1)
                a, b = ((0, 2), (2, NW))[n]
                GP.partition_all_reduce(amax_all[:, a:b], amax[:, a:b], 128, bass.bass_isa.ReduceOp.max).then_inc(s["amax_red"], 1)

            def step(cell):
                GP.tensor_tensor(pool_cell[:, cell:cell + 1], pool_cell[:, 0:1], pool_cell[:, 0:1], ALU.add).then_inc(s["pool_step"], 1)

            def gather_tile(b, u, q, first=False):
                n = (b * T + u * 2 + q) * 3
                if not first:
                    pool.wait_ge(s["val_ready"], b * T + u * 2 + (q - 1))
                step(1 + q)
                GP.tensor_copy(index_now[:, q, :], index[:, bass.ds((u * 2 + q) * TAPS, TAPS)]).then_inc(s["pool_step"], 1)
                pool.wait_ge(s["pool_step"], n + 2)
                step(3 + q)
                for tap in range(TAPS):
                    GP.indirect_dma_start(G[0:TP, q, tap * 4 * C:(tap + 1) * 4 * C], None, table,
                                          bass.IndirectOffsetOnAxis(ap=index_now[:, q, tap:tap + 1], axis=0)).then_inc(gath[q], 16)

            GP.memset(pool_cell[:, :], 0.0).then_inc(s["cell_done"], 1)
            pool.wait_ge(s["cell_done"], 1)
            with pool.Fori(0, B) as b:
                pool.wait_ge(s["geo_done"], b + 1)
                pool.wait_ge(s["table_written"], (b + 1) * 128)
                for q in range(2):
                    gather_tile(b, 0, q, first=True)
                with pool.Fori(1, T // 2) as u:
                    for q in range(2):
                        gather_tile(b, u, q)

        @block.vector
        def _(dve):
            def step(ins):
                dve.drain()
                return ins

            red = lambda o, i, op=ALU.add: V.tensor_reduce(o, i, AX.X, op)

            def split_weights(h, l, src, col):
                V.tensor_scalar(h, src, wscale[:, col:col + 1], None, ALU.mult)
                dve.drain()
                V.scalar_tensor_tensor(l, src, wscale[:, col:col + 1], h, ALU.mult, ALU.subtract)

            def scales(a, b):
                V.tensor_scalar(amax_all[:, a:b], amax_all[:, a:b], 1e-30, None, ALU.max)
                dve.drain()
                V.tensor_scalar(descale[:, a:b].bitcast(i32), amax_all[:, a:b].bitcast(i32), 0x7F800000, None, ALU.bitwise_and)
                dve.drain()
                V.tensor_scalar(wscale[:, a:b].bitcast(i32), descale[:, a:b].bitcast(i32), -1.0, float(262 << 23), ALU.mult, ALU.add)
                dve.drain()
                V.tensor_scalar(descale[:, a:b], descale[:, a:b], 1.0 / (256.0 * XS), None, ALU.mult)
                dve.drain()

            def magnitudes(tensors):
                for col, src in tensors:
                    red(amax[:, col:col + 1], src, ALU.max)
                    red(amin[:, col:col + 1], src, ALU.min)
                dve.drain()
                for col, _src in tensors:
                    V.scalar_tensor_tensor(amax[:, col:col + 1], amin[:, col:col + 1], -1.0, amax[:, col:col + 1], ALU.mult, ALU.max)

            V.memset(padded[:, :], 0.0)
            V.memset(zero16[:, :], 0.0)
            V.memset(ones16[:, :], 1.0)
            V.memset(pick[:, :], 0.0)
            dve.wait_ge(s["w_staged"], 16 * 4)
            magnitudes(((MOE1, stage[:, 0:E * HID]), (MOE2, stage2[:, 0:E * HID])))
            dve.drain()
            V.memset(cnt16[:, :], 0.0).then_inc(s["amax_done"], 1)
            dve.wait_ge(s["amax_red"], 1)
            scales(0, 2)
            split_weights(w1h[:, :], w1l[:, :], stage[:, 0:E * HID], MOE1)
            split_weights(w2h[:, :], w2l[:, :], stage2[:, 0:E * HID], MOE2)
            dve.drain()
            V.memset(stage[:, 0:1280], 0.0).then_inc(s["w_taken"], 1)
            dve.wait_ge(s["w_staged"], 16 * (4 + 10))
            dve.wait_ge(s["w_loaded"], 16 * 15)
            pieces = ((GATE, gateh[:, :], gatel[:, :], stage[:, 0:E]), (OFF, offh[:, :], offl[:, :], stage[:, 64:64 + TAPS * OC]),
                      (FFN1, f1h[:, :], f1l[:, :], stage[:, 1024:1024 + FH]), (ROUTE, wrh[:, 0:1], wrl[:, 0:1], stage[:, 768:769]))
            magnitudes([(col, src) for col, _h, _l, src in pieces])
            V.tensor_copy(ident16[:, :], ident[0:TP, 0:TP])
            V.tensor_copy(tri16[:, :], stage2[0:TP, 0:TP])
            V.tensor_copy(bits[:, :], stage2[0:TP, 128:159])
            dve.drain()
            V.memset(cnt16[:, :], 0.0).then_inc(s["amax_done"], 1)
            dve.wait_ge(s["amax_red"], 2)
            scales(2, NW)
            for col, h, l, src in pieces:
                split_weights(h, l, src, col)
            dve.drain()
            V.memset(cnt16[:, :], 0.0).then_inc(s["w_taken"], 1)
            V.memset(stage[:, :], 0.0).then_inc(s["stage_zero"], 1)
            dve.wait_ge(s["w_staged"], 16 * (4 + 11))
            V.tensor_copy(pick[0:2 * E, :], stage2[0:2 * E, 0:E * 128])
            dve.drain()
            V.memset(cnt16[:, :], 0.0).then_inc(s["const_done"], 1)

            def combine_mul(b, t, q, u):
                dve.wait_ge(gath[q], b * (TAPS * 16 * T // 2) + (u + 1) * (TAPS * 16))
                g = G[0:TP, q, :].rearrange("p (n c) -> p n c", c=C)
                w = corner_w[:, :, :].rearrange("p n s -> p (n s)")[:, bass.ds(t * (4 * TAPS), 4 * TAPS)]
                V.tensor_tensor(g, g, bc(w, 2, C), ALU.mult)

            def combine_add(q):
                g = G[0:TP, q, :].rearrange("p (n s) -> p n s", n=TAPS)
                dve.drain()
                V.tensor_tensor(g[:, :, 0:2 * C], g[:, :, 0:2 * C], g[:, :, 2 * C:4 * C], ALU.add)

            def combine_val(q):
                g = G[0:TP, q, :].rearrange("p (n s) -> p n s", n=TAPS)
                dve.drain()
                V.tensor_tensor(val[:, :].rearrange("p (n c) -> p n c", n=TAPS), g[:, :, 0:C], g[:, :, C:2 * C],
                                ALU.add).then_inc(s["val_ready"], 1)

            def sample_add(b, t):
                dve.wait_ge(s["dcn_done"], b * T + t + 1)
                xt = xB[:, :, :].rearrange("p t c -> p (t c)")[:, bass.ds(t * C, C)]
                V.tensor_tensor(xt, xt, D1[0:TP, 128:128 + C], ALU.add).then_inc(s["x3_added"], 1)

            def layer_norm(src, eps, rounds):
                red(st[:, 0, :], src)
                dve.drain()
                V.tensor_scalar(st[:, 1, :], st[:, 0, :], 1.0 / C, None, ALU.mult)
                dve.drain()
                V.tensor_tensor(xln[:, :, :], src, bc(st[:, 1, :], 2, C), ALU.subtract)
                dve.drain()
                V.tensor_tensor(tmp[:, :, :], xln[:, :, :], xln[:, :, :], ALU.mult)
                dve.drain()
                red(st[:, 2, :], tmp[:, :, :])
                dve.drain()
                V.tensor_scalar(st[:, 3, :], st[:, 2, :], 1.0 / C, eps, ALU.mult, ALU.add).then_inc(s["var_done"], 1)
                dve.wait_ge(s["std_done"], rounds + 1)
                V.reciprocal(st[:, 5, :], st[:, 4, :])
                dve.drain()
                V.tensor_tensor(xln[:, :, :], xln[:, :, :], bc(st[:, 5, :], 2, C), ALU.mult)

            def split_l(n, twice):
                dve.wait_ge(s["h_cast"], n + 1)
                if twice:
                    V.tensor_tensor(split[:, :, 2 * C:4 * C].rearrange("p t (a c) -> p t a c", a=2), bc(tmp[:, :, :], 2, 2),
                                    split[:, :, 0:2 * C].rearrange("p t (a c) -> p t a c", a=2), ALU.subtract).then_inc(s["split_done"], 1)
                else:
                    V.tensor_tensor(split[:, :, 2 * C:3 * C], tmp[:, :, :], split[:, :, C:2 * C], ALU.subtract).then_inc(s["split_done"], 1)

            def mixer_norm(k, r, n):
                dve.wait_ge(s["x_loaded"], (k + 1) * 16)
                layer_norm(xin[:, :, :], LNC_EPS, r)
                V.tensor_tensor(st[:, 6, :], st[:, 2, :], st[:, 5, :], ALU.mult)
                dve.drain()
                V.tensor_tensor(st[:, 6, :], st[:, 6, :], st[:, 5, :], ALU.mult)
                dve.drain()
                V.tensor_scalar(st[:, 3, :], st[:, 6, :], 1e-12, None, ALU.max).then_inc(s["var_done"], 1)
                dve.wait_ge(s["std_done"], r + 2)
                V.reciprocal(st[:, 5, :], st[:, 4, :])
                dve.drain()
                V.tensor_scalar(st[:, 5, :], st[:, 5, :], XS, None, ALU.mult)
                dve.drain()
                V.tensor_tensor(tmp[:, :, :], xln[:, :, :], bc(st[:, 5, :], 2, C), ALU.mult).then_inc(s["scaled"], 1)
                split_l(n, True)

            def norm_and_split(src, eps, r, n):
                layer_norm(src, eps, r)
                dve.drain()
                V.tensor_scalar(tmp[:, :, :], xln[:, :, :], XS, None, ALU.mult).then_inc(s["scaled"], 1)
                split_l(n, False)

            def mixer_body(g, d, sample):
                n = 0
                for u in range(SPB):
                    if sample and u == 0:
                        combine_mul(*sample)
                    if sample and u == 2:
                        combine_add(sample[2])
                    if sample and u == 3:
                        combine_val(sample[2])
                    if u in DVE_STEPS:
                        dve.wait_ge(s["relu_done"], g + u + 1)
                        V.tensor_tensor(sq[:, u % 2], relu[:, u % 2], relu[:, u % 2], ALU.mult).then_inc(s["sq_dve"], 1)
                if sample:
                    sample_add(sample[0], sample[1])

            def mixer(k, back):
                for half in range(2):
                    g0 = k * SPI + half * SPH
                    d0 = (k * 2 + half) * BPH * DVE_N
                    t0 = half * BPH
                    with dve.Fori(0, BPH // 2) as bb:
                        for v in range(2):
                            j = bb * 2 + v
                            q = (t0 + v) % 2
                            u = (t0 // 2 + bb) if (t0 + v) % 2 == v else (bb + (t0 + v) // 2)
                            mixer_body(g0 + j * SPB, d0 + j * DVE_N, (k - 1, j + t0, q, u) if back else None)
                    j = BPH - 1
                    mixer_body(g0 + j * SPB, None, (k - 1, t0 + j, (t0 + j) % 2, (t0 + j) // 2) if back else None)
                    for m in range(2):
                        dve.wait_ge(s["y_done"], k * 4 + half * 2 + m + 1)
                        r = slice(half * 14 + m * 7, half * 14 + m * 7 + 7)
                        V.tensor_tensor(x1[:, r, :], xin[:, r, :], S[m][0:TP, 0:7 * C].rearrange("p (t c) -> p t c", c=C),
                                        ALU.add).then_inc(s["x1_added"], 1)

            def gate(k):
                p = small[:, 0, 0:T * E].rearrange("p (t e) -> p t e", e=E)
                o1 = small[:, 1, 0:T * E].rearrange("p (t e) -> p t e", e=E)
                o2 = small[:, 2, 0:T * E].rearrange("p (t e) -> p t e", e=E)
                c = small[:, 3, 0:T * E].rearrange("p (t e) -> p t e", e=E)
                m, r, m1, m2, den = (smallc[:, i, :] for i in range(5))

                def tt(o, a, b, op):
                    V.tensor_tensor(o, a, b, op)
                    dve.drain()

                def rd(o, a, op):
                    red(o, a, op)
                    dve.drain()

                def first_max(oh, top, src):
                    rd(top, src, ALU.max)
                    tt(oh, src, bc(top, 2, E), ALU.is_equal)
                    tt(c, oh, bc(rank[:, :], 1, T), ALU.mult)
                    rd(den, c, ALU.max)
                    tt(oh, c, bc(den, 2, E), ALU.is_equal)

                dve.wait_ge(s["logits_done"], k + 1)
                V.tensor_scalar(p, D0[0:TP, 0:T * E].rearrange("p (t e) -> p t e", e=E), descale[0:TP, GATE:GATE + 1], None, ALU.mult)
                dve.drain()
                tt(p, p, bc(gbias[:, :], 1, T), ALU.add)
                rd(m, p, ALU.max)
                V.tensor_tensor(p, p, bc(m, 2, E), ALU.subtract).then_inc(s["sm_shift"], 1)
                dve.wait_ge(s["sm_exp"], k + 1)
                rd(m, p, ALU.add)
                V.reciprocal(r, m)
                dve.drain()
                tt(p, p, bc(r, 2, E), ALU.mult)
                first_max(o1, m1, p)
                V.scalar_tensor_tensor(p, o1, -2.0, p, ALU.mult, ALU.add)
                dve.drain()
                first_max(o2, m2, p)
                tt(den, m1, m2, ALU.add)
                V.reciprocal(r, den)
                dve.drain()
                tt(m1, m1, r, ALU.mult)
                tt(m2, m2, r, ALU.mult)
                tt(o1, o1, bc(m1, 2, E), ALU.mult)
                tt(o2, o2, bc(m2, 2, E), ALU.mult)
                V.scalar_tensor_tensor(disp[:, :, :], o1, 1.0, o2, ALU.mult, ALU.add)
                dve.drain()
                V.tensor_scalar(disp[:, :, :], disp[:, :, :], XS, None, ALU.mult)
                dve.drain()
                V.tensor_copy(dsplit[:, :, 0:E], disp[:, :, :])
                dve.drain()
                V.tensor_tensor(dsplit[:, :, E:2 * E], disp[:, :, :], dsplit[:, :, 0:E], ALU.subtract).then_inc(s["disp_split"], 1)

            def experts_chunk(k, c, samples):
                n0 = k * (NCH * E) + c * E

                def gate_mul(e):
                    dve.wait_ge(s["silu_done"], n0 + e + 1)
                    V.scalar_tensor_tensor(silu[:, e % 2, :], S[2 + e % 2][:, 0:CW], descale[:, MOE2:MOE2 + 1], silu[:, e % 2, :],
                                           ALU.mult, ALU.mult).then_inc(s["gate_done"], 1)

                gate_mul(0)
                for e in range(E):
                    h, i = divmod(e, E // 2)
                    if samples:
                        smp = samples[h]
                        if i == 0:
                            combine_mul(*smp)
                        if i == 1:
                            combine_add(smp[2])
                        if i == 2:
                            combine_val(smp[2])
                        if i == 6:
                            sample_add(smp[0], smp[1])
                    if e + 1 < E:
                        gate_mul(e + 1)
                    dve.wait_ge(s["bcast_done"], n0 + e + 1)
                    dve.wait_ge(s["gate_done"], n0 + e + 1)
                    V.tensor_tensor(hid[:, e % 4, :], silu[:, e % 2, :], Y1[:, 0:CW], ALU.mult).then_inc(s["hid_done"], 1)
                dve.wait_ge(s["ytm_done"], k * NCH + c + 1)
                xt = x1[:, :, :].rearrange("p t c -> p (t c)")[:, bass.ds(c * (CT * C), CT * C)]
                V.tensor_tensor(xt, xt, Y0[0:TP, 0:CT * C], ALU.add).then_inc(s["x2_added"], 1)

            def geometry(k, has_back):
                base = grid[:, :, :]
                v18 = lambda i: small[:, i, :].rearrange("p (t n) -> p t n", t=T)
                for g in range(2):
                    dve.wait_ge(s["om_tr"], k * 2 + g + 1)
                    nt = 4 if g == 0 else NCH - 4
                    V.tensor_scalar(om[:, 16 * g:16 * g + CT * nt, :].rearrange("p (g s) o -> p g s o", s=CT),
                                    S[2 + g][0:TP, :].rearrange("p (s g o) -> p g s o", s=CT, o=OC)[:, 0:nt],
                                    descale[0:TP, OFF:OFF + 1], None, ALU.mult)
                dve.drain()
                V.tensor_tensor(om[:, :, 0:27], om[:, :, 0:27], bc(obias[:, :], 1, T), ALU.add).then_inc(s["mask_in"], 1)
                dve.drain()
                V.tensor_tensor(v18(0), om[:, :, 0:18], base, ALU.add)
                dve.drain()
                V.tensor_scalar(v18(0), v18(0), 0.0, float(H + 1), ALU.max, ALU.min)
                dve.drain()
                V.tensor_copy(v18(1).bitcast(i32), v18(0))
                dve.drain()
                V.tensor_copy(v18(2), v18(1).bitcast(i32))
                dve.drain()
                V.tensor_tensor(v18(1), v18(2), v18(0), ALU.is_gt)
                dve.drain()
                V.tensor_tensor(v18(1), v18(2), v18(1), ALU.subtract)
                dve.drain()
                V.tensor_tensor(v18(2), v18(0), v18(1), ALU.subtract)
                dve.drain()
                V.tensor_scalar(v18(3), v18(2), -1.0, 1.0, ALU.mult, ALU.add)
                yx = lambda i: small[:, i, :].rearrange("p (n two) -> p n two", two=2)
                V.scalar_tensor_tensor(small[:, 4, 0:T * TAPS], yx(1)[:, :, 0], float(SIDE), yx(1)[:, :, 1], ALU.mult, ALU.add)
                dve.drain()
                V.tensor_copy(index[:, :], small[:, 4, 0:T * TAPS])
                dve.drain()
                dve.wait_ge(s["mask_out"], k + 1)
                m = mask[:, :, :].rearrange("p t n -> p (t n)")
                a0, a1 = small[:, 0, 0:T * TAPS], small[:, 4, 0:T * TAPS]
                V.tensor_tensor(a0, yx(3)[:, :, 0], m, ALU.mult)
                V.tensor_tensor(a1, yx(2)[:, :, 0], m, ALU.mult)
                dve.drain()
                V.tensor_tensor(corner_w[:, :, 0], a0, yx(3)[:, :, 1], ALU.mult)
                V.tensor_tensor(corner_w[:, :, 1], a0, yx(2)[:, :, 1], ALU.mult)
                V.tensor_tensor(corner_w[:, :, 2], a1, yx(3)[:, :, 1], ALU.mult)
                V.tensor_tensor(corner_w[:, :, 3], a1, yx(2)[:, :, 1], ALU.mult)
                if has_back:
                    dve.wait_ge(s["x3_stored"], 16 * k)
                V.tensor_copy(xB[:, :, :], x1[:, :, :])
                dve.drain()
                V.memset(cnt16[:, :], 0.0).then_inc(s["geo_done"], 1)

            def ffn(b, r, n):
                dve.drain()
                norm_and_split(xB[:, :, :], LNT_EPS, r, n)
                V.tensor_tensor(xB[:, :, :], xB[:, :, :], xln[:, :, :], ALU.add).then_inc(s["skip_added"], 1)
                dve.wait_ge(s["route_done"], b + 1)
                w = w_all[:, :, :].rearrange("p b t -> p (b t)")[:, bass.ds(b * T, T)]
                V.tensor_scalar(w, D0[0:TP, 0:T], descale[0:TP, ROUTE:ROUTE + 1], brc[:, 0:1], ALU.mult, ALU.add).then_inc(s["route_taken"], 1)
                dve.wait_ge(s["route_taken"], b + 1)
                for c in range(NCH):
                    dve.wait_ge(s["fdown_done"], b * NCH + c + 1)
                    o = yw[:, c * CT:(c + 1) * CT, :]
                    V.tensor_tensor(o, (Y0, Y1)[c % 2][0:TP, 0:CT * C].rearrange("p (t c) -> p t c", c=C), bc(fb2r[:, :], 1, CT), ALU.add)
                    dve.drain()
                    wc = w_all[:, :, :].rearrange("p b t -> p (b t)")[:, bass.ds(b * T + c * CT, CT)]
                    V.tensor_tensor(o, o, bc(wc, 2, C), ALU.mult).then_inc(s["yw_done"], 1)

            def image(k, back):
                r0 = 5 * k - (1 if back else 0)
                n0 = 4 * k - (1 if back else 0)
                mixer_norm(k, r0, n0)
                mixer(k, back)
                dve.drain()
                norm_and_split(x1[:, :, :], LNT_EPS, r0 + 2, n0 + 1)
                gate(k)
                with dve.Fori(0, NCH) as c:
                    experts_chunk(k, c, [(k - 1, c * 2 + 14 + q, q, c + 7) for q in range(2)] if back else None)
                if back:
                    ffn(k - 1, r0 + 3, n0 + 2)
                dve.drain()
                if back:
                    dve.wait_ge(s["table_written"], k * 128)
                layer_norm(x1[:, :, :], LNC_EPS, r0 + 3 + (1 if back else 0))
                dve.drain()
                V.tensor_scalar(tmp[:, :, :], xln[:, :, :], XS, None, ALU.mult).then_inc(s["scaled"], 1)
                V.memset(cnt16[:, :], 0.0).then_inc(s["geo_ln"], 1)
                split_l(n0 + 2 + (1 if back else 0), False)
                geometry(k, back)
                dve.wait_ge(s["table_written"], (k + 1) * 128)
                if back:
                    dve.wait_ge(s["yw_stored"], 16 * k)

            image(0, False)
            with dve.Fori(1, B) as k:
                image(k, True)
            with dve.Fori(0, T // 2) as u:
                for q in range(2):
                    combine_mul(B - 1, u * 2 + q, q, u)
                    combine_add(q)
                    combine_val(q)
                    sample_add(B - 1, u * 2 + q)
            ffn(B - 1, 5 * B - 1, 4 * B - 1)

            def count(n, src):
                with nc.allow_low_precision("counts up to T are exact in float16"):
                    red(cnt16[:, :], src)
                dve.drain()
                V.memset(kf[:, 6, :], 0.0).then_inc(s["count_in"], 1)
                dve.wait_ge(s["count_done"], n + 1)

            dve.drain()
            sgn, kth, got, thr, need, zed = (kf[:, i, :] for i in (0, 1, 2, 3, 4, 5))
            V.tensor_scalar(hit, w_all[:, :, :], 0.0, None, ALU.is_ge)
            V.memset(ki[:, 0, :], 0.0)
            dve.drain()
            count(0, hit)
            V.tensor_scalar(got, D0[0:TP, 0:B], float(KTOP), None, ALU.is_ge)
            dve.drain()
            V.tensor_scalar(sgn, got, 2.0, -1.0, ALU.mult, ALU.add)
            V.tensor_scalar(kth, got, float(KTOP - (N - KTOP + 1)), float(N - KTOP + 1), ALU.mult, ALU.add)
            dve.drain()
            V.tensor_tensor(key, w_all[:, :, :], bc(sgn, 2, T), ALU.mult)
            with dve.Fori(0, 31) as i:
                bit = bits[:, bass.ds(i, 1)].to_broadcast([TP, B])
                dve.drain()
                V.tensor_tensor(ki[:, 1, :], ki[:, 0, :], bit, ALU.bitwise_or)
                dve.drain()
                V.tensor_tensor(hit, key, bc(ki[:, 1, :].bitcast(f32), 2, T), ALU.is_ge)
                dve.drain()
                count(i + 1, hit)
                V.tensor_tensor(got, D0[0:TP, 0:B], kth, ALU.is_ge)
                dve.drain()
                V.tensor_tensor(ki[:, 2, :], got, bit, ALU.mult)
                dve.drain()
                V.tensor_tensor(ki[:, 0, :], ki[:, 0, :], ki[:, 2, :], ALU.bitwise_or)
            dve.drain()
            V.tensor_tensor(thr, ki[:, 0, :].bitcast(f32), sgn, ALU.mult)
            dve.drain()
            V.tensor_tensor(sel[:, :, :], w_all[:, :, :], bc(thr, 2, T), ALU.is_gt)
            V.tensor_tensor(eqf, w_all[:, :, :], bc(thr, 2, T), ALU.is_equal)
            dve.drain()
            V.tensor_copy(eq16[:, :], eqf.rearrange("p b t -> p (b t)"))
            count(32, sel[:, :, :])
            V.tensor_scalar(need, D0[0:TP, 0:B], -1.0, float(KTOP), ALU.mult, ALU.add).then_inc(s["tie_in"], 1)
            dve.wait_ge(s["tie_done"], 1)
            V.tensor_copy(pre, D0[0:TP, 0:B * T].rearrange("p (b t) -> p b t", b=B))
            V.tensor_copy(tot, D1[0:TP, 0:B * T].rearrange("p (b t) -> p b t", b=B))
            dve.drain()
            a, o = tot, hit
            V.memset(o[:, :, 0:1], 0.0)
            V.tensor_copy(o[:, :, 1:T], a[:, :, 0:T - 1])
            dve.drain()
            a, o = o, a
            for sh in (1, 2, 4, 8, 16):
                V.tensor_copy(o[:, :, 0:sh], a[:, :, 0:sh])
                V.tensor_tensor(o[:, :, sh:T], a[:, :, sh:T], a[:, :, 0:T - sh], ALU.add)
                dve.drain()
                a, o = o, a
            V.tensor_tensor(pre, pre, a, ALU.add)
            dve.drain()
            V.tensor_tensor(pre, pre, bc(need, 2, T), ALU.is_lt)
            dve.drain()
            V.tensor_tensor(pre, pre, eqf, ALU.mult)
            dve.drain()
            V.tensor_tensor(sel[:, :, :], sel[:, :, :], pre, ALU.add)
            dve.drain()
            for k in range(B):
                q = k % 2
                dve.wait_ge(s[f"x3_back{q}"], 16 * (k // 2 + 1))
                dve.wait_ge(s[f"yw_back{q}"], 16 * (k // 2 + 1))
                xv, yv = (x1, xin)[q][:, :, :], (tmp, xln)[q][:, :, :]
                V.tensor_tensor(yv, yv, bc(sel[:, k, :], 2, C), ALU.mult)
                dve.drain()
                V.tensor_tensor(xv, xv, yv, ALU.add).then_inc(s["fin_ready"], 1)

        @block.scalar
        def _(act):
            def sqrt_round(r):
                act.wait_ge(s["var_done"], r + 1)
                A.activation(st[:, 4, :], st[:, 3, :], ACT.Sqrt).then_inc(s["std_done"], 1)

            def cast_h(n, twice):
                act.wait_ge(s["scaled"], n + 1)
                if twice:
                    A.activation(split[:, :, 0:2 * C].rearrange("p t (a c) -> p t a c", a=2), bc(tmp[:, :, :], 2, 2),
                                 ACT.Copy).then_inc(s["h_cast"], 1)
                else:
                    A.activation(split[:, :, C:2 * C], tmp[:, :, :], ACT.Copy).then_inc(s["h_cast"], 1)

            def sample_evac(b, t):
                act.wait_ge(s["val_tr"], b * T + t + 1)
                A.activation(val_cm[:, 0:4 * TP], D0[:, 0:4 * TP], ACT.Copy)
                A.activation(val_cm[0:C, 4 * TP:5 * TP], D1[0:C, 0:TP], ACT.Copy).then_inc(s["valcm_ready"], 1)

            def stage_sources(n, j0):
                par, first = n
                A.activation(xj[:, par, :, :].rearrange("p j c -> p (j c)"),
                             xln[:, :, :].rearrange("p t c -> p (t c)")[:, bass.ds(j0 * C, JB * C)], ACT.Copy).then_inc(s["xj_ready"], 1)

            def mixer_body(g, a, sample):
                for u in range(SPB):
                    act.wait_ge(s["sim_done"], g + u + 1)
                    A.activation(relu[:, u % 2], PS[u % 2][0:TP, :, 0:IW], ACT.Relu).then_inc(s["relu_done"], 1)
                    if u in ACT_STEPS:
                        act.wait_ge(s["relu_done"], g + u + 1)
                        A.activation(sq[:, u % 2], relu[:, u % 2], ACT.Square).then_inc(s["sq_act"], 1)
                    if sample and u == 6:
                        sample_evac(sample[0], sample[1])

            def mixer(k, back):
                for half in range(2):
                    g0 = k * SPI + half * SPH
                    b0 = (k * 2 + half) * BPH
                    stage_sources((0, True), 0)
                    with act.Fori(0, BPH // 2) as bb:
                        for v in range(2):
                            j = bb * 2 + v
                            act.wait_ge(s["sim_done"], g0 + j * SPB + 2)
                            stage_sources((1 - v, False), (j + 1) * JB)
                            mixer_body(g0 + j * SPB, None, (k - 1, j + half * BPH) if back else None)
                    j = BPH - 1
                    mixer_body(g0 + j * SPB, None, (k - 1, j + half * BPH) if back else None)
                    act.wait_ge(s["z_done"], k * 2 + half + 1)
                    for blk in range(4):
                        r = (blk % 2) * C
                        ins = A.activation(z_cm[:, blk * IW:(blk + 1) * IW], (Y0, Y1)[blk // 2][r:r + C, 0:IW], ACT.Copy,
                                           scale=1.0 / XS ** 4)
                    ins.then_inc(s["z_ready"], 1)

            def experts_chunk(k, c, samples):
                n0 = k * (NCH * E) + c * E
                for e in range(E):
                    act.wait_ge(s["up_done"], n0 + e + 1)
                    A.activation(silu[:, e % 2, :], S[e % 2][:, 0:CW], ACT.Silu, scale=descale[:, MOE1:MOE1 + 1]).then_inc(s["silu_done"], 1)
                    if samples and e % 8 == 4:
                        sample_evac(*samples[e // 8])
                act.wait_ge(s["ycm_done"], k * NCH + c + 1)
                A.activation(om_cm[:, :], Y0[:, 0:CW], ACT.Copy, scale=1.0 / XS).then_inc(s["ycm_ready"], 1)

            def ffn(b):
                for c in range(NCH):
                    for m in range(2):
                        act.wait_ge(s["fup_done"], b * (2 * NCH) + 2 * c + m + 1)
                        A.activation(hid[:, (2 * c + m) % 4, :], S[(2 * c + m) % 4][:, 0:CW], ACT.Gelu_apprx_tanh,
                                     bias=fb1c[:, m:m + 1], scale=descale[:, FFN1:FFN1 + 1]).then_inc(s["gelu_done"], 1)

            def evac_tr(n, dsts):
                for i, dst in enumerate(dsts):
                    act.wait_ge(s["tr_done"], n + i + 1)
                    A.activation(dst, S[i % 4][:, 0:CW] if len(dst.shape) == 2 else
                                 S[i % 4][:, 0:CW].rearrange("p (y x) -> p y x", x=W), ACT.Copy).then_inc(s["tr_cm"], 1)

            def image(k, back):
                r0 = 5 * k - (1 if back else 0)
                n0 = 4 * k - (1 if back else 0)
                tr0 = k * (6 * NCH) - (NCH if back else 0)
                sqrt_round(r0)
                sqrt_round(r0 + 1)
                cast_h(n0, True)
                with act.Fori(0, NCH) as c:
                    for i, dst in enumerate((xn_hl, xn_hh, xn_ll)):
                        act.wait_ge(s["tr_done"], tr0 + c * 3 + i + 1)
                        A.activation(dst[:, bass.ds(c * CW, CW)], S[i][:, 0:CW], ACT.Copy).then_inc(s["tr_cm"], 1)
                mixer(k, back)
                sqrt_round(r0 + 2)
                cast_h(n0 + 1, False)
                evac_tr(tr0 + 3 * NCH, [xn_hl[:, c * CW:(c + 1) * CW] for c in range(NCH)])
                act.wait_ge(s["sm_shift"], k + 1)
                A.activation(small[:, 0, 0:T * E], small[:, 0, 0:T * E], ACT.Exp).then_inc(s["sm_exp"], 1)
                for c in range(NCH):
                    act.wait_ge(s["disp_tr"], k * NCH + c + 1)
                    A.activation(dT[0:2 * E, c * CW:(c + 1) * CW], S[c % 4][0:2 * E, 0:CW], ACT.Copy).then_inc(s["disp_cm"], 1)
                with act.Fori(0, NCH) as c:
                    experts_chunk(k, c, [(k - 1, c * 2 + 14 + q) for q in range(2)] if back else None)
                if back:
                    sqrt_round(r0 + 3)
                    cast_h(n0 + 2, False)
                    evac_tr(tr0 + 4 * NCH, [xn_hl[:, c * CW:(c + 1) * CW] for c in range(NCH)])
                    ffn(k - 1)
                bk = 1 if back else 0
                sqrt_round(r0 + 3 + bk)
                cast_h(n0 + 2 + bk, False)
                evac_tr(tr0 + (4 + bk) * NCH, [pad_v[:, 1 + 8 * c:9 + 8 * c, 1:1 + W] for c in range(NCH)])
                for g in range(2):
                    act.wait_ge(s["om_done"], k * 2 + g + 1)
                    rows = 128 if g == 0 else OC * (NCH - 4)
                    A.activation(om_c[g][0:rows, :], S[g][0:rows, 0:CW], ACT.Copy).then_inc(s["om_ready"], 1)
                act.wait_ge(s["mask_in"], k + 1)
                A.activation(mask[:, :, :], om[:, :, 18:27], ACT.Sigmoid).then_inc(s["mask_out"], 1)

            act.wait_ge(s["w_loaded"], 16 * 15)
            act.wait_ge(s["const_done"], 1)
            image(0, False)
            with act.Fori(1, B) as k:
                image(k, True)
            with act.Fori(0, T) as t:
                sample_evac(B - 1, t)
            sqrt_round(5 * B - 1)
            cast_h(4 * B - 1, False)
            evac_tr(B * 6 * NCH - NCH, [xn_hl[:, c * CW:(c + 1) * CW] for c in range(NCH)])
            ffn(B - 1)
            for k in range(B):
                q = k % 2
                act.wait_ge(s["fin_ready"], k + 1)
                act.dma_start(tm_dram(out.rearrange("b h w c -> b (h w) c"), k), (x1, xin)[q][:, :, :]).then_inc(s[f"out_stored{q}"], 16)
            for q in range(2):
                act.wait_ge(s[f"out_stored{q}"], 16 * ((B + 1 - q) // 2))

        @block.tensor
        def _(pe):
            def mm(o, a, b, start=True, stop=True):
                return P.matmul(o, a, b, start=start, stop=stop, skip_group_check=True)

            def transpose_tile(o, t, kind):
                c0 = {"hl": C, "hh": 0, "ll": 2 * C}[kind]
                return mm(o, split[:, :, :].rearrange("p t c -> p (t c)")[:, bass.ds(t * (4 * C) + c0, 2 * C)], ident16[:, :])

            def transpose_all(n):
                for c in range(NCH):
                    if c >= 4:
                        pe.wait_ge(s["tr_cm"], n + c - 3)
                    for i in range(CT):
                        ins = transpose_tile(S[c % 4][:, i * TP:(i + 1) * TP], c * CT + i, "hl")
                    ins.then_inc(s["tr_done"], 1)

            def sample_tr(b, t):
                pe.wait_ge(s["val_ready"], b * T + t + 1)
                for n in range(4):
                    P.transpose(D0[:, n * TP:(n + 1) * TP], val[:, n * 128:(n + 1) * 128], ident[0:TP, 0:TP])
                P.transpose(D1[0:C, 0:TP], val[:, 512:576], ident[0:TP, 0:TP]).then_inc(s["val_tr"], 1)

            def sample_conv(b, t):
                pe.wait_ge(s["valcm_ready"], b * T + t + 1)
                for n in range(5):
                    r = 128 if n < 4 else C
                    ins = mm(D1[0:TP, 128:128 + C], val_cm[0:r, n * TP:(n + 1) * TP], dcn[0:r, n, :], n == 0, n == 4)
                ins.then_inc(s["dcn_done"], 1)

            def sims(j, i0, u):
                for b in range(2):
                    i = i0 + (u % 2 * 2 + b) * IW
                    o = PS[u % 2][0:TP, b, 0:IW]
                    mm(o, xn_hh[:, bass.ds(j * TP, TP)], xn_hl[:, i:i + IW], True, False)
                    ins = mm(o, xn_ll[:, bass.ds(j * TP, TP)], xn_hl[:, i:i + IW], False, True)
                ins.then_inc(s["sim_done"], 1)

            def mixer_body(k, i0, j0, par, na, nd, xn, last, sample):
                a = d = 0
                pe.wait_ge(s["xj_ready"], xn + 1)
                for u in range(SPB):
                    if sample and u == 5:
                        sample_tr(*sample)
                    if sample and u == 7:
                        sample_conv(*sample)
                    if not (last and u == SPB - 1):
                        sims(j0 + (u + 1) // 2, i0, (u + 1) % 2)
                    if u in ACT_STEPS:
                        a += 1
                        pe.wait_ge(s["sq_act"], na + a)
                    else:
                        d += 1
                        pe.wait_ge(s["sq_dve"], nd + d)
                    for b in range(2):
                        ins = mm((Y0, Y1)[u % 2][b * C:(b + 1) * C, 0:IW], xj[:, par, u // 2, :], sq[:, u % 2, b], False, False)
                return ins

            def mixer(k, back):
                for half in range(2):
                    i0 = half * 4 * IW
                    b0 = (k * 2 + half) * BPH
                    if half:
                        pe.wait_ge(s["x1_added"], k * 4 + 2)
                    for y in (Y0, Y1):
                        mm(y[:, 0:IW], zero16[:, 0:128], zero16[:, 0:IW], True, False)
                    sims(0, i0, 0)
                    with pe.Fori(0, BPH // 2) as bb:
                        for v in range(2):
                            j = bb * 2 + v
                            mixer_body(k, i0, j * JB, v, (j + b0) * ACT_N, (j + b0) * DVE_N, j + b0, False,
                                       (k - 1, j + half * BPH) if back else None)
                    j = BPH - 1
                    mixer_body(k, i0, j * JB, 0, (b0 + j) * ACT_N, (b0 + j) * DVE_N, b0 + j, True,
                               (k - 1, j + half * BPH) if back else None).then_inc(s["z_done"], 1)
                    pe.wait_ge(s["z_ready"], k * 2 + half + 1)
                    for m in range(2):
                        for t in range(7):
                            c0 = (m * 7 + t) * TP
                            ins = mm(S[m][0:TP, t * C:(t + 1) * C], z_cm[:, c0:c0 + TP], w_mix[:, :])
                        ins.then_inc(s["y_done"], 1)

            def experts_chunk(k, c, samples):
                n0 = k * (NCH * E) + c * E
                cols = bass.ds(c * CW, CW)

                def up(e):
                    for h, l, o in ((w1h, w1l, S[e % 2]), (w2h, w2l, S[2 + e % 2])):
                        mm(o[:, 0:CW], h[:, e * HID:(e + 1) * HID], xn_hl[:, cols], True, False)
                        ins = mm(o[:, 0:CW], l[:, e * HID:(e + 1) * HID], xn_hl[:, cols], False, True)
                    ins.then_inc(s["up_done"], 1)

                def bcast(e):
                    mm(Y1[:, 0:CW], pick[:, e * 128:(e + 1) * 128], dT[:, cols]).then_inc(s["bcast_done"], 1)

                pe.wait_ge(s["disp_cm"], (k + 1) * NCH)
                up(0)
                bcast(0)
                for e in range(E):
                    if samples and e % 8 == 4:
                        sample_tr(*samples[e // 8])
                    if samples and e % 8 == 5:
                        sample_conv(*samples[e // 8])
                    if e + 1 < E:
                        up(e + 1)
                    pe.wait_ge(s["hid_done"], n0 + e + 1)
                    if e + 1 < E:
                        bcast(e + 1)
                    if e % 2:
                        for b in range(2):
                            f = e - 1 + b
                            ins = mm(Y0[b * C:(b + 1) * C, 0:CW], w3s[:, f, :], hid[:, f % 4, :], f < 2, f >= E - 2)
                ins.then_inc(s["ycm_done"], 1)
                pe.wait_ge(s["ycm_ready"], k * NCH + c + 1)
                for t in range(CT):
                    ins = mm(Y0[0:TP, t * C:(t + 1) * C], om_cm[:, t * TP:(t + 1) * TP], ident2[:, :])
                ins.then_inc(s["ytm_done"], 1)
                pe.wait_ge(s["x2_added"], k * NCH + c + 1)

            def ffn(b):
                for t in range(T):
                    for w in (wrh, wrl):
                        ins = mm(D0[0:TP, t:t + 1], xn_hl[:, t * TP:(t + 1) * TP], w[:, 0:1], w is wrh, w is wrl)
                ins.then_inc(s["route_done"], 1)

                def up(c):
                    for m in range(2):
                        o = S[(2 * c + m) % 4][:, 0:CW]
                        mm(o, f1h[:, m * 128:(m + 1) * 128], xn_hl[:, c * CW:(c + 1) * CW], True, False)
                        mm(o, f1l[:, m * 128:(m + 1) * 128], xn_hl[:, c * CW:(c + 1) * CW], False, True).then_inc(s["fup_done"], 1)

                up(0)
                for c in range(NCH):
                    if c >= 1 and c + 1 < NCH:
                        pe.wait_ge(s["gelu_done"], b * (2 * NCH) + 2 * c)
                    if c + 1 < NCH:
                        up(c + 1)
                    if c >= 2:
                        pe.wait_ge(s["yw_done"], b * NCH + c - 1)
                    pe.wait_ge(s["gelu_done"], b * (2 * NCH) + 2 * c + 2)
                    for t in range(CT):
                        for m in range(2):
                            ins = mm((Y0, Y1)[c % 2][0:TP, t * C:(t + 1) * C], hid[:, (2 * c + m) % 4, t * TP:(t + 1) * TP],
                                     f2s[:, m, :], m == 0, m == 1)
                    ins.then_inc(s["fdown_done"], 1)

            def image(k, back):
                n0 = 4 * k - (1 if back else 0)
                tr0 = k * (6 * NCH) - (NCH if back else 0)
                def stacks(c, first=False):
                    pe.wait_ge(s["split_done"], n0 + 1)
                    for i, kind in enumerate(("hl", "hh", "ll")):
                        if not first:
                            pe.wait_ge(s["tr_cm"], tr0 + c * 3 + (i - 2))
                        for n in range(CT):
                            ins = transpose_tile(S[i][:, n * TP:(n + 1) * TP], c * CT + n, kind)
                        ins.then_inc(s["tr_done"], 1)

                stacks(0, True)
                with pe.Fori(1, NCH) as c:
                    stacks(c)
                pe.wait_ge(s["tr_cm"], tr0 + 3 * NCH)
                mixer(k, back)
                pe.wait_ge(s["split_done"], n0 + 2)
                transpose_all(tr0 + 3 * NCH)
                pe.wait_ge(s["tr_cm"], tr0 + 4 * NCH)
                for t in range(T):
                    for w in (gateh, gatel):
                        ins = mm(D0[0:TP, t * E:(t + 1) * E], xn_hl[:, t * TP:(t + 1) * TP], w[:, :], w is gateh, w is gatel)
                ins.then_inc(s["logits_done"], 1)
                pe.wait_ge(s["disp_split"], k + 1)
                for c in range(NCH):
                    if c >= 4:
                        pe.wait_ge(s["disp_cm"], k * NCH + c - 3)
                    for i in range(CT):
                        ins = mm(S[c % 4][0:2 * E, i * TP:(i + 1) * TP], dsplit[:, c * CT + i, :], ident16[:, :])
                    ins.then_inc(s["disp_tr"], 1)
                with pe.Fori(0, NCH) as c:
                    experts_chunk(k, c, [(k - 1, c * 2 + 14 + q) for q in range(2)] if back else None)
                if back:
                    pe.wait_ge(s["split_done"], n0 + 3)
                    transpose_all(tr0 + 4 * NCH)
                    pe.wait_ge(s["tr_cm"], tr0 + 5 * NCH)
                    ffn(k - 1)
                bk = 1 if back else 0
                pe.wait_ge(s["split_done"], n0 + 3 + bk)
                transpose_all(tr0 + (4 + bk) * NCH)
                pe.wait_ge(s["tr_cm"], tr0 + (5 + bk) * NCH)
                for g in range(2):
                    nt = 4 if g == 0 else NCH - 4
                    for tap in range(TAPS):
                        for w in (offh, offl):
                            for i in range(nt):
                                y = 8 * (4 * g + i) + tap // 3
                                ins = mm(S[g][i * OC:(i + 1) * OC, 0:CW].rearrange("p (y x) -> p y x", x=W), w[:, tap * OC:(tap + 1) * OC],
                                         pad_v[:, y:y + 8, tap % 3:tap % 3 + W], tap == 0 and w is offh, tap == TAPS - 1 and w is offl)
                    ins.then_inc(s["om_done"], 1)
                for g in range(2):
                    rows = 128 if g == 0 else OC * (NCH - 4)
                    pe.wait_ge(s["om_ready"], k * 2 + g + 1)
                    for i in range(CT):
                        ins = P.transpose(S[2 + g][0:TP, i * 128:i * 128 + rows], om_c[g][0:rows, i * TP:(i + 1) * TP], ident[0:rows, 0:rows])
                    ins.then_inc(s["om_tr"], 1)
                pe.wait_ge(s["geo_done"], k + 1)

            pe.wait_ge(s["w_loaded"], 16 * 15)
            pe.wait_ge(s["const_done"], 1)
            image(0, False)
            with pe.Fori(1, B) as k:
                image(k, True)
            with pe.Fori(0, T) as t:
                sample_tr(B - 1, t)
                sample_conv(B - 1, t)
            pe.wait_ge(s["split_done"], 4 * B)
            transpose_all(B * 6 * NCH - NCH)
            pe.wait_ge(s["tr_cm"], B * 6 * NCH)
            ffn(B - 1)
            def count_tokens():
                return mm(D0[0:TP, 0:B], ones16[:, :], cnt16[:, :]).then_inc(s["count_done"], 1)

            pe.wait_ge(s["count_in"], 1)
            count_tokens()
            with pe.Fori(0, 32) as i:
                pe.wait_ge(s["count_in"], i + 2)
                count_tokens()
            pe.wait_ge(s["tie_in"], 1)
            mm(D0[0:TP, 0:B * T], tri16[:, :], eq16[:, :])
            mm(D1[0:TP, 0:B * T], ones16[:, :], eq16[:, :]).then_inc(s["tie_done"], 1)


def kernel(**inputs):
    import numpy as _np
    import concourse.bacc as _bacc
    from concourse import mybir as _mybir
    from concourse.bass_utils import run_bass_kernel_spmd as _run

    a = {n: _np.ascontiguousarray(v) for n, v in inputs.items()}
    B, H, W, C = a["x"].shape
    T, TP, E = H // 2, 2 * W, a["L0_ffn_w1"].shape[0]
    p, t, tap = _np.arange(TP)[:, None, None], _np.arange(T)[None, :, None], _np.arange(9)[None, None, :]
    grid = _np.zeros((TP, T, 18), _np.float32)
    grid[:, :, 0::2] = 2 * t + p // W + tap // 3
    grid[:, :, 1::2] = p % W + tap % 3
    pick = _np.zeros((2 * E, E, 128), _np.float32)
    for e in range(E):
        pick[e, e, :] = pick[E + e, e, :] = 1
    arrays = {
        "x": a["x"], "conv_w": a["L0_conv_W"], "gate_w": a["L0_ffn_gate_w"], "gate_b": a["L0_ffn_gate_b"].reshape(1, -1),
        "w1": a["L0_ffn_w1"], "w2": a["L0_ffn_w2"], "w3": a["L0_ffn_w3"],
        "off_w": a["L1_conv_offset_w"].reshape(9 * C, 27), "off_b": a["L1_conv_offset_b"].reshape(1, 27),
        "dcn_w": _np.ascontiguousarray(a["L1_conv_dcn_weight"].transpose(2, 3, 1, 0)).reshape(9 * C, C),
        "wr": a["L1_ffn_wr"], "br": a["L1_ffn_br"].reshape(1, 1), "f1": a["L1_ffn_w1"], "fb1": a["L1_ffn_b1"].reshape(-1, 1),
        "f2": a["L1_ffn_w2"], "fb2": a["L1_ffn_b2"].reshape(1, -1),
        "ident_in": _np.eye(128, dtype=_np.float32), "grid_in": grid,
        "rank_in": _np.tile(_np.arange(E, 0, -1, dtype=_np.float32), (TP, 1)), "pick_in": pick.reshape(2 * E, E * 128),
        "tri_in": _np.triu(_np.ones((TP, TP), _np.float32), 1),
        "bits_in": _np.tile((2.0 ** _np.arange(30, -1, -1)).astype(_np.float32), (TP, 1)),
    }
    nc = _bacc.Bacc("TRN2", target_bir_lowering=False, num_devices=1)
    args = {n: nc.dram_tensor(n, v.shape, _mybir.dt.from_np(v.dtype), kind="ExternalInput").ap() for n, v in arrays.items()}
    out = nc.dram_tensor("out", (B, H, W, C), _mybir.dt.float32, kind="ExternalOutput").ap()
    metaformer_kernel(nc, **args, out=out)
    r = _run(nc, [arrays], core_ids=[0])
    return r.results[0]["out"]
```

```python
from contextlib import ExitStack

import numpy as np
import concourse.bass as bass
from concourse import mybir

ACT_STEPS = (1, 4, 7)
SAMPLE_STEPS = (0, 2, 3, 5, 6)
EVAC_STEPS = (1, 2, 4, 5)
ADD_STEP = 7
WEIGH_STEPS = (1, 3, 7)


def metaformer_kernel(nc, x, conv_w, gate_w, gate_b, w1, w2, w3, off_w, off_b, dcn_w, wr, br, f1, fb1, f2, fb2,
                      ident_in, grid_in, rank_in, pick_in, tri_in, bits_in, out):
    f32, f16, i32, u32 = mybir.dt.float32, mybir.dt.float16, mybir.dt.int32, mybir.dt.uint32
    ALU, ACT, AX = mybir.AluOpType, mybir.ActivationFunctionType, mybir.AxisListType

    B, H, W, C = x.shape
    N = H * W
    TP = 2 * W
    T = N // TP
    E, HID = w1.shape[0], w1.shape[2]
    FH = f1.shape[1]
    TAPS = 9
    CT = 4
    CW = CT * TP
    NCH = T // CT
    IW = 392
    JB = 4
    SPB = 2 * JB
    BPH = T // JB
    SPH = SPB * BPH
    SPI = 2 * SPH
    OC = 32
    SIDE = W + 2
    XS = 256.0
    KTOP = int(0.5 * N) - 1
    LNC_EPS, LNT_EPS = 1e-6, 1e-5
    MOE1, MOE2, GATE, OFF, FFN1, ROUTE = range(6)
    NW = 6
    ACT_N = len(ACT_STEPS)
    DVE_STEPS = tuple(u for u in range(SPB) if u not in ACT_STEPS)
    DVE_N = len(DVE_STEPS)

    table = nc.dram_tensor("corner_table", [SIDE * SIDE, 4 * C], f32).ap()
    x3_dram = nc.dram_tensor("x3_scratch", [B, N, C], f32).ap()
    yw_dram = nc.dram_tensor("yw_scratch", [B, N, C], f32).ap()

    ctx = ExitStack()
    with ctx:
        def sb(name, shape, dt=f32):
            return ctx.enter_context(nc.sbuf_tensor(name, shape, dt))

        ident = sb("ident", [128, 128])
        ident2 = sb("ident2", [128, C])
        ident16 = sb("ident16", [TP, TP], f16)
        ones16 = sb("ones16", [TP, TP], f16)
        tri16 = sb("tri16", [TP, TP], f16)
        pick = sb("pick", [128, E * C], f16)
        zero16 = sb("zero16", [128, IW], f16)
        grid = sb("grid", [TP, T, 2 * TAPS])
        rank = sb("rank", [TP, E])
        bits = sb("bits", [TP, 31], i32)
        w_mix = sb("w_mix", [C, C])
        w1h = sb("w1h", [128, E * HID], f16)
        w1l = sb("w1l", [128, E * HID], f16)
        w2h = sb("w2h", [128, E * HID], f16)
        w2l = sb("w2l", [128, E * HID], f16)
        w3s = sb("w3s", [HID, E, C])
        gateh = sb("gateh", [128, E], f16)
        gatel = sb("gatel", [128, E], f16)
        gbias = sb("gbias", [TP, E])
        offh = sb("offh", [128, TAPS * OC], f16)
        offl = sb("offl", [128, TAPS * OC], f16)
        obias = sb("obias", [TP, 27])
        dcn = sb("dcn", [128, TAPS, C])
        wrh = sb("wrh", [128, 2], f16)
        wrl = sb("wrl", [128, 2], f16)
        brc = sb("brc", [TP, 1])
        f1h = sb("f1h", [128, FH], f16)
        f1l = sb("f1l", [128, FH], f16)
        fb1c = sb("fb1c", [128, 2])
        f2s = sb("f2s", [128, 2, C])
        fb2r = sb("fb2r", [TP, C])
        amax = sb("amax", [128, NW])
        amin = sb("amin", [128, NW])
        amax_all = sb("amax_all", [128, NW])
        wscale = sb("wscale", [128, NW])
        descale = sb("descale", [128, NW])

        xin = sb("xin", [TP, T, C])
        xln = sb("xln", [TP, T, C])
        tmp = sb("tmp", [TP, T, C])
        x1 = sb("x1", [TP, T, C])
        xB = sb("xB", [TP, T, C])
        yw = sb("yw", [TP, T, C])
        st = sb("st", [TP, 8, T])
        split = sb("split", [TP, T, 4 * C], f16)
        xn_hl = sb("xn_hl", [128, N], f16)
        xn_hh = sb("xn_hh", [128, N], f16)
        xn_ll = sb("xn_ll", [128, N], f16)
        dT = xn_hh
        padded = sb("padded", [128, SIDE * SIDE], f16)
        pad_v = padded[:, :].rearrange("p (y x) -> p y x", x=SIDE)
        work = sb("work", [128, 8 * IW])
        relu = work[0:TP, 0:4 * IW].rearrange("p (q b n) -> p q b n", q=2, b=2)
        sq = work[0:TP, 4 * IW:8 * IW].rearrange("p (q b n) -> p q b n", q=2, b=2)
        silu = work[:, 0:2 * CW].rearrange("p (q n) -> p q n", q=2)
        hid = work[:, 2 * CW:6 * CW].rearrange("p (q n) -> p q n", q=4)
        xj = sb("xj", [TP, 2, JB, C])
        small = sb("small", [TP, 5, 2 * TAPS * T])
        z_cm = small[0:C, 0:4, :].rearrange("p a b -> p (a b)")[:, 0:4 * IW]
        smallc = sb("smallc", [TP, 8, T])
        disp = sb("disp", [TP, T, E])
        dsplit = sb("dsplit", [TP, T, 2 * E], f16)
        om = sb("om", [TP, T, OC])
        mask = sb("mask", [TP, T, TAPS])
        om_cm = sb("om_cm", [128, CW])
        om_c = (om_cm, silu[:, 0, :])
        corner_w = sb("corner_w", [TP, T * TAPS, 4])
        index = sb("index", [TP, T * TAPS], u32)
        pool_cell = sb("pool_cell", [TP, 5])
        index_now = sb("index_now", [TP, 2, TAPS], u32)
        G = sb("G", [128, 2, 4 * TAPS * C])
        stage, stage2 = G[:, 0, :], G[:, 1, :]
        val_cm = sb("val_cm", [128, TAPS * TP])
        dcn_cm = sb("dcn_cm", [128, TP])
        share = sb("share", [128, 2, CW])
        scaled_y = sb("scaled_y", [128, 2, CW])
        w_all = sb("w_all", [TP, B, T])
        key = small[:, 0, 0:B * T].rearrange("p (b t) -> p b t", b=B)
        hit = small[:, 1, 0:B * T].rearrange("p (b t) -> p b t", b=B)
        eqf = small[:, 2, 0:B * T].rearrange("p (b t) -> p b t", b=B)
        tot = small[:, 3, 0:B * T].rearrange("p (b t) -> p b t", b=B)
        pre = small[:, 4, 0:B * T].rearrange("p (b t) -> p b t", b=B)
        sel = sb("sel", [TP, B, T])
        eq16 = sb("eq16", [TP, B * T], f16)
        kf = sb("kf", [TP, 8, B])
        ki = sb("ki", [TP, 3, B], i32)
        cnt16 = sb("cnt16", [TP, B], f16)

        PS = [ctx.enter_context(nc.psum_tensor(f"PS{i}", [128, 2, 512], f32)) for i in range(4)]
        S = [PS[0][:, 0, :], PS[0][:, 1, :], PS[1][:, 0, :], PS[1][:, 1, :]]
        Y0, Y1, D0, D1 = PS[2][:, 0, :], PS[2][:, 1, :], PS[3][:, 0, :], PS[3][:, 1, :]

        s = {n: ctx.enter_context(nc.semaphore(n)) for n in """
            w_loaded w_staged w_taken amax_done amax_red stage_zero table_zeroed const_done
            x_loaded x1_added var_done std_done scaled h_cast split_done tr_done tr_cm
            sim_done relu_done sq_act sq_dve mixed xj_ready z_done z_ready y_done
            logits_done sm_shift sm_exp disp_split disp_tr disp_cm
            up_done silu_done hid_done share_done share_ready down_done scaled_done ytm_done x2_added
            geo_ln pad_ready om_done om_ready om_tr om_taken mask_in mask_out geo_done xb_copied
            table_written gath0 gath1 cell_done pool_step weighted val_tr val_ready conv_done conv_ready dcn_done
            route_done route_taken fup_done gelu_done fdown_done yw_done skip_added x3_stored yw_stored
            count_in count_done tie_in tie_done x3_back0 x3_back1 yw_back0 yw_back1 fin_ready out_stored0
            out_stored1""".split()}
        gath = (s["gath0"], s["gath1"])
        V, A, P, GP = nc.vector, nc.scalar, nc.tensor, nc.gpsimd
        block = ctx.enter_context(nc.Block())

        def bc(ap, axis, n):
            v = ap.unsqueeze(axis)
            shape = list(v.shape)
            shape[axis] = n
            return v.to_broadcast(shape)

        def tm_dram(t, k):
            return t[bass.ds(k, 1), :, :].rearrange("a (t p) c -> p (a t) c", p=TP)


        @block.sync
        def _(sp):
            x_flat = x.rearrange("b h w c -> b (h w) c")

            def load_x(k):
                sp.dma_start(xin[:, :, :], tm_dram(x_flat, k)).then_inc(s["x_loaded"], 16)

            def write_table(k):
                sp.wait_ge(s["geo_ln"], k + 1)
                for slot, (dy, dx) in enumerate(((1, 1), (1, 0), (0, 1), (0, 0))):
                    tv = table.rearrange("(y x) (s c) -> x y s c", x=SIDE, c=C)
                    for r in range(2):
                        dst = tv[dx:dx + W, dy + r:dy + r + H, slot, :].rearrange("x (t two) c -> x t two c", two=2)[:, :, 0, :]
                        sp.dma_start(dst, xln[r * W:(r + 1) * W, :, :]).then_inc(s["table_written"], 16)

            def back_stores(b):
                sp.wait_ge(s["skip_added"], b + 1)
                sp.dma_start(tm_dram(x3_dram, b), xB[:, :, :]).then_inc(s["x3_stored"], 16)
                sp.wait_ge(s["yw_done"], (b + 1) * NCH)
                sp.dma_start(tm_dram(yw_dram, b), yw[:, :, :]).then_inc(s["yw_stored"], 16)

            load_x(0)
            loads = [(ident[:, :], ident_in), (ident2[0:C, :], ident_in[0:C, 0:C]), (ident2[C:128, :], ident_in[0:C, 0:C]),
                     (grid[:, :, :], grid_in), (rank[:, :], rank_in), (w_mix[:, :], conv_w),
                     (w3s[:, :, :], w3.rearrange("e h c -> h e c")),
                     (gbias[:, :], gate_b.to_broadcast([TP, E])), (obias[:, :], off_b.to_broadcast([TP, 27])),
                     (dcn[0:C, :, :], dcn_w.rearrange("(n k) c -> k n c", k=C)),
                     (dcn[C:128, :, :], dcn_w.rearrange("(n k) c -> k n c", k=C)),
                     (brc[:, :], br.to_broadcast([TP, 1])), (fb1c[:, :], fb1.rearrange("(m p) o -> p (m o)", p=128)),
                     (f2s[:, :, :], f2.rearrange("(m k) c -> k m c", m=2)),
                     (fb2r[:, :], fb2.to_broadcast([TP, C]))]
            with nc.allow_non_contiguous_dma(reason="small constants"):
                for dst, src in loads:
                    sp.dma_start(dst, src).then_inc(s["w_loaded"], 16)
            for w, dst in ((w1, stage), (w2, stage2)):
                for h in range(2):
                    sp.dma_start(dst[h * C:(h + 1) * C, 0:E * HID].rearrange("c (e h) -> c e h", e=E),
                                 w.rearrange("e c h -> c e h")).then_inc(s["w_staged"], 16)
            sp.wait_ge(s["w_taken"], 1)
            with nc.allow_non_contiguous_dma(reason="small weights"):
                for h in range(2):
                    r = slice(h * C, (h + 1) * C)
                    for dst, src in ((stage[r, 0:E], gate_w), (stage[r, 768:769], wr), (stage[r, 1024:1024 + FH], f1),
                                     (stage[r, 64:64 + TAPS * OC].rearrange("c (t o) -> c t o", o=OC)[:, :, 0:27],
                                      off_w.rearrange("(t c) o -> c t o", c=C))):
                        sp.dma_start(dst, src).then_inc(s["w_staged"], 16)
            sp.dma_start(stage2[0:TP, 0:TP], tri_in).then_inc(s["w_staged"], 16)
            sp.dma_start(stage2[0:TP, 128:159], bits_in).then_inc(s["w_staged"], 16)
            sp.wait_ge(s["w_taken"], 2)
            sp.dma_start(stage2[0:2 * E, 0:E * C], pick_in).then_inc(s["w_staged"], 16)
            sp.wait_ge(s["stage_zero"], 1)
            tz = table.rearrange("e n -> (e n)").rearrange("(p n) -> p n", p=128)
            pieces = range(0, tz.shape[1], 1682)
            for a in pieces:
                sp.dma_start(tz[:, a:a + 1682], stage[:, 0:1682]).then_inc(s["table_zeroed"], 16)
            sp.wait_ge(s["table_zeroed"], 16 * len(pieces))

            def image(k, has_back, has_next):
                if has_next:
                    sp.wait_ge(s["x1_added"], 4 * (k + 1))
                    load_x(k + 1)
                if has_back:
                    back_stores(k - 1)
                write_table(k)

            image(0, False, True)
            with sp.Fori(1, B - 1) as k:
                image(k, True, True)
            image(B - 1, True, False)
            back_stores(B - 1)
            sp.wait_ge(s["x3_stored"], 16 * B)
            sp.wait_ge(s["yw_stored"], 16 * B)
            for k in range(B):
                q = k % 2
                if k >= 2:
                    sp.wait_ge(s[f"out_stored{q}"], 16 * (k // 2))
                sp.dma_start((x1, xin)[q][:, :, :], tm_dram(x3_dram, k)).then_inc(s[f"x3_back{q}"], 16)
                sp.dma_start((tmp, xln)[q][:, :, :], tm_dram(yw_dram, k)).then_inc(s[f"yw_back{q}"], 16)

        @block.gpsimd
        def _(pool):
            for n in range(2):
                pool.wait_ge(s["amax_done"], n + 1)
                a, b = ((0, 2), (2, NW))[n]
                GP.partition_all_reduce(amax_all[:, a:b], amax[:, a:b], 128, bass.bass_isa.ReduceOp.max).then_inc(s["amax_red"], 1)

            def step(cell):
                GP.tensor_tensor(pool_cell[:, cell:cell + 1], pool_cell[:, 0:1], pool_cell[:, 0:1], ALU.add).then_inc(s["pool_step"], 1)

            def gather_tile(b, u, q, first=False):
                n = (b * T + u * 2 + q) * 3
                if not first:
                    pool.wait_ge(s["val_tr"], (b * T + u * 2 + (q - 1)) * 3)
                step(1 + q)
                GP.tensor_copy(index_now[:, q, :], index[:, bass.ds((u * 2 + q) * TAPS, TAPS)]).then_inc(s["pool_step"], 1)
                pool.wait_ge(s["pool_step"], n + 2)
                step(3 + q)
                for tap in range(TAPS):
                    GP.indirect_dma_start(G[0:TP, q, tap * 4 * C:(tap + 1) * 4 * C], None, table,
                                          bass.IndirectOffsetOnAxis(ap=index_now[:, q, tap:tap + 1], axis=0)).then_inc(gath[q], 16)

            GP.memset(pool_cell[:, :], 0.0).then_inc(s["cell_done"], 1)
            pool.wait_ge(s["cell_done"], 1)
            with pool.Fori(0, B) as b:
                pool.wait_ge(s["geo_done"], b + 1)
                pool.wait_ge(s["table_written"], (b + 1) * 128)
                for q in range(2):
                    gather_tile(b, 0, q, first=True)
                with pool.Fori(1, T // 2) as u:
                    for q in range(2):
                        gather_tile(b, u, q)

        @block.vector
        def _(dve):
            def step(ins):
                dve.drain()
                return ins

            red = lambda o, i, op=ALU.add: V.tensor_reduce(o, i, AX.X, op)

            def split_weights(h, l, src, col):
                V.tensor_scalar(h, src, wscale[:, col:col + 1], None, ALU.mult)
                dve.drain()
                V.scalar_tensor_tensor(l, src, wscale[:, col:col + 1], h, ALU.mult, ALU.subtract)

            def scales(a, b):
                V.tensor_scalar(amax_all[:, a:b], amax_all[:, a:b], 1e-30, None, ALU.max)
                dve.drain()
                V.tensor_scalar(descale[:, a:b].bitcast(i32), amax_all[:, a:b].bitcast(i32), 0x7F800000, None, ALU.bitwise_and)
                dve.drain()
                V.tensor_scalar(wscale[:, a:b].bitcast(i32), descale[:, a:b].bitcast(i32), -1.0, float(262 << 23), ALU.mult, ALU.add)
                dve.drain()
                V.tensor_scalar(descale[:, a:b], descale[:, a:b], 1.0 / (256.0 * XS), None, ALU.mult)
                dve.drain()

            def magnitudes(tensors):
                for col, src in tensors:
                    red(amax[:, col:col + 1], src, ALU.max)
                    red(amin[:, col:col + 1], src, ALU.min)
                dve.drain()
                for col, _src in tensors:
                    V.scalar_tensor_tensor(amax[:, col:col + 1], amin[:, col:col + 1], -1.0, amax[:, col:col + 1], ALU.mult, ALU.max)

            V.memset(padded[:, :], 0.0)
            V.memset(zero16[:, :], 0.0)
            V.memset(ones16[:, :], 1.0)
            V.memset(pick[:, :], 0.0)
            dve.wait_ge(s["w_staged"], 16 * 4)
            magnitudes(((MOE1, stage[:, 0:E * HID]), (MOE2, stage2[:, 0:E * HID])))
            dve.drain()
            V.memset(cnt16[:, :], 0.0).then_inc(s["amax_done"], 1)
            dve.wait_ge(s["amax_red"], 1)
            scales(0, 2)
            split_weights(w1h[:, :], w1l[:, :], stage[:, 0:E * HID], MOE1)
            split_weights(w2h[:, :], w2l[:, :], stage2[:, 0:E * HID], MOE2)
            dve.drain()
            V.memset(stage[:, 0:1280], 0.0).then_inc(s["w_taken"], 1)
            dve.wait_ge(s["w_staged"], 16 * (4 + 10))
            dve.wait_ge(s["w_loaded"], 16 * 15)
            pieces = ((GATE, gateh[:, :], gatel[:, :], stage[:, 0:E]), (OFF, offh[:, :], offl[:, :], stage[:, 64:64 + TAPS * OC]),
                      (FFN1, f1h[:, :], f1l[:, :], stage[:, 1024:1024 + FH]), (ROUTE, wrh[:, 0:1], wrl[:, 0:1], stage[:, 768:769]))
            magnitudes([(col, src) for col, _h, _l, src in pieces])
            V.tensor_copy(ident16[:, :], ident[0:TP, 0:TP])
            V.tensor_copy(tri16[:, :], stage2[0:TP, 0:TP])
            V.tensor_copy(bits[:, :], stage2[0:TP, 128:159])
            dve.drain()
            V.memset(cnt16[:, :], 0.0).then_inc(s["amax_done"], 1)
            dve.wait_ge(s["amax_red"], 2)
            scales(2, NW)
            for col, h, l, src in pieces:
                split_weights(h, l, src, col)
            dve.drain()
            V.memset(cnt16[:, :], 0.0).then_inc(s["w_taken"], 1)
            V.memset(stage[:, :], 0.0).then_inc(s["stage_zero"], 1)
            dve.wait_ge(s["w_staged"], 16 * (4 + 11))
            V.tensor_copy(pick[0:2 * E, :], stage2[0:2 * E, 0:E * C])
            dve.drain()
            V.memset(cnt16[:, :], 0.0).then_inc(s["const_done"], 1)

            def weigh(b, t, q, u, third):
                if third == 0:
                    dve.wait_ge(gath[q], b * (TAPS * 16 * T // 2) + (u + 1) * (TAPS * 16))
                n = 4 * TAPS // 3
                g = G[0:TP, q, :].rearrange("p (n c) -> p n c", c=C)[:, third * n:(third + 1) * n, :]
                w = corner_w[:, :, :].rearrange("p n s -> p (n s)")[:, bass.ds(t * (4 * TAPS) + third * n, n)]
                ins = V.tensor_tensor(g, g, bc(w, 2, C), ALU.mult)
                if third == 2:
                    ins.then_inc(s["weighted"], 1)

            def sample_add(b, t):
                dve.wait_ge(s["dcn_done"], b * T + t + 1)
                xt = xB[:, :, :].rearrange("p t c -> p (t c)")[:, bass.ds(t * C, C)]
                V.tensor_tensor(xt, xt, D0[0:TP, 448:448 + C], ALU.add)

            def layer_norm(src, eps, rounds):
                red(st[:, 0, :], src)
                dve.drain()
                V.tensor_scalar(st[:, 1, :], st[:, 0, :], 1.0 / C, None, ALU.mult)
                dve.drain()
                V.tensor_tensor(xln[:, :, :], src, bc(st[:, 1, :], 2, C), ALU.subtract)
                dve.drain()
                V.tensor_tensor(tmp[:, :, :], xln[:, :, :], xln[:, :, :], ALU.mult)
                dve.drain()
                red(st[:, 2, :], tmp[:, :, :])
                dve.drain()
                V.tensor_scalar(st[:, 3, :], st[:, 2, :], 1.0 / C, eps, ALU.mult, ALU.add).then_inc(s["var_done"], 1)
                dve.wait_ge(s["std_done"], rounds + 1)
                V.reciprocal(st[:, 5, :], st[:, 4, :])
                dve.drain()
                V.tensor_tensor(xln[:, :, :], xln[:, :, :], bc(st[:, 5, :], 2, C), ALU.mult)

            def split_l(n, twice):
                dve.wait_ge(s["h_cast"], n + 1)
                if twice:
                    V.tensor_tensor(split[:, :, 2 * C:4 * C].rearrange("p t (a c) -> p t a c", a=2), bc(tmp[:, :, :], 2, 2),
                                    split[:, :, 0:2 * C].rearrange("p t (a c) -> p t a c", a=2), ALU.subtract).then_inc(s["split_done"], 1)
                else:
                    V.tensor_tensor(split[:, :, 2 * C:3 * C], tmp[:, :, :], split[:, :, C:2 * C], ALU.subtract).then_inc(s["split_done"], 1)

            def mixer_norm(k, r, n):
                dve.wait_ge(s["x_loaded"], (k + 1) * 16)
                layer_norm(xin[:, :, :], LNC_EPS, r)
                V.tensor_tensor(st[:, 6, :], st[:, 2, :], st[:, 5, :], ALU.mult)
                dve.drain()
                V.tensor_tensor(st[:, 6, :], st[:, 6, :], st[:, 5, :], ALU.mult)
                dve.drain()
                V.tensor_scalar(st[:, 3, :], st[:, 6, :], 1e-12, None, ALU.max).then_inc(s["var_done"], 1)
                dve.wait_ge(s["std_done"], r + 2)
                V.reciprocal(st[:, 5, :], st[:, 4, :])
                dve.drain()
                V.tensor_scalar(st[:, 5, :], st[:, 5, :], XS, None, ALU.mult)
                dve.drain()
                V.tensor_tensor(tmp[:, :, :], xln[:, :, :], bc(st[:, 5, :], 2, C), ALU.mult).then_inc(s["scaled"], 1)
                split_l(n, True)

            def norm_and_split(src, eps, r, n):
                layer_norm(src, eps, r)
                dve.drain()
                V.tensor_scalar(tmp[:, :, :], xln[:, :, :], XS, None, ALU.mult).then_inc(s["scaled"], 1)
                split_l(n, False)

            def mixer_body(g, half_no, tile, nxt):
                for u in range(SPB):
                    if u in DVE_STEPS:
                        dve.wait_ge(s["relu_done"], g + u + 1)
                        dve.wait_ge(s["mixed"], 2 * half_no + g + u + 1)
                        V.tensor_tensor(sq[:, u % 2], relu[:, u % 2], relu[:, u % 2], ALU.mult).then_inc(s["sq_dve"], 1)
                    if tile and u == ADD_STEP:
                        sample_add(*tile)
                    if nxt and u in WEIGH_STEPS:
                        weigh(*nxt, WEIGH_STEPS.index(u))

            def mixer(k, back):
                if back:
                    for third in range(3):
                        weigh(k - 1, 0, 0, 0, third)
                for half in range(2):
                    g0 = k * SPI + half * SPH
                    t0 = half * BPH

                    def body(j, n):
                        q = (t0 + n + 1) % 2
                        u = (j + (t0 + 1 - q)) // 2 if isinstance(j, int) else None
                        return q, u

                    with dve.Fori(0, BPH // 2) as bb:
                        for v in range(2):
                            j = bb * 2 + v
                            nt = t0 + v + 1
                            nxt = (k - 1, bb * 2 + nt, nt % 2, bb + nt // 2) if back else None
                            mixer_body(g0 + j * SPB, k * 2 + half, (k - 1, j + t0) if back else None, nxt)
                    j = BPH - 1
                    nt = t0 + j + 1
                    mixer_body(g0 + j * SPB, k * 2 + half, (k - 1, t0 + j) if back else None,
                               (k - 1, nt, nt % 2, nt // 2) if back else None)
                    for m in range(2):
                        dve.wait_ge(s["y_done"], k * 4 + half * 2 + m + 1)
                        r = slice(half * 14 + m * 7, half * 14 + m * 7 + 7)
                        V.tensor_tensor(x1[:, r, :], xin[:, r, :], S[m][0:TP, 0:7 * C].rearrange("p (t c) -> p t c", c=C),
                                        ALU.add).then_inc(s["x1_added"], 1)

            def gate(k):
                p = small[:, 0, 0:T * E].rearrange("p (t e) -> p t e", e=E)
                o1 = small[:, 1, 0:T * E].rearrange("p (t e) -> p t e", e=E)
                o2 = small[:, 2, 0:T * E].rearrange("p (t e) -> p t e", e=E)
                c = small[:, 3, 0:T * E].rearrange("p (t e) -> p t e", e=E)
                m, r, m1, m2, den = (smallc[:, i, :] for i in range(5))

                def tt(o, a, b, op):
                    V.tensor_tensor(o, a, b, op)
                    dve.drain()

                def rd(o, a, op):
                    red(o, a, op)
                    dve.drain()

                def first_max(oh, top, src):
                    rd(top, src, ALU.max)
                    tt(oh, src, bc(top, 2, E), ALU.is_equal)
                    tt(c, oh, bc(rank[:, :], 1, T), ALU.mult)
                    rd(den, c, ALU.max)
                    tt(oh, c, bc(den, 2, E), ALU.is_equal)

                dve.wait_ge(s["logits_done"], k + 1)
                V.tensor_scalar(p, D0[0:TP, 0:T * E].rearrange("p (t e) -> p t e", e=E), descale[0:TP, GATE:GATE + 1], None, ALU.mult)
                dve.drain()
                tt(p, p, bc(gbias[:, :], 1, T), ALU.add)
                rd(m, p, ALU.max)
                V.tensor_tensor(p, p, bc(m, 2, E), ALU.subtract).then_inc(s["sm_shift"], 1)
                dve.wait_ge(s["sm_exp"], k + 1)
                rd(m, p, ALU.add)
                V.reciprocal(r, m)
                dve.drain()
                tt(p, p, bc(r, 2, E), ALU.mult)
                first_max(o1, m1, p)
                V.scalar_tensor_tensor(p, o1, -2.0, p, ALU.mult, ALU.add)
                dve.drain()
                first_max(o2, m2, p)
                tt(den, m1, m2, ALU.add)
                V.reciprocal(r, den)
                dve.drain()
                tt(m1, m1, r, ALU.mult)
                tt(m2, m2, r, ALU.mult)
                tt(o1, o1, bc(m1, 2, E), ALU.mult)
                tt(o2, o2, bc(m2, 2, E), ALU.mult)
                V.scalar_tensor_tensor(disp[:, :, :], o1, 1.0, o2, ALU.mult, ALU.add)
                dve.drain()
                V.tensor_scalar(disp[:, :, :], disp[:, :, :], XS, None, ALU.mult)
                dve.drain()
                V.tensor_copy(dsplit[:, :, 0:E], disp[:, :, :])
                dve.drain()
                V.tensor_tensor(dsplit[:, :, E:2 * E], disp[:, :, :], dsplit[:, :, 0:E], ALU.subtract).then_inc(s["disp_split"], 1)

            def experts_chunk(k, c, tiles, nexts):
                n0 = k * (NCH * E) + c * E
                p0 = k * (NCH * E // 2) + c * (E // 2)

                def scale_pair(p):
                    dve.wait_ge(s["share_ready"], p0 + p + 1)
                    dve.wait_ge(s["down_done"], p0 + p + 1)
                    V.tensor_tensor(scaled_y[:, p % 2, :], Y0[:, 0:CW], share[:, p % 2, :], ALU.mult).then_inc(s["scaled_done"], 1)

                for e in range(E):
                    dve.wait_ge(s["silu_done"], n0 + e + 1)
                    V.scalar_tensor_tensor(hid[:, e % 4, :], S[2 + e % 2][:, 0:CW], descale[:, MOE2:MOE2 + 1], silu[:, e % 2, :],
                                           ALU.mult, ALU.mult).then_inc(s["hid_done"], 1)
                    if e % 2 and e > 1:
                        scale_pair(e // 2 - 1)
                    if tiles and e % 8 == ADD_STEP:
                        sample_add(*tiles[e // 8])
                    if nexts and nexts[e // 8] and e % 8 in WEIGH_STEPS:
                        weigh(*nexts[e // 8], WEIGH_STEPS.index(e % 8))
                scale_pair(E // 2 - 1)
                dve.wait_ge(s["ytm_done"], k * NCH + c + 1)
                xt = x1[:, :, :].rearrange("p t c -> p (t c)")[:, bass.ds(c * (CT * C), CT * C)].rearrange("p (t c) -> p t c", t=CT)
                y = D1[0:TP, :].rearrange("p (t h c) -> p t h c", t=CT, h=2)
                V.tensor_tensor(xt, xt, y[:, :, 0, :], ALU.add)
                dve.drain()
                V.tensor_tensor(xt, xt, y[:, :, 1, :], ALU.add).then_inc(s["x2_added"], 1)

            def geometry(k, has_back):
                base = grid[:, :, :]
                v18 = lambda i: small[:, i, :].rearrange("p (t n) -> p t n", t=T)
                for g in range(2):
                    dve.wait_ge(s["om_tr"], k * 2 + g + 1)
                    nt = 4 if g == 0 else NCH - 4
                    V.tensor_scalar(om[:, 16 * g:16 * g + CT * nt, :].rearrange("p (g s) o -> p g s o", s=CT),
                                    S[2 + g][0:TP, :].rearrange("p (s g o) -> p g s o", s=CT, o=OC)[:, 0:nt],
                                    descale[0:TP, OFF:OFF + 1], None, ALU.mult)
                dve.drain()
                V.tensor_tensor(om[:, :, 0:27], om[:, :, 0:27], bc(obias[:, :], 1, T), ALU.add).then_inc(s["mask_in"], 1)
                dve.drain()
                V.tensor_tensor(v18(0), om[:, :, 0:18], base, ALU.add)
                dve.drain()
                V.tensor_scalar(v18(0), v18(0), 0.0, float(H + 1), ALU.max, ALU.min)
                dve.drain()
                V.tensor_copy(v18(1).bitcast(i32), v18(0))
                dve.drain()
                V.tensor_copy(v18(2), v18(1).bitcast(i32))
                dve.drain()
                V.tensor_tensor(v18(1), v18(2), v18(0), ALU.is_gt)
                dve.drain()
                V.tensor_tensor(v18(1), v18(2), v18(1), ALU.subtract)
                dve.drain()
                V.tensor_tensor(v18(2), v18(0), v18(1), ALU.subtract)
                dve.drain()
                V.tensor_scalar(v18(3), v18(2), -1.0, 1.0, ALU.mult, ALU.add)
                yx = lambda i: small[:, i, :].rearrange("p (n two) -> p n two", two=2)
                V.scalar_tensor_tensor(small[:, 4, 0:T * TAPS], yx(1)[:, :, 0], float(SIDE), yx(1)[:, :, 1], ALU.mult, ALU.add)
                dve.drain()
                V.tensor_copy(index[:, :], small[:, 4, 0:T * TAPS])
                dve.drain()
                dve.wait_ge(s["mask_out"], k + 1)
                m = mask[:, :, :].rearrange("p t n -> p (t n)")
                a0, a1 = small[:, 0, 0:T * TAPS], small[:, 4, 0:T * TAPS]
                V.tensor_tensor(a0, yx(3)[:, :, 0], m, ALU.mult)
                V.tensor_tensor(a1, yx(2)[:, :, 0], m, ALU.mult)
                dve.drain()
                V.tensor_tensor(corner_w[:, :, 0], a0, yx(3)[:, :, 1], ALU.mult)
                V.tensor_tensor(corner_w[:, :, 1], a0, yx(2)[:, :, 1], ALU.mult)
                V.tensor_tensor(corner_w[:, :, 2], a1, yx(3)[:, :, 1], ALU.mult)
                V.tensor_tensor(corner_w[:, :, 3], a1, yx(2)[:, :, 1], ALU.mult)
                if has_back:
                    dve.wait_ge(s["x3_stored"], 16 * k)
                V.tensor_copy(xB[:, :, :], x1[:, :, :])
                dve.drain()
                V.memset(cnt16[:, :], 0.0).then_inc(s["geo_done"], 1)

            def ffn(b, r, n):
                dve.drain()
                norm_and_split(xB[:, :, :], LNT_EPS, r, n)
                V.tensor_tensor(xB[:, :, :], xB[:, :, :], xln[:, :, :], ALU.add).then_inc(s["skip_added"], 1)
                dve.wait_ge(s["route_done"], b + 1)
                w = w_all[:, :, :].rearrange("p b t -> p (b t)")[:, bass.ds(b * T, T)]
                V.tensor_scalar(w, D0[0:TP, 0:T], descale[0:TP, ROUTE:ROUTE + 1], brc[:, 0:1], ALU.mult, ALU.add).then_inc(s["route_taken"], 1)
                dve.wait_ge(s["route_taken"], b + 1)
                for c in range(NCH):
                    dve.wait_ge(s["fdown_done"], b * NCH + c + 1)
                    o = yw[:, c * CT:(c + 1) * CT, :]
                    V.tensor_tensor(o, (Y0, Y1)[c % 2][0:TP, 0:CT * C].rearrange("p (t c) -> p t c", c=C), bc(fb2r[:, :], 1, CT), ALU.add)
                    dve.drain()
                    wc = w_all[:, :, :].rearrange("p b t -> p (b t)")[:, bass.ds(b * T + c * CT, CT)]
                    V.tensor_tensor(o, o, bc(wc, 2, C), ALU.mult).then_inc(s["yw_done"], 1)

            def image(k, back):
                r0 = 5 * k - (1 if back else 0)
                n0 = 4 * k - (1 if back else 0)
                mixer_norm(k, r0, n0)
                mixer(k, back)
                dve.drain()
                norm_and_split(x1[:, :, :], LNT_EPS, r0 + 2, n0 + 1)
                gate(k)
                def chunk(c, last):
                    tiles = [(k - 1, c * 2 + 14 + i) for i in range(2)] if back else None
                    nexts = [(k - 1, c * 2 + 15, 1, c + 7), None if last else (k - 1, c * 2 + 16, 0, c + 8)] if back else None
                    experts_chunk(k, c, tiles, nexts)

                with dve.Fori(0, NCH - 1) as c:
                    chunk(c, False)
                chunk(NCH - 1, True)
                if back:
                    ffn(k - 1, r0 + 3, n0 + 2)
                dve.drain()
                if back:
                    dve.wait_ge(s["table_written"], k * 128)
                layer_norm(x1[:, :, :], LNC_EPS, r0 + 3 + (1 if back else 0))
                dve.drain()
                V.tensor_scalar(tmp[:, :, :], xln[:, :, :], XS, None, ALU.mult).then_inc(s["scaled"], 1)
                V.memset(cnt16[:, :], 0.0).then_inc(s["geo_ln"], 1)
                split_l(n0 + 2 + (1 if back else 0), False)
                geometry(k, back)
                dve.wait_ge(s["table_written"], (k + 1) * 128)
                if back:
                    dve.wait_ge(s["yw_stored"], 16 * k)

            image(0, False)
            with dve.Fori(1, B) as k:
                image(k, True)
            with dve.Fori(0, T // 2) as u:
                for q in range(2):
                    for third in range(3):
                        weigh(B - 1, u * 2 + q, q, u, third)
                    sample_add(B - 1, u * 2 + q)
            ffn(B - 1, 5 * B - 1, 4 * B - 1)

            def count(n, src):
                with nc.allow_low_precision("counts up to T are exact in float16"):
                    red(cnt16[:, :], src)
                dve.drain()
                V.memset(kf[:, 6, :], 0.0).then_inc(s["count_in"], 1)
                dve.wait_ge(s["count_done"], n + 1)

            dve.drain()
            sgn, kth, got, thr, need, zed = (kf[:, i, :] for i in (0, 1, 2, 3, 4, 5))
            V.tensor_scalar(hit, w_all[:, :, :], 0.0, None, ALU.is_ge)
            V.memset(ki[:, 0, :], 0.0)
            dve.drain()
            count(0, hit)
            V.tensor_scalar(got, D0[0:TP, 0:B], float(KTOP), None, ALU.is_ge)
            dve.drain()
            V.tensor_scalar(sgn, got, 2.0, -1.0, ALU.mult, ALU.add)
            V.tensor_scalar(kth, got, float(KTOP - (N - KTOP + 1)), float(N - KTOP + 1), ALU.mult, ALU.add)
            dve.drain()
            V.tensor_tensor(key, w_all[:, :, :], bc(sgn, 2, T), ALU.mult)
            with dve.Fori(0, 31) as i:
                bit = bits[:, bass.ds(i, 1)].to_broadcast([TP, B])
                dve.drain()
                V.tensor_tensor(ki[:, 1, :], ki[:, 0, :], bit, ALU.bitwise_or)
                dve.drain()
                V.tensor_tensor(hit, key, bc(ki[:, 1, :].bitcast(f32), 2, T), ALU.is_ge)
                dve.drain()
                count(i + 1, hit)
                V.tensor_tensor(got, D0[0:TP, 0:B], kth, ALU.is_ge)
                dve.drain()
                V.tensor_tensor(ki[:, 2, :], got, bit, ALU.mult)
                dve.drain()
                V.tensor_tensor(ki[:, 0, :], ki[:, 0, :], ki[:, 2, :], ALU.bitwise_or)
            dve.drain()
            V.tensor_tensor(thr, ki[:, 0, :].bitcast(f32), sgn, ALU.mult)
            dve.drain()
            V.tensor_tensor(sel[:, :, :], w_all[:, :, :], bc(thr, 2, T), ALU.is_gt)
            V.tensor_tensor(eqf, w_all[:, :, :], bc(thr, 2, T), ALU.is_equal)
            dve.drain()
            V.tensor_copy(eq16[:, :], eqf.rearrange("p b t -> p (b t)"))
            count(32, sel[:, :, :])
            V.tensor_scalar(need, D0[0:TP, 0:B], -1.0, float(KTOP), ALU.mult, ALU.add).then_inc(s["tie_in"], 1)
            dve.wait_ge(s["tie_done"], 1)
            V.tensor_copy(pre, D0[0:TP, 0:B * T].rearrange("p (b t) -> p b t", b=B))
            V.tensor_copy(tot, D1[0:TP, 0:B * T].rearrange("p (b t) -> p b t", b=B))
            dve.drain()
            a, o = tot, hit
            V.memset(o[:, :, 0:1], 0.0)
            V.tensor_copy(o[:, :, 1:T], a[:, :, 0:T - 1])
            dve.drain()
            a, o = o, a
            for sh in (1, 2, 4, 8, 16):
                V.tensor_copy(o[:, :, 0:sh], a[:, :, 0:sh])
                V.tensor_tensor(o[:, :, sh:T], a[:, :, sh:T], a[:, :, 0:T - sh], ALU.add)
                dve.drain()
                a, o = o, a
            V.tensor_tensor(pre, pre, a, ALU.add)
            dve.drain()
            V.tensor_tensor(pre, pre, bc(need, 2, T), ALU.is_lt)
            dve.drain()
            V.tensor_tensor(pre, pre, eqf, ALU.mult)
            dve.drain()
            V.tensor_tensor(sel[:, :, :], sel[:, :, :], pre, ALU.add)
            dve.drain()
            for k in range(B):
                q = k % 2
                dve.wait_ge(s[f"x3_back{q}"], 16 * (k // 2 + 1))
                dve.wait_ge(s[f"yw_back{q}"], 16 * (k // 2 + 1))
                xv, yv = (x1, xin)[q][:, :, :], (tmp, xln)[q][:, :, :]
                V.tensor_tensor(yv, yv, bc(sel[:, k, :], 2, C), ALU.mult)
                dve.drain()
                V.tensor_tensor(xv, xv, yv, ALU.add).then_inc(s["fin_ready"], 1)

        @block.scalar
        def _(act):
            def sqrt_round(r):
                act.wait_ge(s["var_done"], r + 1)
                A.activation(st[:, 4, :], st[:, 3, :], ACT.Sqrt).then_inc(s["std_done"], 1)

            def cast_h(n, twice):
                act.wait_ge(s["scaled"], n + 1)
                if twice:
                    A.activation(split[:, :, 0:2 * C].rearrange("p t (a c) -> p t a c", a=2), bc(tmp[:, :, :], 2, 2),
                                 ACT.Copy).then_inc(s["h_cast"], 1)
                else:
                    A.activation(split[:, :, C:2 * C], tmp[:, :, :], ACT.Copy).then_inc(s["h_cast"], 1)

            def sample_evac(b, t, stage):
                if stage < 3:
                    act.wait_ge(s["val_tr"], (b * T + t) * 3 + stage + 1)
                    A.activation(val_cm[:, stage * 3 * TP:(stage + 1) * 3 * TP], D0[:, 0:3 * TP], ACT.Copy).then_inc(s["val_ready"], 1)
                else:
                    act.wait_ge(s["conv_done"], b * T + t + 1)
                    A.activation(dcn_cm[:, :], D0[:, 0:TP], ACT.Copy).then_inc(s["conv_ready"], 1)

            def stage_sources(par, j0):
                A.activation(xj[:, par, :, :].rearrange("p j c -> p (j c)"),
                             xln[:, :, :].rearrange("p t c -> p (t c)")[:, bass.ds(j0 * C, JB * C)], ACT.Copy).then_inc(s["xj_ready"], 1)

            def relu_step(s_no, u):
                act.wait_ge(s["sim_done"], s_no + 1)
                A.activation(relu[:, u % 2], PS[u % 2][0:TP, :, 0:IW], ACT.Relu).then_inc(s["relu_done"], 1)

            def mixer_body(g, body_no, half_no, tile, first, last):
                for u in range(SPB):
                    if u + 1 < SPB or not last:
                        v = (u - 1) % SPB
                        no = body_no + (0 if u else -1)
                        if not (first and u == 0):
                            if v in DVE_STEPS:
                                act.wait_ge(s["sq_dve"], no * DVE_N + DVE_STEPS.index(v) + 1)
                            else:
                                act.wait_ge(s["sq_act"], no * ACT_N + ACT_STEPS.index(v) + 1)
                        relu_step(g + u + 1, u + 1)
                    if u in ACT_STEPS:
                        act.wait_ge(s["relu_done"], g + u + 1)
                        act.wait_ge(s["mixed"], 2 * half_no + g + u + 1)
                        A.activation(sq[:, u % 2], relu[:, u % 2], ACT.Square).then_inc(s["sq_act"], 1)
                    if tile and u in EVAC_STEPS:
                        sample_evac(*tile, EVAC_STEPS.index(u))

            def mixer(k, back):
                for half in range(2):
                    g0 = k * SPI + half * SPH
                    hn = k * 2 + half
                    stage_sources(0, 0)
                    relu_step(g0, 0)

                    def body(j, v, first, last):
                        if not last:
                            act.wait_ge(s["mixed"], 2 * (hn + 1) + g0 + j * SPB)
                            stage_sources(1 - v, (j + 1) * JB)
                        mixer_body(g0 + j * SPB, hn * BPH + j, hn, (k - 1, j + half * BPH) if back else None, first, last)

                    for j in range(2):
                        body(j, j, j == 0, False)
                    with act.Fori(1, BPH // 2) as bb:
                        for v in range(2):
                            body(bb * 2 + v, v, False, False)
                    body(BPH - 1, (BPH - 1) % 2, False, True)
                    act.wait_ge(s["mixed"], 2 * (hn + 1) + g0 + SPH)
                    for blk in range(4):
                        r = (blk % 2) * C
                        ins = A.activation(z_cm[:, blk * IW:(blk + 1) * IW], (Y0, Y1)[blk // 2][r:r + C, 0:IW], ACT.Copy,
                                           scale=1.0 / XS ** 4)
                    ins.then_inc(s["z_ready"], 1)

            def experts_chunk(k, c, tiles):
                n0 = k * (NCH * E) + c * E
                p0 = k * (NCH * E // 2) + c * (E // 2)

                for e in range(E):
                    act.wait_ge(s["up_done"], n0 + e + 1)
                    A.activation(silu[:, e % 2, :], S[e % 2][:, 0:CW], ACT.Silu, scale=descale[:, MOE1:MOE1 + 1]).then_inc(s["silu_done"], 1)
                    if e % 2 == 0:
                        act.wait_ge(s["share_done"], p0 + e // 2 + 1)
                        A.activation(share[:, e // 2 % 2, :], Y1[:, 0:CW], ACT.Copy, scale=1.0 / XS).then_inc(s["share_ready"], 1)
                    if tiles and e % 8 in EVAC_STEPS:
                        sample_evac(*tiles[e // 8], EVAC_STEPS.index(e % 8))

            def ffn(b):
                for c in range(NCH):
                    for m in range(2):
                        act.wait_ge(s["fup_done"], b * (2 * NCH) + 2 * c + m + 1)
                        A.activation(hid[:, (2 * c + m) % 4, :], S[(2 * c + m) % 4][:, 0:CW], ACT.Gelu_apprx_tanh,
                                     bias=fb1c[:, m:m + 1], scale=descale[:, FFN1:FFN1 + 1]).then_inc(s["gelu_done"], 1)

            def evac_tr(n, dsts):
                for i, dst in enumerate(dsts):
                    act.wait_ge(s["tr_done"], n + i + 1)
                    A.activation(dst, S[i % 4][:, 0:CW] if len(dst.shape) == 2 else
                                 S[i % 4][:, 0:CW].rearrange("p (y x) -> p y x", x=W), ACT.Copy).then_inc(s["tr_cm"], 1)

            def image(k, back):
                r0 = 5 * k - (1 if back else 0)
                n0 = 4 * k - (1 if back else 0)
                tr0 = k * (6 * NCH) - (NCH if back else 0)
                sqrt_round(r0)
                sqrt_round(r0 + 1)
                cast_h(n0, True)
                with act.Fori(0, NCH) as c:
                    for i, dst in enumerate((xn_hl, xn_hh, xn_ll)):
                        act.wait_ge(s["tr_done"], tr0 + c * 3 + i + 1)
                        A.activation(dst[:, bass.ds(c * CW, CW)], S[i][:, 0:CW], ACT.Copy).then_inc(s["tr_cm"], 1)
                mixer(k, back)
                sqrt_round(r0 + 2)
                cast_h(n0 + 1, False)
                evac_tr(tr0 + 3 * NCH, [xn_hl[:, c * CW:(c + 1) * CW] for c in range(NCH)])
                act.wait_ge(s["sm_shift"], k + 1)
                A.activation(small[:, 0, 0:T * E], small[:, 0, 0:T * E], ACT.Exp).then_inc(s["sm_exp"], 1)
                for c in range(NCH):
                    act.wait_ge(s["disp_tr"], k * NCH + c + 1)
                    A.activation(dT[0:2 * E, c * CW:(c + 1) * CW], S[c % 4][0:2 * E, 0:CW], ACT.Copy).then_inc(s["disp_cm"], 1)
                with act.Fori(0, NCH) as c:
                    experts_chunk(k, c, [(k - 1, c * 2 + 14 + q) for q in range(2)] if back else None)
                if back:
                    sqrt_round(r0 + 3)
                    cast_h(n0 + 2, False)
                    evac_tr(tr0 + 4 * NCH, [xn_hl[:, c * CW:(c + 1) * CW] for c in range(NCH)])
                    ffn(k - 1)
                bk = 1 if back else 0
                sqrt_round(r0 + 3 + bk)
                cast_h(n0 + 2 + bk, False)
                evac_tr(tr0 + (4 + bk) * NCH, [pad_v[:, 1 + 8 * c:9 + 8 * c, 1:1 + W] for c in range(NCH)])
                for g in range(2):
                    act.wait_ge(s["om_done"], k * 2 + g + 1)
                    rows = 128 if g == 0 else OC * (NCH - 4)
                    A.activation(om_c[g][0:rows, :], S[g][0:rows, 0:CW], ACT.Copy).then_inc(s["om_ready"], 1)
                act.wait_ge(s["mask_in"], k + 1)
                A.activation(mask[:, :, :], om[:, :, 18:27], ACT.Sigmoid).then_inc(s["mask_out"], 1)

            act.wait_ge(s["w_loaded"], 16 * 15)
            act.wait_ge(s["const_done"], 1)
            image(0, False)
            with act.Fori(1, B) as k:
                image(k, True)
            with act.Fori(0, T) as t:
                for n in range(4):
                    sample_evac(B - 1, t, n)
            sqrt_round(5 * B - 1)
            cast_h(4 * B - 1, False)
            evac_tr(B * 6 * NCH - NCH, [xn_hl[:, c * CW:(c + 1) * CW] for c in range(NCH)])
            ffn(B - 1)
            for k in range(B):
                q = k % 2
                act.wait_ge(s["fin_ready"], k + 1)
                act.dma_start(tm_dram(out.rearrange("b h w c -> b (h w) c"), k), (x1, xin)[q][:, :, :]).then_inc(s[f"out_stored{q}"], 16)
            for q in range(2):
                act.wait_ge(s[f"out_stored{q}"], 16 * ((B + 1 - q) // 2))

        @block.tensor
        def _(pe):
            START = "start"

            def mm(o, a, b, start=True, stop=True):
                return P.matmul(o, a, b, start=start, stop=stop, skip_group_check=True)

            def transpose_tile(o, t, kind):
                c0 = {"hl": C, "hh": 0, "ll": 2 * C}[kind]
                return mm(o, split[:, :, :].rearrange("p t c -> p (t c)")[:, bass.ds(t * (4 * C) + c0, 2 * C)], ident16[:, :])

            def transpose_all(n):
                for c in range(NCH):
                    if c >= 4:
                        pe.wait_ge(s["tr_cm"], n + c - 3)
                    for i in range(CT):
                        ins = transpose_tile(S[c % 4][:, i * TP:(i + 1) * TP], c * CT + i, "hl")
                    ins.then_inc(s["tr_done"], 1)

            def sample(b, t, q, stage):
                n = b * T + t
                if stage < 3:
                    if stage == 0:
                        pe.wait_ge(s["weighted"], n + 1)
                    else:
                        pe.wait_ge(s["val_ready"], n * 3 + stage)
                    for i in range(3):
                        tap = 3 * stage + i
                        for pair in range(2):
                            c0 = (tap * 4 + pair * 2) * C
                            ins = P.matmul(D0[:, i * TP:(i + 1) * TP], G[0:TP, q, c0:c0 + 2 * C], ident[0:TP, 0:TP],
                                           start=i == 0 and pair == 0, stop=pair == 1, is_transpose=True, skip_group_check=True)
                    ins.then_inc(s["val_tr"], 1)
                if stage == 3:
                    pe.wait_ge(s["val_ready"], n * 3 + 3)
                    for tap in range(TAPS):
                        h = tap % 2
                        ins = mm(D0[h * C:(h + 1) * C, 0:TP], dcn[:, tap, :], val_cm[:, tap * TP:(tap + 1) * TP], tap < 2, tap > 6)
                    ins.then_inc(s["conv_done"], 1)
                if stage == 4:
                    pe.wait_ge(s["conv_ready"], n + 1)
                    mm(D0[0:TP, 448:448 + C], dcn_cm[:, :], ident2[:, :]).then_inc(s["dcn_done"], 1)

            def sims(j, i0, u):
                for b in range(2):
                    i = i0 + (u % 2 * 2 + b) * IW
                    o = PS[u % 2][0:TP, b, 0:IW]
                    mm(o, xn_hh[:, bass.ds(j * TP, TP)], xn_hl[:, i:i + IW], True, False)
                    ins = mm(o, xn_ll[:, bass.ds(j * TP, TP)], xn_hl[:, i:i + IW], False, True)
                ins.then_inc(s["sim_done"], 1)

            def mixer_body(i0, j0, par, g, na, nd, xn, last, tile):
                a = d = 0
                pe.wait_ge(s["xj_ready"], xn + 1)
                for u in range(SPB):
                    if not (last and u >= SPB - 2):
                        pe.wait_ge(s["relu_done"], g + u + 1)
                        sims(j0 + (u + 2) // 2, i0, u)
                    if tile and u in SAMPLE_STEPS:
                        sample(*tile, SAMPLE_STEPS.index(u))
                    if u in ACT_STEPS:
                        a += 1
                        pe.wait_ge(s["sq_act"], na + a)
                    else:
                        d += 1
                        pe.wait_ge(s["sq_dve"], nd + d)
                    for b in range(2):
                        ins = mm((Y0, Y1)[u % 2][b * C:(b + 1) * C, 0:IW], xj[:, par, u // 2, :], sq[:, u % 2, b], False, False)
                    ins.then_inc(s["mixed"], 1)

            def mixer(k, back):
                for half in range(2):
                    i0 = half * 4 * IW
                    hn = k * 2 + half
                    g0 = k * SPI + half * SPH
                    if half:
                        pe.wait_ge(s["x1_added"], k * 4 + 2)
                    sims(0, i0, 0)
                    sims(0, i0, 1)
                    if half:
                        pe.wait_ge(s["z_ready"], k * 2 + half)
                    for y in (Y0, Y1):
                        mm(y[:, 0:IW], zero16[:, 0:128], zero16[:, 0:IW], True, False).then_inc(s["mixed"], 1)

                    def body(j, v, last):
                        n = hn * BPH + j
                        t = j + half * BPH
                        mixer_body(i0, j * JB, v % 2, g0 + j * SPB, n * ACT_N, n * DVE_N, n, last,
                                   (k - 1, t, (v + half * BPH) % 2) if back else None)

                    with pe.Fori(0, BPH // 2) as bb:
                        for v in range(2):
                            body(bb * 2 + v, v, False)
                    body(BPH - 1, BPH - 1, True)
                    pe.wait_ge(s["z_ready"], k * 2 + half + 1)
                    for m in range(2):
                        for t in range(7):
                            c0 = (m * 7 + t) * TP
                            ins = mm(S[m][0:TP, t * C:(t + 1) * C], z_cm[:, c0:c0 + TP], w_mix[:, :])
                        ins.then_inc(s["y_done"], 1)

            def experts_chunk(k, c, tiles, last):
                n0 = k * (NCH * E) + c * E
                p0 = k * (NCH * E // 2) + c * (E // 2)

                def up(e, c):
                    cols = bass.ds(c * CW, CW)
                    for h, l, o in ((w1h, w1l, S[e % 2]), (w2h, w2l, S[2 + e % 2])):
                        mm(o[:, 0:CW], h[:, e * HID:(e + 1) * HID], xn_hl[:, cols], True, False)
                        ins = mm(o[:, 0:CW], l[:, e * HID:(e + 1) * HID], xn_hl[:, cols], False, True)
                    ins.then_inc(s["up_done"], 1)

                def spread(p, c):
                    mm(Y1[:, 0:CW], pick[:, p * 128:(p + 1) * 128], dT[:, bass.ds(c * CW, CW)]).then_inc(s["share_done"], 1)

                def collect(p):
                    for t in range(CT):
                        ins = P.matmul(D1[0:TP, t * 128:(t + 1) * 128], scaled_y[:, p % 2, t * TP:(t + 1) * TP], ident[:, :],
                                       start=p == 0 and t == 0, stop=p == E // 2 - 1, is_transpose=True, skip_group_check=True)
                    return ins

                if tiles is START:
                    spread(0, c)
                    up(0, c)
                    up(1, c)
                    return
                for e in range(E):
                    pe.wait_ge(s["hid_done"], n0 + e + 1)
                    if e + 2 < E:
                        up(e + 2, c)
                    if tiles and e % 8 in SAMPLE_STEPS:
                        sample(*tiles[e // 8], SAMPLE_STEPS.index(e % 8))
                    if e % 2:
                        p = e // 2
                        if p:
                            pe.wait_ge(s["scaled_done"], p0 + p)
                        for b in range(2):
                            f = e - 1 + b
                            ins = mm(Y0[b * C:(b + 1) * C, 0:CW], w3s[:, f, :], hid[:, f % 4, :], True, True)
                        ins.then_inc(s["down_done"], 1)
                        pe.wait_ge(s["share_ready"], p0 + p + 1)
                        if p + 1 < E // 2:
                            spread(p + 1, c)
                        if p:
                            if p == 1:
                                if isinstance(k, int) and isinstance(c, int) and k * NCH + c == 0:
                                    pass
                                elif isinstance(k, int) and k == 0:
                                    pe.wait_ge(s["x2_added"], c)
                                else:
                                    pe.wait_ge(s["x2_added"], k * NCH + c)
                            collect(p - 1)
                if not last:
                    spread(0, c + 1)
                    up(0, c + 1)
                pe.wait_ge(s["scaled_done"], p0 + E // 2)
                collect(E // 2 - 1).then_inc(s["ytm_done"], 1)
                if not last:
                    up(1, c + 1)

            def ffn(b):
                for t in range(T):
                    for w in (wrh, wrl):
                        ins = mm(D0[0:TP, t:t + 1], xn_hl[:, t * TP:(t + 1) * TP], w[:, 0:1], w is wrh, w is wrl)
                ins.then_inc(s["route_done"], 1)

                def up(c):
                    for m in range(2):
                        o = S[(2 * c + m) % 4][:, 0:CW]
                        mm(o, f1h[:, m * 128:(m + 1) * 128], xn_hl[:, c * CW:(c + 1) * CW], True, False)
                        mm(o, f1l[:, m * 128:(m + 1) * 128], xn_hl[:, c * CW:(c + 1) * CW], False, True).then_inc(s["fup_done"], 1)

                up(0)
                for c in range(NCH):
                    if c >= 1 and c + 1 < NCH:
                        pe.wait_ge(s["gelu_done"], b * (2 * NCH) + 2 * c)
                    if c + 1 < NCH:
                        up(c + 1)
                    if c >= 2:
                        pe.wait_ge(s["yw_done"], b * NCH + c - 1)
                    pe.wait_ge(s["gelu_done"], b * (2 * NCH) + 2 * c + 2)
                    for t in range(CT):
                        for m in range(2):
                            ins = mm((Y0, Y1)[c % 2][0:TP, t * C:(t + 1) * C], hid[:, (2 * c + m) % 4, t * TP:(t + 1) * TP],
                                     f2s[:, m, :], m == 0, m == 1)
                    ins.then_inc(s["fdown_done"], 1)

            def image(k, back):
                n0 = 4 * k - (1 if back else 0)
                tr0 = k * (6 * NCH) - (NCH if back else 0)
                def stacks(c, first=False):
                    pe.wait_ge(s["split_done"], n0 + 1)
                    for i, kind in enumerate(("hl", "hh", "ll")):
                        if not first:
                            pe.wait_ge(s["tr_cm"], tr0 + c * 3 + (i - 2))
                        for n in range(CT):
                            ins = transpose_tile(S[i][:, n * TP:(n + 1) * TP], c * CT + n, kind)
                        ins.then_inc(s["tr_done"], 1)

                stacks(0, True)
                with pe.Fori(1, NCH) as c:
                    stacks(c)
                pe.wait_ge(s["tr_cm"], tr0 + 3 * NCH)
                mixer(k, back)
                pe.wait_ge(s["split_done"], n0 + 2)
                transpose_all(tr0 + 3 * NCH)
                pe.wait_ge(s["tr_cm"], tr0 + 4 * NCH)
                for t in range(T):
                    for w in (gateh, gatel):
                        ins = mm(D0[0:TP, t * E:(t + 1) * E], xn_hl[:, t * TP:(t + 1) * TP], w[:, :], w is gateh, w is gatel)
                ins.then_inc(s["logits_done"], 1)
                pe.wait_ge(s["disp_split"], k + 1)
                for c in range(NCH):
                    if c >= 4:
                        pe.wait_ge(s["disp_cm"], k * NCH + c - 3)
                    for i in range(CT):
                        ins = mm(S[c % 4][0:2 * E, i * TP:(i + 1) * TP], dsplit[:, c * CT + i, :], ident16[:, :])
                    ins.then_inc(s["disp_tr"], 1)
                pe.wait_ge(s["disp_cm"], (k + 1) * NCH)
                experts_chunk(k, 0, START, False)

                def chunk(c, last):
                    experts_chunk(k, c, [(k - 1, c * 2 + 14 + q, q) for q in range(2)] if back else None, last)

                if back:
                    with pe.Fori(0, NCH - 1) as c:
                        chunk(c, False)
                else:
                    chunk(0, False)
                    with pe.Fori(1, NCH - 1) as c:
                        chunk(c, False)
                chunk(NCH - 1, True)
                if back:
                    pe.wait_ge(s["split_done"], n0 + 3)
                    transpose_all(tr0 + 4 * NCH)
                    pe.wait_ge(s["tr_cm"], tr0 + 5 * NCH)
                    ffn(k - 1)
                bk = 1 if back else 0
                pe.wait_ge(s["split_done"], n0 + 3 + bk)
                transpose_all(tr0 + (4 + bk) * NCH)
                pe.wait_ge(s["tr_cm"], tr0 + (5 + bk) * NCH)
                for g in range(2):
                    nt = 4 if g == 0 else NCH - 4
                    for tap in range(TAPS):
                        for w in (offh, offl):
                            for i in range(nt):
                                y = 8 * (4 * g + i) + tap // 3
                                ins = mm(S[g][i * OC:(i + 1) * OC, 0:CW].rearrange("p (y x) -> p y x", x=W), w[:, tap * OC:(tap + 1) * OC],
                                         pad_v[:, y:y + 8, tap % 3:tap % 3 + W], tap == 0 and w is offh, tap == TAPS - 1 and w is offl)
                    ins.then_inc(s["om_done"], 1)
                for g in range(2):
                    rows = 128 if g == 0 else OC * (NCH - 4)
                    pe.wait_ge(s["om_ready"], k * 2 + g + 1)
                    for i in range(CT):
                        ins = P.transpose(S[2 + g][0:TP, i * 128:i * 128 + rows], om_c[g][0:rows, i * TP:(i + 1) * TP], ident[0:rows, 0:rows])
                    ins.then_inc(s["om_tr"], 1)
                pe.wait_ge(s["geo_done"], k + 1)

            pe.wait_ge(s["w_loaded"], 16 * 15)
            pe.wait_ge(s["const_done"], 1)
            image(0, False)
            with pe.Fori(1, B) as k:
                image(k, True)
            with pe.Fori(0, T // 2) as u:
                for q in range(2):
                    for n in range(5):
                        sample(B - 1, u * 2 + q, q, n)
            pe.wait_ge(s["split_done"], 4 * B)
            transpose_all(B * 6 * NCH - NCH)
            pe.wait_ge(s["tr_cm"], B * 6 * NCH)
            ffn(B - 1)
            def count_tokens():
                return mm(D0[0:TP, 0:B], ones16[:, :], cnt16[:, :]).then_inc(s["count_done"], 1)

            pe.wait_ge(s["count_in"], 1)
            count_tokens()
            with pe.Fori(0, 32) as i:
                pe.wait_ge(s["count_in"], i + 2)
                count_tokens()
            pe.wait_ge(s["tie_in"], 1)
            mm(D0[0:TP, 0:B * T], tri16[:, :], eq16[:, :])
            mm(D1[0:TP, 0:B * T], ones16[:, :], eq16[:, :]).then_inc(s["tie_done"], 1)


def kernel(**inputs):
    import numpy as _np
    import concourse.bacc as _bacc
    from concourse import mybir as _mybir
    from concourse.bass_utils import run_bass_kernel_spmd as _run

    a = {n: _np.ascontiguousarray(v) for n, v in inputs.items()}
    B, H, W, C = a["x"].shape
    T, TP, E = H // 2, 2 * W, a["L0_ffn_w1"].shape[0]
    p, t, tap = _np.arange(TP)[:, None, None], _np.arange(T)[None, :, None], _np.arange(9)[None, None, :]
    grid = _np.zeros((TP, T, 18), _np.float32)
    grid[:, :, 0::2] = 2 * t + p // W + tap // 3
    grid[:, :, 1::2] = p % W + tap % 3
    pick = _np.zeros((2 * E, E, C), _np.float32)
    for e in range(E):
        pick[e, e, :] = pick[E + e, e, :] = 1
    arrays = {
        "x": a["x"], "conv_w": a["L0_conv_W"], "gate_w": a["L0_ffn_gate_w"], "gate_b": a["L0_ffn_gate_b"].reshape(1, -1),
        "w1": a["L0_ffn_w1"], "w2": a["L0_ffn_w2"], "w3": a["L0_ffn_w3"],
        "off_w": a["L1_conv_offset_w"].reshape(9 * C, 27), "off_b": a["L1_conv_offset_b"].reshape(1, 27),
        "dcn_w": _np.ascontiguousarray(a["L1_conv_dcn_weight"].transpose(2, 3, 1, 0)).reshape(9 * C, C),
        "wr": a["L1_ffn_wr"], "br": a["L1_ffn_br"].reshape(1, 1), "f1": a["L1_ffn_w1"], "fb1": a["L1_ffn_b1"].reshape(-1, 1),
        "f2": a["L1_ffn_w2"], "fb2": a["L1_ffn_b2"].reshape(1, -1),
        "ident_in": _np.eye(128, dtype=_np.float32), "grid_in": grid,
        "rank_in": _np.tile(_np.arange(E, 0, -1, dtype=_np.float32), (TP, 1)), "pick_in": pick.reshape(2 * E, E * C),
        "tri_in": _np.triu(_np.ones((TP, TP), _np.float32), 1),
        "bits_in": _np.tile((2.0 ** _np.arange(30, -1, -1)).astype(_np.float32), (TP, 1)),
    }
    nc = _bacc.Bacc("TRN2", target_bir_lowering=False, num_devices=1)
    args = {n: nc.dram_tensor(n, v.shape, _mybir.dt.from_np(v.dtype), kind="ExternalInput").ap() for n, v in arrays.items()}
    out = nc.dram_tensor("out", (B, H, W, C), _mybir.dt.float32, kind="ExternalOutput").ap()
    metaformer_kernel(nc, **args, out=out)
    r = _run(nc, [arrays], core_ids=[0])
    return r.results[0]["out"]
```

```python
from contextlib import ExitStack

import numpy as np
import concourse.bass as bass
from concourse import mybir

ACT_STEPS = (0, 3, 6)
FFN_CUT = (3, 5)
MIX = dict(sample=(0, 2, 4, 6), evac=(1, 3, 5), add=7, weigh=(0, 1, 3, 5, 7))
MIX_FIRST = dict(own=(1, 2, 3, 4, 4), sample=(5, 6, 7, 7), evac=(5, 6, 7), add=7, weigh=(5, 6, 7, 7, 7))
MOE_SAMPLE, MOE_EVAC, MOE_ADD, MOE_WEIGH = (0, 2, 4, 6), (2, 4, 6), 7, (1, 3, 4, 5, 7)


def metaformer_kernel(nc, x, conv_w, gate_w, gate_b, w1, w2, w3, off_w, off_b, dcn_w, wr, br, f1, fb1, f2, fb2,
                      ident_in, grid_in, rank_in, pick_in, tri_in, bits_in, out):
    f32, f16, i32, u32 = mybir.dt.float32, mybir.dt.float16, mybir.dt.int32, mybir.dt.uint32
    ALU, ACT, AX = mybir.AluOpType, mybir.ActivationFunctionType, mybir.AxisListType

    B, H, W, C = x.shape
    N = H * W
    TP = 2 * W
    T = N // TP
    E, HID = w1.shape[0], w1.shape[2]
    FH = f1.shape[1]
    TAPS = 9
    CT = 4
    CW = CT * TP
    NCH = T // CT
    IW = 392
    JB = 4
    SPB = 2 * JB
    BPH = T // JB
    SPH = SPB * BPH
    SPI = 2 * SPH
    OC = 32
    SIDE = W + 2
    XS = 256.0
    KTOP = int(0.5 * N) - 1
    ROUNDS = bits_in.shape[1] // 6
    LNC_EPS, LNT_EPS = 1e-6, 1e-5
    MOE1, MOE2, GATE, OFF, FFN1, ROUTE = range(6)
    NW = 6
    ACT_N = len(ACT_STEPS)
    DVE_STEPS = tuple(u for u in range(SPB) if u not in ACT_STEPS)
    DVE_N = len(DVE_STEPS)

    table = nc.dram_tensor("corner_table", [SIDE * SIDE, 4 * C], f32).ap()
    x3_dram = nc.dram_tensor("x3_scratch", [B - 1, N, C], f32).ap()
    yw_dram = nc.dram_tensor("yw_scratch", [B, N, C], f32).ap()

    ctx = ExitStack()
    with ctx:
        def sb(name, shape, dt=f32):
            return ctx.enter_context(nc.sbuf_tensor(name, shape, dt))

        ident = sb("ident", [128, 128])
        ident2 = sb("ident2", [128, C])
        ident16 = sb("ident16", [TP, TP], f16)
        ones16 = sb("ones16", [TP, TP], f16)
        tri16 = sb("tri16", [TP, TP], f16)
        pick = sb("pick", [128, E * C], f16)
        zero16 = sb("zero16", [128, IW], f16)
        grid = sb("grid", [TP, T, 2 * TAPS])
        rank = sb("rank", [TP, E])
        bits = sb("bits", [TP, ROUNDS, 3], i32)
        incs = sb("incs", [TP, ROUNDS, 3])
        w_mix = sb("w_mix", [C, C])
        w1h = sb("w1h", [128, E * HID], f16)
        w1l = sb("w1l", [128, E * HID], f16)
        w2h = sb("w2h", [128, E * HID], f16)
        w2l = sb("w2l", [128, E * HID], f16)
        w3s = sb("w3s", [HID, E, C])
        gateh = sb("gateh", [128, E], f16)
        gatel = sb("gatel", [128, E], f16)
        gbias = sb("gbias", [TP, E])
        offh = sb("offh", [128, TAPS * OC], f16)
        offl = sb("offl", [128, TAPS * OC], f16)
        obias = sb("obias", [128, 1])
        dcn = sb("dcn", [128, (TAPS + 1) // 2, C])
        wrh = sb("wrh", [128, 2], f16)
        wrl = sb("wrl", [128, 2], f16)
        brc = sb("brc", [TP, 1])
        f1h = sb("f1h", [128, FH], f16)
        f1l = sb("f1l", [128, FH], f16)
        fb1c = sb("fb1c", [128, 2])
        f2s = sb("f2s", [128, 2, C])
        fb2r = sb("fb2r", [TP, C])
        amax = sb("amax", [128, NW])
        amin = sb("amin", [128, NW])
        amax_all = sb("amax_all", [128, NW])
        wscale = sb("wscale", [128, NW])
        descale = sb("descale", [128, NW])

        xin = sb("xin", [TP, T, C])
        xln = sb("xln", [TP, T, C])
        xm = sb("xm", [TP, T, C])
        tmp = sb("tmp", [TP, T, C])
        x1 = sb("x1", [TP, T, C])
        xB = sb("xB", [TP, T, C])
        yw = sb("yw", [TP, T, C])
        st = sb("st", [TP, 3, 8, T])
        split = sb("split", [TP, T, 4 * C], f16)
        split_f = split[:, :, 2 * C:4 * C].bitcast(f32)
        fin_x = (x1[:, :, :], xin[:, :, :])
        fin_y = (split[:, :, 0:2 * C].bitcast(f32), xln[:, :, :])
        xn_hl = sb("xn_hl", [128, N], f16)
        xn_hh = sb("xn_hh", [128, N], f16)
        xn_ll = sb("xn_ll", [128, N], f16)
        xf = sb("xf", [128, N], f16)
        dT = xn_hh
        padded = sb("padded", [128, SIDE * SIDE], f16)
        pad_v = padded[:, :].rearrange("p (y x) -> p y x", x=SIDE)
        work = sb("work", [128, 8 * IW])
        relu = work[0:TP, 0:4 * IW].rearrange("p (q b n) -> p q b n", q=2, b=2)
        sq = work[0:TP, 4 * IW:8 * IW].rearrange("p (q b n) -> p q b n", q=2, b=2)
        silu = work[:, 0:2 * CW].rearrange("p (q n) -> p q n", q=2)
        hid = work[:, 2 * CW:6 * CW].rearrange("p (q n) -> p q n", q=4)
        xj = sb("xj", [TP, 2, JB, C])
        small_all = sb("small", [128, 5, 2 * TAPS * T])
        small = small_all[0:TP, :, :]
        small_flat = small_all[:, :, :].rearrange("p a b -> p (a b)")
        z_cm = small_all[0:C, 0:4, :].rearrange("p a b -> p (a b)")[:, 0:4 * IW]
        smallc = sb("smallc", [TP, 8, T])
        disp = sb("disp", [TP, T, E])
        dsplit = sb("dsplit", [TP, T, 2 * E], f16)
        om = sb("om", [TP, T, OC])
        mask = sb("mask", [TP, T, TAPS])
        om_cm = sb("om_cm", [128, CW])
        om_c = (om_cm, silu[:, 0, :])
        corner_w = sb("corner_w", [TP, T * TAPS, 4])
        index = sb("index", [TP, T * TAPS], u32)
        pool_cell = sb("pool_cell", [TP, 5])
        table_cell = sb("table_cell", [1, 4])
        index_now = sb("index_now", [TP, 2, TAPS], u32)
        G = sb("G", [128, 2, 4 * TAPS * C])
        stage, stage2 = G[:, 0, :], G[:, 1, :]
        stage3 = work
        value = sb("value", [TP, 2, TAPS * C])
        val_cm = sb("val_cm", [128, 5 * TP])
        dcn_cm = sb("dcn_cm", [128, TP])
        share = small_flat[:, 0:2 * CW].rearrange("p (q n) -> p q n", q=2)
        scaled_y = small_flat[:, 2 * CW:4 * CW].rearrange("p (q n) -> p q n", q=2)
        w_all = sb("w_all", [TP, B + 1, T])
        w_img = w_all[:, 1:B + 1, :]
        hit = small_flat[0:TP, 0:3 * (B - 1) * T]
        key, eqf, tot, run, pre = (small_flat[0:TP, (3 + i) * (B - 1) * T:(4 + i) * (B - 1) * T] for i in range(5))
        sel = sb("sel", [TP, B, T])
        eq16 = sb("eq16", [TP, B * T], f16)
        cand = sb("cand", [TP, 3 * B], i32)
        got3 = sb("got3", [TP, 3 * B])
        kf = sb("kf", [TP, 8, B])
        ki = sb("ki", [TP, 3, B], i32)
        cnt16 = sb("cnt16", [TP, 3 * B], f16)

        PS = [ctx.enter_context(nc.psum_tensor(f"PS{i}", [128, 2, 512], f32)) for i in range(4)]
        S = [PS[0][:, 0, :], PS[0][:, 1, :], PS[1][:, 0, :], PS[1][:, 1, :]]
        Y0, Y1, D0, D1 = PS[2][:, 0, :], PS[2][:, 1, :], PS[3][:, 0, :], PS[3][:, 1, :]

        s = {n: ctx.enter_context(nc.semaphore(n)) for n in """
            w_loaded w_staged  amax_done amax_red stage_zero table_zeroed const_done
            x_loaded x1_added centered squared var_done std_done scaled h_cast split_done tr_done tr_cm
            sim_done relu_done sq_act sq_dve mixed xj_ready z_ready y_done
            logits_done sm_shift sm_exp disp_split disp_tr disp_cm
            up_done silu_done hid_done share_done share_ready down_done scaled_done ytm_done x2_added
            geo_ln om_done om_ready om_tr om_taken mask_out geo_done 
            table_written gath0 gath1 cell_done pool_step valued val_tr val_ready conv_done conv_ready dcn_done
            fup_done gelu_done fdown_done fout_read yw_done skip_added x3_stored yw_stored
            count_in count_done tie_in tie_done x3_back0 x3_back1 yw_back0 yw_back1 bias_zero ident_loaded fin_ready out_stored0
            out_stored1""".split()}
        gath = (s["gath0"], s["gath1"])
        V, A, P, GP = nc.vector, nc.scalar, nc.tensor, nc.gpsimd
        block = ctx.enter_context(nc.Block())

        def bc(ap, axis, n):
            v = ap.unsqueeze(axis)
            shape = list(v.shape)
            shape[axis] = n
            return v.to_broadcast(shape)

        def tm_dram(t, k):
            return t[bass.ds(k, 1), :, :].rearrange("a (t p) c -> p (a t) c", p=TP)

        def rounds_before(k, back):
            return 5 * k + (1 if back else 2)

        def splits_before(k, back):
            return 4 * k + (0 if back else 1)

        def chunks_before(k, back):
            return 6 * NCH * k + (2 if back else 3) * NCH

        @block.sync
        def _(sp):
            x_flat = x.rearrange("b h w c -> b (h w) c")

            def load_x(k):
                sp.dma_start(xin[:, :, :], tm_dram(x_flat, k)).then_inc(s["x_loaded"], 16)

            def write_table(k):
                sp.wait_ge(s["geo_ln"], k + 1)
                for slot, (dy, dx) in enumerate(((1, 1), (1, 0), (0, 1), (0, 0))):
                    tv = table.rearrange("(y x) (s c) -> x y s c", x=SIDE, c=C)
                    for r in range(2):
                        dst = tv[dx:dx + W, dy + r:dy + r + H, slot, :].rearrange("x (t two) c -> x t two c", two=2)[:, :, 0, :]
                        sp.dma_start(dst, xln[r * W:(r + 1) * W, :, :]).then_inc(s["table_written"], 16)

            def store_x3(b):
                sp.wait_ge(s["skip_added"], b + 1)
                sp.dma_start(tm_dram(x3_dram, b), xB[:, :, :]).then_inc(s["x3_stored"], 16)

            def store_yw(f):
                sp.wait_ge(s["yw_done"], f + 1)
                sp.dma_start(tm_dram(yw_dram, f), yw[:, :, :]).then_inc(s["yw_stored"], 16)

            load_x(0)
            sp.dma_start(ident[:, :], ident_in).then_inc(s["ident_loaded"], 16)
            sp.wait_ge(s["bias_zero"], 1)
            loads = [(ident2[0:C, :], ident_in[0:C, 0:C]), (ident2[C:128, :], ident_in[0:C, 0:C]),
                     (grid[:, :, :], grid_in), (rank[:, :], rank_in), (w_mix[:, :], conv_w),
                     (w3s[:, :, :], w3.rearrange("e h c -> h e c")),
                     (gbias[:, :], gate_b.to_broadcast([TP, E])), *[(obias[i * OC:i * OC + 27, :], off_b) for i in range(4)],
                     (dcn[:, 0:TAPS // 2, :], dcn_w[0:(TAPS - 1) * C, :].rearrange("(n k) c -> k n c", k=128)),
                     (dcn[C:128, TAPS // 2, :], dcn_w[(TAPS - 1) * C:TAPS * C, :]),
                     (brc[:, :], br.to_broadcast([TP, 1])), (fb1c[:, :], fb1.rearrange("(m p) o -> p (m o)", p=128)),
                     (f2s[:, :, :], f2.rearrange("(m k) c -> k m c", m=2)),
                     (fb2r[:, :], fb2.to_broadcast([TP, C]))]
            with nc.allow_non_contiguous_dma(reason="small constants"):
                for dst, src in loads:
                    sp.dma_start(dst, src).then_inc(s["w_loaded"], 16)
            for w, dst in ((w1, stage), (w2, stage2)):
                for h in range(2):
                    sp.dma_start(dst[h * C:(h + 1) * C, 0:E * HID].rearrange("c (e h) -> c e h", e=E),
                                 w.rearrange("e c h -> c e h")).then_inc(s["w_staged"], 16)
            with nc.allow_non_contiguous_dma(reason="small weights"):
                for h in range(2):
                    r = slice(h * C, (h + 1) * C)
                    for dst, src in ((stage3[r, 0:E], gate_w), (stage3[r, 768:769], wr), (stage3[r, 1024:1024 + FH], f1),
                                     (stage3[r, 64:64 + TAPS * OC].rearrange("c (t o) -> c t o", o=OC)[:, :, 0:27],
                                      off_w.rearrange("(t c) o -> c t o", c=C))):
                        sp.dma_start(dst, src).then_inc(s["w_staged"], 16)
            sp.dma_start(stage3[0:TP, 1280:1280 + TP], tri_in).then_inc(s["w_staged"], 16)
            sp.dma_start(stage3[0:TP, 1408:1408 + 6 * ROUNDS], bits_in).then_inc(s["w_staged"], 16)
            sp.dma_start(stage3[0:2 * E, 1536:1536 + E * C], pick_in).then_inc(s["w_staged"], 16)
            sp.wait_ge(s["stage_zero"], 1)
            tz = table.rearrange("e n -> (e n)").rearrange("(p n) -> p n", p=128)
            pieces = range(0, tz.shape[1], 1682)
            for a in pieces:
                sp.dma_start(tz[:, a:a + 1682], stage[:, 0:1682]).then_inc(s["table_zeroed"], 16)
            sp.wait_ge(s["table_zeroed"], 16 * len(pieces))

            def image(k, has_back, has_next):
                if has_next:
                    sp.wait_ge(s["x1_added"], 4 * (k + 1))
                    load_x(k + 1)
                write_table(k)
                if has_back:
                    store_x3(k - 1)
                    store_yw(k - 1)

            image(0, False, True)
            with sp.Fori(1, B - 1) as k:
                image(k, True, True)
            image(B - 1, True, False)
            store_yw(B - 1)
            sp.wait_ge(s["geo_done"], B)
            sp.wait_ge(s["table_written"], B * 128)
            sp.wait_ge(s["x3_stored"], 16 * (B - 1))
            sp.wait_ge(s["yw_stored"], 16 * B)
            o = out.rearrange("b h w c -> b (h w) c")

            def load_back(k):
                q = k % 2
                if k >= 2:
                    sp.wait_ge(s[f"out_stored{q}"], 16 * (k // 2))
                sp.dma_start(fin_x[q], tm_dram(x3_dram, k)).then_inc(s[f"x3_back{q}"], 16)
                sp.dma_start(fin_y[q], tm_dram(yw_dram, k + 1)).then_inc(s[f"yw_back{q}"], 16)

            load_back(0)
            for k in range(B - 1):
                if k + 1 < B - 1:
                    load_back(k + 1)
                sp.wait_ge(s["fin_ready"], k + 1)
                sp.dma_start(tm_dram(o, k), fin_x[k % 2]).then_inc(s[f"out_stored{k % 2}"], 16)
            sp.wait_ge(s["fin_ready"], B)
            sp.dma_start(tm_dram(o, B - 1), xB[:, :, :]).then_inc(s[f"out_stored{(B - 1) % 2}"], 16)
            for q in range(2):
                sp.wait_ge(s[f"out_stored{q}"], 16 * ((B + 1 - q) // 2))

        @block.gpsimd
        def _(pool):
            pool.wait_ge(s["amax_done"], 1)
            GP.partition_all_reduce(amax_all[:, :], amax[:, :], 128, bass.bass_isa.ReduceOp.max).then_inc(s["amax_red"], 1)

            def step(cell):
                GP.tensor_tensor(pool_cell[:, cell:cell + 1], pool_cell[:, 0:1], pool_cell[:, 0:1], ALU.add).then_inc(s["pool_step"], 1)

            def gather_tile(b, u, q, first=False):
                n = (b * T + u * 2 + q) * 3
                if not first:
                    pool.wait_ge(s["valued"], b * T + u * 2 + (q - 1))
                step(1 + q)
                GP.tensor_copy(index_now[:, q, :], index[:, bass.ds((u * 2 + q) * TAPS, TAPS)]).then_inc(s["pool_step"], 1)
                pool.wait_ge(s["pool_step"], n + 2)
                step(3 + q)
                for tap in range(TAPS):
                    GP.indirect_dma_start(G[0:TP, q, tap * 4 * C:(tap + 1) * 4 * C], None, table,
                                          bass.IndirectOffsetOnAxis(ap=index_now[:, q, tap:tap + 1], axis=0)).then_inc(gath[q], 16)

            GP.memset(pool_cell[:, :], 0.0).then_inc(s["cell_done"], 1)
            pool.wait_ge(s["cell_done"], 1)
            with pool.Fori(0, B) as b:
                pool.wait_ge(s["geo_done"], b + 1)
                pool.wait_ge(s["table_written"], (b + 1) * 128)
                for q in range(2):
                    gather_tile(b, 0, q, first=True)
                with pool.Fori(1, T // 2) as u:
                    for q in range(2):
                        gather_tile(b, u, q)

        @block.vector
        def _(dve):
            red = lambda o, i, op=ALU.add: V.tensor_reduce(o, i, AX.X, op)

            def scales(a, b):
                V.tensor_scalar(amax_all[:, a:b], amax_all[:, a:b], 1e-30, None, ALU.max)
                dve.drain()
                V.tensor_scalar(descale[:, a:b].bitcast(i32), amax_all[:, a:b].bitcast(i32), 0x7F800000, None, ALU.bitwise_and)
                dve.drain()
                V.tensor_scalar(wscale[:, a:b].bitcast(i32), descale[:, a:b].bitcast(i32), -1.0, float(262 << 23), ALU.mult, ALU.add)
                dve.drain()
                V.tensor_scalar(descale[:, a:b], descale[:, a:b], 1.0 / (256.0 * XS), None, ALU.mult)
                dve.drain()

            def magnitudes(tensors):
                for col, src in tensors:
                    red(amax[:, col:col + 1], src, ALU.max)
                    red(amin[:, col:col + 1], src, ALU.min)
                dve.drain()
                for col, _src in tensors:
                    V.scalar_tensor_tensor(amax[:, col:col + 1], amin[:, col:col + 1], -1.0, amax[:, col:col + 1], ALU.mult, ALU.max)

            def weigh(b, t, q, u, piece):
                g = G[0:TP, q, :].rearrange("p (n s c) -> p n s c", n=TAPS, s=4)
                if piece < 3:
                    if piece == 0:
                        dve.wait_ge(gath[q], b * (TAPS * 16 * T // 2) + (u + 1) * (TAPS * 16))
                    n = 4 * TAPS // 3
                    g = G[0:TP, q, :].rearrange("p (n c) -> p n c", c=C)[:, piece * n:(piece + 1) * n, :]
                    w = corner_w[:, :, :].rearrange("p n s -> p (n s)")[:, bass.ds(t * (4 * TAPS) + piece * n, n)]
                    V.tensor_tensor(g, g, bc(w, 2, C), ALU.mult)
                else:
                    dve.drain()
                    if piece == 3:
                        V.tensor_tensor(g[:, :, 0:2, :], g[:, :, 0:2, :], g[:, :, 2:4, :], ALU.add)
                    else:
                        V.tensor_tensor(value[:, q, :].rearrange("p (n c) -> p n c", n=TAPS), g[:, :, 0, :], g[:, :, 1, :],
                                        ALU.add).then_inc(s["valued"], 1)

            def sample_add(b, t):
                dve.wait_ge(s["dcn_done"], b * T + t + 1)
                xt = xB[:, :, :].rearrange("p t c -> p (t c)")[:, bass.ds(t * C, C)]
                V.tensor_tensor(xt, xt, D0[0:TP, 448:448 + C], ALU.add)

            def ln_center(dst, src, q, summed=False):
                if not summed:
                    red(st[:, q, 0, :], src)
                    dve.drain()
                V.tensor_scalar(st[:, q, 1, :], st[:, q, 0, :], 1.0 / C, None, ALU.mult)
                dve.drain()
                V.tensor_tensor(dst[:, :, :], src, bc(st[:, q, 1, :], 2, C), ALU.subtract).then_inc(s["centered"], 1)

            def ln_var(squares, q, eps, n):
                dve.wait_ge(s["squared"], n + 1)
                red(st[:, q, 2, :], squares[:, :, :])
                dve.drain()
                V.tensor_scalar(st[:, q, 3, :], st[:, q, 2, :], 1.0 / C, eps, ALU.mult, ALU.add).then_inc(s["var_done"], 1)

            def ln_scale(centered, q, r):
                dve.wait_ge(s["std_done"], r + 1)
                V.reciprocal(st[:, q, 5, :], st[:, q, 4, :])
                dve.drain()
                V.tensor_scalar(st[:, q, 5, :], st[:, q, 5, :], XS, None, ALU.mult)
                dve.drain()
                V.tensor_tensor(tmp[:, :, :], centered[:, :, :], bc(st[:, q, 5, :], 2, C), ALU.mult).then_inc(s["scaled"], 1)

            def split_l(n, half):
                dve.wait_ge(s["h_cast"], n + 1)
                if half is None:
                    V.tensor_tensor(split[:, :, 2 * C:4 * C].rearrange("p t (a c) -> p t a c", a=2), bc(tmp[:, :, :], 2, 2),
                                    split[:, :, 0:2 * C].rearrange("p t (a c) -> p t a c", a=2), ALU.subtract).then_inc(s["split_done"], 1)
                else:
                    h = half * 2 * C
                    V.tensor_tensor(split[:, :, h + C:h + 2 * C], tmp[:, :, :], split[:, :, h:h + C], ALU.subtract).then_inc(s["split_done"], 1)

            def nothing(): pass

            def mixer_norm(k, r, n, taken=None, summed=False, beside=(nothing, nothing)):
                if not summed:
                    dve.wait_ge(s["x_loaded"], (k + 1) * 16)
                ln_center(xm, xin[:, :, :], 2, summed)
                beside[0]()
                ln_var(tmp, 2, LNC_EPS, n)
                dve.wait_ge(s["std_done"], r + 1)
                V.reciprocal(st[:, 2, 5, :], st[:, 2, 4, :])
                dve.drain()
                V.tensor_tensor(st[:, 2, 6, :], st[:, 2, 2, :], st[:, 2, 5, :], ALU.mult)
                dve.drain()
                V.tensor_tensor(st[:, 2, 6, :], st[:, 2, 6, :], st[:, 2, 5, :], ALU.mult)
                dve.drain()
                V.tensor_scalar(st[:, 2, 3, :], st[:, 2, 6, :], 1e-12, None, ALU.max).then_inc(s["var_done"], 1)
                V.tensor_tensor(xm[:, :, :], xm[:, :, :], bc(st[:, 2, 5, :], 2, C), ALU.mult)
                dve.wait_ge(s["std_done"], r + 2)
                V.reciprocal(st[:, 2, 7, :], st[:, 2, 4, :])
                dve.drain()
                V.tensor_scalar(st[:, 2, 7, :], st[:, 2, 7, :], XS, None, ALU.mult)
                dve.drain()
                if taken:
                    dve.wait_ge(s["tr_done"], taken[0])
                V.tensor_tensor(tmp[:, :, :], xm[:, :, :], bc(st[:, 2, 7, :], 2, C), ALU.mult).then_inc(s["scaled"], 1)
                beside[1]()
                if taken:
                    dve.wait_ge(s["tr_done"], taken[1])
                split_l(n, None)

            def mixer_body(g, half_no, tile, nxt, own=None):
                plan = MIX_FIRST if own else MIX
                for u in range(SPB):
                    if u in DVE_STEPS:
                        dve.wait_ge(s["relu_done"], g + u + 1)
                        dve.wait_ge(s["mixed"], 2 * half_no + g + u + 1)
                        V.tensor_tensor(sq[:, u % 2], relu[:, u % 2], relu[:, u % 2], ALU.mult).then_inc(s["sq_dve"], 1)
                    for piece in range(5):
                        if own and plan["own"][piece] == u:
                            weigh(*own, piece)
                    if tile and u == plan["add"]:
                        sample_add(*tile)
                    for piece in range(5):
                        if nxt and plan["weigh"][piece] == u:
                            weigh(*nxt, piece)

            def mixer(k, back):
                for half in range(2):
                    g0 = k * SPI + half * SPH
                    t0 = half * BPH

                    def body(j, v, u2):
                        nt = t0 + v + 1
                        nxt = (k - 1, j - v + nt, nt % 2, u2 + nt // 2) if back else None
                        first = back and half == 0 and isinstance(j, int) and j == 0
                        mixer_body(g0 + j * SPB, k * 2 + half, (k - 1, j + t0) if back else None, nxt,
                                   (k - 1, 0, 0, 0) if first else None)

                    for j in range(2):
                        body(j, j, 0)
                    with dve.Fori(1, BPH // 2) as bb:
                        for v in range(2):
                            body(bb * 2 + v, v, bb)
                    body(BPH - 1, 0, (BPH - 1) // 2)
                    for m in range(2):
                        dve.wait_ge(s["y_done"], k * 4 + half * 2 + m + 1)
                        r = slice(half * 14 + m * 7, half * 14 + m * 7 + 7)
                        V.tensor_tensor(x1[:, r, :], xin[:, r, :], (D1, Y1)[m][0:TP, 0:7 * C].rearrange("p (t c) -> p t c", c=C),
                                        ALU.add).then_inc(s["x1_added"], 1)

            def gate(k):
                p = small[:, 0, 0:T * E].rearrange("p (t e) -> p t e", e=E)
                o1 = small[:, 1, 0:T * E].rearrange("p (t e) -> p t e", e=E)
                o2 = small[:, 2, 0:T * E].rearrange("p (t e) -> p t e", e=E)
                c = small[:, 3, 0:T * E].rearrange("p (t e) -> p t e", e=E)
                m, r, m1, m2, den = (smallc[:, i, :] for i in range(5))

                def tt(o, a, b, op):
                    V.tensor_tensor(o, a, b, op)
                    dve.drain()

                def rd(o, a, op):
                    red(o, a, op)
                    dve.drain()

                def first_max(oh, top, src):
                    rd(top, src, ALU.max)
                    tt(oh, src, bc(top, 2, E), ALU.is_equal)
                    tt(c, oh, bc(rank[:, :], 1, T), ALU.mult)
                    rd(den, c, ALU.max)
                    tt(oh, c, bc(den, 2, E), ALU.is_equal)

                dve.wait_ge(s["logits_done"], k + 1)
                V.scalar_tensor_tensor(p, D0[0:TP, 0:T * E].rearrange("p (t e) -> p t e", e=E), descale[0:TP, GATE:GATE + 1],
                                       bc(gbias[:, :], 1, T), ALU.mult, ALU.add)
                dve.drain()
                rd(m, p, ALU.max)
                V.tensor_tensor(p, p, bc(m, 2, E), ALU.subtract).then_inc(s["sm_shift"], 1)
                dve.wait_ge(s["sm_exp"], k + 1)
                rd(m, p, ALU.add)
                V.reciprocal(r, m)
                dve.drain()
                tt(p, p, bc(r, 2, E), ALU.mult)
                first_max(o1, m1, p)
                V.scalar_tensor_tensor(p, o1, -2.0, p, ALU.mult, ALU.add)
                dve.drain()
                first_max(o2, m2, p)
                tt(den, m1, m2, ALU.add)
                V.reciprocal(r, den)
                dve.drain()
                V.scalar_tensor_tensor(m1, m1, XS, r, ALU.mult, ALU.mult)
                V.scalar_tensor_tensor(m2, m2, XS, r, ALU.mult, ALU.mult)
                dve.drain()
                V.tensor_tensor(o1, o1, bc(m1, 2, E), ALU.mult)
                V.tensor_tensor(o2, o2, bc(m2, 2, E), ALU.mult)
                dve.drain()
                tt(disp[:, :, :], o1, o2, ALU.add)
                V.tensor_copy(dsplit[:, :, 0:E], disp[:, :, :])
                dve.drain()
                V.tensor_tensor(dsplit[:, :, E:2 * E], disp[:, :, :], dsplit[:, :, 0:E], ALU.subtract).then_inc(s["disp_split"], 1)

            def experts_chunk(k, c, tiles, nexts):
                n0 = k * (NCH * E) + c * E
                p0 = k * (NCH * E // 2) + c * (E // 2)

                def scale_pair(p):
                    dve.wait_ge(s["share_ready"], p0 + p + 1)
                    dve.wait_ge(s["down_done"], p0 + p + 1)
                    V.tensor_tensor(scaled_y[:, p % 2, :], Y0[:, 0:CW], share[:, p % 2, :], ALU.mult).then_inc(s["scaled_done"], 1)

                for e in range(E):
                    dve.wait_ge(s["silu_done"], n0 + e + 1)
                    V.scalar_tensor_tensor(hid[:, e % 4, :], S[2 + e % 2][:, 0:CW], descale[:, MOE2:MOE2 + 1], silu[:, e % 2, :],
                                           ALU.mult, ALU.mult).then_inc(s["hid_done"], 1)
                    if e % 2 and e > 1:
                        scale_pair(e // 2 - 1)
                    if tiles and e % 8 == MOE_ADD:
                        sample_add(*tiles[e // 8])
                    if nexts and nexts[e // 8] and e % 8 in MOE_WEIGH:
                        weigh(*nexts[e // 8], MOE_WEIGH.index(e % 8))
                scale_pair(E // 2 - 1)
                dve.wait_ge(s["ytm_done"], k * NCH + c + 1)
                xt = x1[:, :, :].rearrange("p t c -> p (t c)")[:, bass.ds(c * (CT * C), CT * C)].rearrange("p (t c) -> p t c", t=CT)
                y = D1[0:TP, :].rearrange("p (t h c) -> p t h c", t=CT, h=2)
                V.tensor_tensor(xt, xt, y[:, :, 0, :], ALU.add)
                dve.drain()
                V.tensor_tensor(xt, xt, y[:, :, 1, :], ALU.add).then_inc(s["x2_added"], 1)

            def positions(k):
                base = grid[:, :, :]
                v18 = lambda i: small[:, i, :].rearrange("p (t n) -> p t n", t=T)
                dve.wait_ge(s["om_taken"], k * 2 + 2)
                V.tensor_tensor(v18(0), om[:, :, 0:18], base, ALU.add)
                dve.drain()
                V.tensor_scalar(v18(0), v18(0), 0.0, float(H + 1), ALU.max, ALU.min)
                dve.drain()
                V.tensor_copy(v18(1).bitcast(i32), v18(0))
                dve.drain()
                V.tensor_copy(v18(2), v18(1).bitcast(i32))
                dve.drain()
                V.tensor_tensor(v18(1), v18(2), v18(0), ALU.is_gt)
                dve.drain()
                V.tensor_tensor(v18(1), v18(2), v18(1), ALU.subtract)
                dve.drain()
                V.tensor_tensor(v18(2), v18(0), v18(1), ALU.subtract)
                dve.drain()
                V.tensor_scalar(v18(3), v18(2), -1.0, 1.0, ALU.mult, ALU.add)

            def corners(k, has_back):
                dve.drain()
                yx = lambda i: small[:, i, :].rearrange("p (n two) -> p n two", two=2)
                V.scalar_tensor_tensor(small[:, 4, 0:T * TAPS], yx(1)[:, :, 0], float(SIDE), yx(1)[:, :, 1], ALU.mult, ALU.add)
                dve.drain()
                V.tensor_copy(index[:, :], small[:, 4, 0:T * TAPS])
                dve.drain()
                dve.wait_ge(s["mask_out"], k * 2 + 2)
                m = mask[:, :, :].rearrange("p t n -> p (t n)")
                a0, a1 = small[:, 0, 0:T * TAPS], small[:, 4, 0:T * TAPS]
                V.tensor_tensor(a0, yx(3)[:, :, 0], m, ALU.mult)
                V.tensor_tensor(a1, yx(2)[:, :, 0], m, ALU.mult)
                dve.drain()
                V.tensor_tensor(corner_w[:, :, 0], a0, yx(3)[:, :, 1], ALU.mult)
                V.tensor_tensor(corner_w[:, :, 1], a0, yx(2)[:, :, 1], ALU.mult)
                V.tensor_tensor(corner_w[:, :, 2], a1, yx(3)[:, :, 1], ALU.mult)
                V.tensor_tensor(corner_w[:, :, 3], a1, yx(2)[:, :, 1], ALU.mult)
                if has_back:
                    dve.wait_ge(s["x3_stored"], 16 * k)
                V.tensor_copy(xB[:, :, :], x1[:, :, :])
                dve.drain()
                V.memset(cnt16[:, :], 0.0).then_inc(s["geo_done"], 1)

            def add_skip():
                dve.drain()
                V.scalar_tensor_tensor(xB[:, :, :], tmp[:, :, :], 1.0 / XS, xB[:, :, :], ALU.mult, ALU.add).then_inc(s["skip_added"], 1)

            def ffn_bias(f):
                dve.wait_ge(s["fdown_done"], f + 1)
                w = w_all[:, :, :].rearrange("p b t -> p (b t)")[:, bass.ds(f * T, T)]
                V.tensor_scalar(w, D1[0:TP, 448:448 + T], descale[0:TP, ROUTE:ROUTE + 1], brc[:, 0:1], ALU.mult, ALU.add)
                for i, bank in enumerate((Y0, Y1, D0, D1)):
                    t0, t1 = i * 2 * CT, min((i + 1) * 2 * CT, T)
                    ins = V.tensor_tensor(yw[:, t0:t1, :], bank[0:TP, 0:(t1 - t0) * C].rearrange("p (t c) -> p t c", c=C),
                                          bc(fb2r[:, :], 1, t1 - t0), ALU.add)
                ins.then_inc(s["fout_read"], 1)

            def ffn_weigh(f):
                dve.drain()
                w = w_all[:, :, :].rearrange("p b t -> p (b t)")[:, bass.ds(f * T, T)]
                V.tensor_tensor(yw[:, :, :], yw[:, :, :], bc(w, 2, C), ALU.mult).then_inc(s["yw_done"], 1)

            def image(k, back, has_next):
                r0, n0, c0 = rounds_before(k, back), splits_before(k, back), chunks_before(k, back)
                bk = 1 if back else 0
                mixer(k, back)
                dve.drain()
                ln_center(xm, x1[:, :, :], 0)
                ln_var(tmp, 0, LNT_EPS, n0)
                ln_scale(xm, 0, r0)
                split_l(n0, 0)
                gate(k)

                def chunk(c, last):
                    tiles = [(k - 1, c * 2 + 14 + i) for i in range(2)] if back else None
                    nexts = [(k - 1, c * 2 + 15, 1, c + 7), None if last else (k - 1, c * 2 + 16, 0, c + 8)] if back else None
                    experts_chunk(k, c, tiles, nexts)

                with dve.Fori(0, NCH - 1) as c:
                    chunk(c, False)
                chunk(NCH - 1, True)
                dve.drain()
                if back:
                    dve.wait_ge(s["table_written"], k * 128)
                ln_center(xln, x1[:, :, :], 0)
                if back:
                    ln_center(xm, xB[:, :, :], 1)
                ln_var(tmp, 0, LNC_EPS, n0 + 1)
                if back:
                    ln_var(split_f, 1, LNT_EPS, n0 + 2)
                if has_next:
                    dve.wait_ge(s["x_loaded"], (k + 2) * 16)
                    red(st[:, 2, 0, :], xin[:, :, :])
                ln_scale(xln, 0, r0 + 1)
                if back:
                    ffn_bias(k - 1)
                split_l(n0 + 1, 0)
                if back:
                    dve.wait_ge(s["geo_ln"], k + 1)
                    ln_scale(xm, 1, r0 + 2)
                    add_skip()
                    split_l(n0 + 2, 1)
                if has_next:
                    dve.drain()
                    mixer_norm(k + 1, r0 + 2 + bk, n0 + 2 + bk, (c0 + 2 * NCH, c0 + (2 + bk) * NCH), True,
                               (lambda: ffn_weigh(k - 1) if back else None, lambda: positions(k)))
                else:
                    if back:
                        ffn_weigh(k - 1)
                    positions(k)
                corners(k, back)
                if back:
                    dve.wait_ge(s["yw_stored"], 16 * k)

            V.memset(table_cell[:, :], 0.0)
            V.memset(stage3[:, 0:1280], 0.0)
            V.memset(obias[:, :], 0.0).then_inc(s["bias_zero"], 1)
            dve.wait_ge(s["ident_loaded"], 16)
            V.tensor_copy(ident16[:, :], ident[0:TP, 0:TP])
            mixer_norm(0, 0, 0)
            V.memset(padded[:, :], 0.0)
            V.memset(zero16[:, :], 0.0)
            V.memset(xf[:, :], 0.0)
            V.memset(ones16[:, :], 1.0)
            V.memset(pick[:, :], 0.0)
            V.memset(dcn[0:C, TAPS // 2, :], 0.0)
            dve.wait_ge(s["w_staged"], 16 * 15)
            dve.wait_ge(s["w_loaded"], 16 * 17)
            pieces = ((MOE1, w1h[:, :], w1l[:, :], stage[:, 0:E * HID]), (MOE2, w2h[:, :], w2l[:, :], stage2[:, 0:E * HID]),
                      (GATE, gateh[:, :], gatel[:, :], stage3[:, 0:E]), (OFF, offh[:, :], offl[:, :], stage3[:, 64:64 + TAPS * OC]),
                      (FFN1, f1h[:, :], f1l[:, :], stage3[:, 1024:1024 + FH]), (ROUTE, wrh[:, 0:1], wrl[:, 0:1], stage3[:, 768:769]))
            magnitudes([(col, src) for col, _h, _l, src in pieces])
            V.tensor_copy(tri16[:, :], stage3[0:TP, 1280:1280 + TP])
            V.tensor_copy(bits[:, :, :], stage3[0:TP, 1408:1408 + 3 * ROUNDS].rearrange("p (r c) -> p r c", c=3))
            V.tensor_copy(incs[:, :, :], stage3[0:TP, 1408 + 3 * ROUNDS:1408 + 6 * ROUNDS].rearrange("p (r c) -> p r c", c=3))
            V.tensor_copy(pick[0:2 * E, :], stage3[0:2 * E, 1536:1536 + E * C])
            dve.drain()
            V.memset(cnt16[:, :], 0.0).then_inc(s["amax_done"], 1)
            dve.wait_ge(s["amax_red"], 1)
            scales(0, NW)
            for col, h, l, src in pieces:
                V.tensor_scalar(h, src, wscale[:, col:col + 1], None, ALU.mult)
            dve.drain()
            for col, h, l, src in pieces:
                V.scalar_tensor_tensor(l, src, wscale[:, col:col + 1], h, ALU.mult, ALU.subtract)
            dve.drain()
            V.memset(cnt16[:, :], 0.0).then_inc(s["const_done"], 1)
            V.memset(stage[:, :], 0.0).then_inc(s["stage_zero"], 1)

            image(0, False, True)
            with dve.Fori(1, B - 1) as k:
                image(k, True, True)
            image(B - 1, True, False)
            def views(b0, nb):
                f = lambda v: v[:, 0:nb * T].rearrange("p (b t) -> p b t", b=nb)
                img = slice(b0, b0 + nb)
                return f, w_img[:, img, :], [kf[:, i, img] for i in range(8)], [ki[:, i, img] for i in range(3)], S[0][0:TP, :]

            def choose_start(b0, nb, n):
                f, w, (sgn, kth, got, *_r), (now, *_i), ps = views(b0, nb)
                V.tensor_scalar(f(hit), w, 0.0, None, ALU.is_ge)
                V.memset(now, 0.0)
                dve.drain()
                tokens(cnt16[:, 0:nb], f(hit))
                dve.wait_ge(s["count_done"], n + 1)
                V.tensor_scalar(got, ps[:, 0:nb], float(KTOP), None, ALU.is_ge)
                dve.drain()
                V.tensor_scalar(sgn, got, 2.0, -1.0, ALU.mult, ALU.add)
                V.tensor_scalar(kth, got, float(KTOP - (N - KTOP + 1)), float(N - KTOP + 1), ALU.mult, ALU.add)
                dve.drain()
                V.tensor_tensor(f(key), w, bc(sgn, 2, T), ALU.mult)

            def tokens(dst, src):
                with nc.allow_low_precision("counts up to T are exact in float16"):
                    red(dst, src).then_inc(s["count_in"], 1)

            def round_try(b0, nb, i):
                f, _w, _kf, (now, *_i), _ps = views(b0, nb)
                c3 = cand[:, 0:3 * nb].rearrange("p (b c) -> p b c", b=nb)
                dve.drain()
                V.tensor_tensor(c3, bc(now, 2, 3), bits[:, bass.ds(i, 1), :].to_broadcast([TP, nb, 3]), ALU.bitwise_or)
                dve.drain()
                h3 = hit[:, 0:3 * nb * T].rearrange("p (b c t) -> p b c t", b=nb, c=3)
                V.tensor_tensor(h3, bc(f(key), 2, 3), bc(c3.bitcast(f32), 3, T), ALU.is_ge)
                dve.drain()
                tokens(cnt16[:, 0:3 * nb], hit[:, 0:3 * nb * T].rearrange("p (c t) -> p c t", t=T))

            def round_take(b0, nb, i, n):
                _f, _w, (_sgn, kth, *_r), (now, add, *_i), ps = views(b0, nb)
                g3 = got3[:, 0:3 * nb].rearrange("p (b c) -> p b c", b=nb)
                dve.wait_ge(s["count_done"], n + i + 2)
                V.tensor_tensor(g3, ps[:, 0:3 * nb].rearrange("p (b c) -> p b c", b=nb), bc(kth, 2, 3), ALU.is_ge)
                dve.drain()
                V.tensor_tensor(g3, g3, incs[:, bass.ds(i, 1), :].to_broadcast([TP, nb, 3]), ALU.mult)
                dve.drain()
                with nc.allow_low_precision("two bits of an integer are exact"):
                    red(add, g3)
                dve.drain()
                V.tensor_tensor(now, now, add, ALU.bitwise_or)

            def choose_end(b0, nb, n):
                f, w, (sgn, _k, _g, thr, need, *_r), (now, *_i), ps = views(b0, nb)
                chosen = sel[:, b0:b0 + nb, :]
                dve.drain()
                V.tensor_tensor(thr, now.bitcast(f32), sgn, ALU.mult)
                dve.drain()
                V.tensor_tensor(chosen, w, bc(thr, 2, T), ALU.is_gt)
                V.tensor_tensor(f(eqf), w, bc(thr, 2, T), ALU.is_equal)
                dve.drain()
                V.tensor_copy(eq16[:, 0:nb * T], eqf[:, 0:nb * T])
                tokens(cnt16[:, 0:nb], chosen)
                dve.wait_ge(s["count_done"], n + ROUNDS + 2)
                V.tensor_scalar(need, ps[:, 0:nb], -1.0, float(KTOP), ALU.mult, ALU.add).then_inc(s["tie_in"], 1)
                dve.wait_ge(s["tie_done"], 1 if n == 0 else 2)
                V.tensor_copy(pre[:, 0:nb * T], S[0][0:TP, 0:nb * T])
                V.tensor_copy(tot[:, 0:nb * T], S[1][0:TP, 0:nb * T])
                dve.drain()
                a, o = f(tot), f(run)
                V.memset(o[:, :, 0:1], 0.0)
                V.tensor_copy(o[:, :, 1:T], a[:, :, 0:T - 1])
                dve.drain()
                a, o = o, a
                for sh in (1, 2, 4, 8, 16):
                    V.tensor_copy(o[:, :, 0:sh], a[:, :, 0:sh])
                    V.tensor_tensor(o[:, :, sh:T], a[:, :, sh:T], a[:, :, 0:T - sh], ALU.add)
                    dve.drain()
                    a, o = o, a
                V.tensor_tensor(f(pre), f(pre), a, ALU.add)
                dve.drain()
                V.tensor_tensor(f(pre), f(pre), bc(need, 2, T), ALU.is_lt)
                dve.drain()
                V.tensor_tensor(f(pre), f(pre), f(eqf), ALU.mult)
                dve.drain()
                V.tensor_tensor(chosen, chosen, f(pre), ALU.add)
                dve.drain()

            def final(k, xv, yv):
                V.tensor_tensor(yv, yv, bc(sel[:, k, :], 2, C), ALU.mult)
                dve.drain()
                V.tensor_tensor(xv, xv, yv, ALU.add).then_inc(s["fin_ready"], 1)

            def final_back(k):
                q = k % 2
                dve.wait_ge(s[f"x3_back{q}"], 16 * (k // 2 + 1))
                dve.wait_ge(s[f"yw_back{q}"], 16 * (k // 2 + 1))
                final(k, fin_x[q], fin_y[q])

            ffn_bias(B - 1)
            ffn_weigh(B - 1)
            choose_start(0, B - 1, 0)
            for piece in range(5):
                weigh(B - 1, 0, 0, 0, piece)

            def sample_rest(u, q, beside=nothing, after=nothing, last=False):
                nxt = (B - 1, u * 2 + q + 1, 1 - q, u + q)
                for piece in range(0 if last else 4):
                    weigh(*nxt, piece)
                beside()
                sample_add(B - 1, u * 2 + q)
                if not last:
                    weigh(*nxt, 4)
                after()

            with dve.Fori(0, ROUNDS // 2) as u:
                for q in range(2):
                    sample_rest(u, q, lambda: round_try(0, B - 1, u * 2 + q), lambda: round_take(0, B - 1, u * 2 + q, 0))
            for u in range(ROUNDS // 2, T // 2):
                for q in range(2):
                    sample_rest(u, q, last=u * 2 + q == T - 1)
                    if u == ROUNDS // 2 and q == 0:
                        choose_end(0, B - 1, 0)
                    elif q == 1 and u - ROUNDS // 2 < B - 1:
                        final_back(u - ROUNDS // 2)
            for k in range(T // 2 - ROUNDS // 2, B - 1):
                final_back(k)
            dve.drain()
            ln_center(xm, xB[:, :, :], 1)
            ln_var(split_f, 1, LNT_EPS, 4 * B - 1)
            ln_scale(xm, 1, 5 * B - 1)
            split_l(4 * B - 1, 0)
            add_skip()
            dve.wait_ge(s["yw_stored"], 16 * B)
            ffn_bias(B)
            ffn_weigh(B)
            dve.drain()
            choose_start(B - 1, 1, ROUNDS + 2)
            with dve.Fori(0, ROUNDS) as i:
                round_try(B - 1, 1, i)
                round_take(B - 1, 1, i, ROUNDS + 2)
            choose_end(B - 1, 1, ROUNDS + 2)
            final(B - 1, xB[:, :, :], yw[:, :, :])

        @block.scalar
        def _(act):
            def sqrt_round(r, q=0):
                act.wait_ge(s["var_done"], r + 1)
                A.activation(st[:, q, 4, :], st[:, q, 3, :], ACT.Sqrt).then_inc(s["std_done"], 1)

            def square(n, dst, src):
                act.wait_ge(s["centered"], n + 1)
                A.activation(dst[:, :, :], src[:, :, :], ACT.Square).then_inc(s["squared"], 1)

            def cast_h(n, half):
                act.wait_ge(s["scaled"], n + 1)
                if half is None:
                    A.activation(split[:, :, 0:2 * C].rearrange("p t (a c) -> p t a c", a=2), bc(tmp[:, :, :], 2, 2),
                                 ACT.Copy).then_inc(s["h_cast"], 1)
                else:
                    A.activation(split[:, :, half * 2 * C:half * 2 * C + C], tmp[:, :, :], ACT.Copy).then_inc(s["h_cast"], 1)

            def sample_evac(b, t, stage):
                n = b * T + t + 1
                if stage == 0:
                    act.wait_ge(s["val_tr"], n * 2 - 1)
                    A.activation(val_cm[:, 0:4 * TP], D0[:, 0:4 * TP], ACT.Copy).then_inc(s["val_ready"], 1)
                if stage == 1:
                    act.wait_ge(s["val_tr"], n * 2)
                    A.activation(val_cm[:, 4 * TP:5 * TP], D0[:, 0:TP], ACT.Copy).then_inc(s["val_ready"], 1)
                if stage == 2:
                    act.wait_ge(s["conv_done"], n)
                    A.activation(dcn_cm[:, :], D0[:, 128:128 + TP], ACT.Copy).then_inc(s["conv_ready"], 1)

            def stage_sources(par, j0):
                A.activation(xj[:, par, :, :].rearrange("p j c -> p (j c)"),
                             xm[:, :, :].rearrange("p t c -> p (t c)")[:, bass.ds(j0 * C, JB * C)], ACT.Copy).then_inc(s["xj_ready"], 1)

            def relu_step(s_no, u):
                act.wait_ge(s["sim_done"], s_no + 1)
                A.activation(relu[:, u % 2], PS[u % 2][0:TP, :, 0:IW], ACT.Relu).then_inc(s["relu_done"], 1)

            def mixer_body(g, body_no, half_no, tile, first, last, next_sources, plan):
                for u in range(SPB):
                    if u + 1 < SPB or not last:
                        v = (u - 1) % SPB
                        no = body_no + (0 if u else -1)
                        if not (first and u == 0):
                            if v in DVE_STEPS:
                                act.wait_ge(s["sq_dve"], no * DVE_N + DVE_STEPS.index(v) + 1)
                            else:
                                act.wait_ge(s["sq_act"], no * ACT_N + ACT_STEPS.index(v) + 1)
                        relu_step(g + u + 1, u + 1)
                    if u in ACT_STEPS:
                        act.wait_ge(s["relu_done"], g + u + 1)
                        act.wait_ge(s["mixed"], 2 * half_no + g + u + 1)
                        A.activation(sq[:, u % 2], relu[:, u % 2], ACT.Square).then_inc(s["sq_act"], 1)
                    for stage in range(3):
                        if tile and plan["evac"][stage] == u:
                            sample_evac(*tile, stage)
                    if u == SPB - 2 and not last:
                        act.wait_ge(s["mixed"], 2 * (half_no + 1) + g)
                        stage_sources(*next_sources)

            def mixer(k, back):
                for half in range(2):
                    g0 = k * SPI + half * SPH
                    hn = k * 2 + half
                    stage_sources(0, 0)
                    relu_step(g0, 0)

                    def body(j, v, first, last):
                        mixer_body(g0 + j * SPB, hn * BPH + j, hn, (k - 1, j + half * BPH) if back else None, first, last,
                                   (1 - v, (j + 1) * JB), MIX_FIRST if first and half == 0 else MIX)

                    for j in range(2):
                        body(j, j, j == 0, False)
                    with act.Fori(1, BPH // 2) as bb:
                        for v in range(2):
                            body(bb * 2 + v, v, False, False)
                    body(BPH - 1, (BPH - 1) % 2, False, True)
                    act.wait_ge(s["mixed"], 2 * (hn + 1) + g0 + SPH)
                    for blk in range(4):
                        r = (blk % 2) * C
                        ins = A.activation(z_cm[:, blk * IW:(blk + 1) * IW], (Y0, Y1)[blk // 2][r:r + C, 0:IW], ACT.Copy,
                                           scale=1.0 / XS ** 4)
                    ins.then_inc(s["z_ready"], 1)

            def experts_chunk(k, c, tiles):
                n0 = k * (NCH * E) + c * E
                p0 = k * (NCH * E // 2) + c * (E // 2)

                for e in range(E):
                    act.wait_ge(s["up_done"], n0 + e + 1)
                    A.activation(silu[:, e % 2, :], S[e % 2][:, 0:CW], ACT.Silu, scale=descale[:, MOE1:MOE1 + 1]).then_inc(s["silu_done"], 1)
                    if tiles and e % 8 in MOE_EVAC:
                        sample_evac(*tiles[e // 8], MOE_EVAC.index(e % 8))
                    if e % 2:
                        act.wait_ge(s["share_done"], p0 + e // 2 + 1)
                        A.activation(share[:, e // 2 % 2, :], Y1[:, 0:CW], ACT.Copy, scale=1.0 / XS).then_inc(s["share_ready"], 1)

            def ffn(f, first=0, end=NCH):
                for c in range(first, end):
                    for m in range(2):
                        act.wait_ge(s["fup_done"], f * (2 * NCH) + 2 * c + m + 1)
                        A.activation(hid[:, (2 * c + m) % 4, :], S[(2 * c + m) % 4][:, 0:CW], ACT.Gelu_apprx_tanh,
                                     bias=fb1c[:, m:m + 1], scale=descale[:, FFN1:FFN1 + 1]).then_inc(s["gelu_done"], 1)

            def evac_tr(n, dsts, first=0, end=None):
                for i, dst in list(enumerate(dsts))[first:end]:
                    act.wait_ge(s["tr_done"], n + i + 1)
                    A.activation(dst, S[i % 4][:, 0:CW] if len(dst.shape) == 2 else
                                 S[i % 4][:, 0:CW].rearrange("p (y x) -> p y x", x=W), ACT.Copy).then_inc(s["tr_cm"], 1)

            def stacks(c0):
                evac_tr(c0, [dst[:, c * CW:(c + 1) * CW] for c in range(NCH) for dst in (xn_hl, xn_hh, xn_ll)])

            def image(k, back, has_next):
                r0, n0, c0 = rounds_before(k, back), splits_before(k, back), chunks_before(k, back)
                bk = 1 if back else 0
                mixer(k, back)
                A.activation(table_cell[:, 2:3], table_cell[:, 0:1], ACT.Sqrt)
                square(n0, tmp, xm)
                sqrt_round(r0)
                cast_h(n0, 0)
                evac_tr(c0, [xn_hl[:, c * CW:(c + 1) * CW] for c in range(NCH)])
                act.wait_ge(s["sm_shift"], k + 1)
                A.activation(small[:, 0, 0:T * E], small[:, 0, 0:T * E], ACT.Exp).then_inc(s["sm_exp"], 1)
                A.activation(table_cell[:, 1:2], table_cell[:, 0:1], ACT.Silu)
                for c in range(NCH):
                    act.wait_ge(s["disp_tr"], k * NCH + c + 1)
                    A.activation(dT[0:2 * E, c * CW:(c + 1) * CW], (D0, D1, Y0)[c % 3][0:2 * E, 0:CW], ACT.Copy).then_inc(s["disp_cm"], 1)
                with act.Fori(0, NCH) as c:
                    experts_chunk(k, c, [(k - 1, c * 2 + 14 + q) for q in range(2)] if back else None)
                if back:
                    ffn(k - 1, 0, FFN_CUT[0])
                square(n0 + 1, tmp, xln)
                if back:
                    ffn(k - 1, FFN_CUT[0], FFN_CUT[1])
                    square(n0 + 2, split_f, xm)
                    ffn(k - 1, FFN_CUT[1])
                sqrt_round(r0 + 1)
                if back:
                    sqrt_round(r0 + 2, 1)
                cast_h(n0 + 1, 0)
                A.activation(xln[:, :, :], tmp[:, :, :], ACT.Copy, scale=1.0 / XS).then_inc(s["geo_ln"], 1)
                pad_rows = [pad_v[:, 1 + 8 * c:9 + 8 * c, 1:1 + W] for c in range(NCH)]
                evac_tr(c0 + NCH, pad_rows, 0, 4)
                if back:
                    cast_h(n0 + 2, 1)
                evac_tr(c0 + NCH, pad_rows, 4)
                if has_next:
                    square(n0 + 2 + bk, tmp, xm)
                    sqrt_round(r0 + 2 + bk, 2)
                    sqrt_round(r0 + 3 + bk, 2)
                for g in range(2):
                    act.wait_ge(s["om_done"], k * 2 + g + 1)
                    rows = 128 if g == 0 else OC * (NCH - 4)
                    A.activation(om_c[g][0:rows, :], S[g][0:rows, 0:CW], ACT.Identity, bias=obias[0:rows, 0:1],
                                 scale=descale[0:rows, OFF:OFF + 1]).then_inc(s["om_ready"], 1)

                def taken(g):
                    nt = 4 if g == 0 else NCH - 4
                    tiles = slice(16 * g, 16 * g + CT * nt)
                    ps = (Y0, Y1)[g][0:TP, :].rearrange("p (s g o) -> p g s o", s=CT, o=OC)[:, 0:nt]
                    return tiles, ps

                for g in range(2):
                    act.wait_ge(s["om_tr"], k * 2 + g + 1)
                    tiles, ps = taken(g)
                    A.activation(om[:, tiles, :].rearrange("p (g s) o -> p g s o", s=CT), ps, ACT.Copy).then_inc(s["om_taken"], 1)
                xf_chunks = [xf[:, c * CW:(c + 1) * CW] for c in range(NCH)]
                if back:
                    evac_tr(c0 + 2 * NCH, xf_chunks, 0, 3)
                if has_next:
                    cast_h(n0 + 2 + bk, None)
                for g in range(2):
                    tiles, ps = taken(g)
                    A.activation(mask[:, tiles, :].rearrange("p (g s) o -> p g s o", s=CT), ps[:, :, :, 18:27],
                                 ACT.Sigmoid).then_inc(s["mask_out"], 1)
                if back:
                    evac_tr(c0 + 2 * NCH, xf_chunks, 3)
                if has_next:
                    stacks(c0 + (2 + bk) * NCH)

            square(0, tmp, xm)
            sqrt_round(0, 2)
            sqrt_round(1, 2)
            cast_h(0, None)
            stacks(0)
            act.wait_ge(s["w_loaded"], 16 * 17)
            act.wait_ge(s["const_done"], 1)
            image(0, False, True)
            with act.Fori(1, B - 1) as k:
                image(k, True, True)
            image(B - 1, True, False)
            ffn(B - 1)
            with act.Fori(0, T) as t:
                for n in range(3):
                    sample_evac(B - 1, t, n)
            square(4 * B - 1, split_f, xm)
            sqrt_round(5 * B - 1, 1)
            cast_h(4 * B - 1, 0)
            evac_tr(B * 6 * NCH - NCH, [xf[:, c * CW:(c + 1) * CW] for c in range(NCH)])
            ffn(B)

        @block.tensor
        def _(pe):
            UPS, START = "ups", "start"

            def mm(o, a, b, start=True, stop=True):
                return P.matmul(o, a, b, start=start, stop=stop, skip_group_check=True)

            def transpose_tile(o, t, col):
                return mm(o, split[:, :, :].rearrange("p t c -> p (t c)")[:, bass.ds(t * (4 * C) + col, 2 * C)], ident16[:, :])

            def transpose_all(n, half=0, use=None):
                for c in range(NCH + 4 if use else NCH):
                    if c >= 4:
                        pe.wait_ge(s["tr_cm"], n + c - 3)
                        if use:
                            use(c - 4)
                    if c >= NCH:
                        continue
                    for i in range(CT):
                        ins = transpose_tile(S[c % 4][:, i * TP:(i + 1) * TP], c * CT + i, half * 2 * C)
                    ins.then_inc(s["tr_done"], 1)

            def stacks(c0, n):
                pe.wait_ge(s["split_done"], n + 1)
                for i in range(3 * NCH):
                    c, col = i // 3, (C, 0, 2 * C)[i % 3]
                    if i >= 4:
                        pe.wait_ge(s["tr_cm"], c0 + i - 3)
                    for m in range(CT):
                        ins = transpose_tile(S[i % 4][:, m * TP:(m + 1) * TP], c * CT + m, col)
                    ins.then_inc(s["tr_done"], 1)
                pe.wait_ge(s["tr_cm"], c0 + 3 * NCH)

            def sample(b, t, q, stage):
                n = b * T + t + 1
                if stage == 0:
                    pe.wait_ge(s["valued"], n)
                    for i in range(4):
                        ins = P.transpose(D0[:, i * TP:(i + 1) * TP], value[:, q, i * 128:(i + 1) * 128], ident[0:TP, 0:TP])
                    ins.then_inc(s["val_tr"], 1)
                if stage == 1:
                    pe.wait_ge(s["val_ready"], n * 2 - 1)
                    P.transpose(D0[:, 0:TP], value[:, q, 7 * C:9 * C], ident[0:TP, 0:TP])
                    for i in range(4):
                        h = i % 2
                        ins = mm(D0[h * C:(h + 1) * C, 128:128 + TP], dcn[:, i, :], val_cm[:, i * TP:(i + 1) * TP], i < 2, i == 3)
                    ins.then_inc(s["val_tr"], 1)
                if stage == 2:
                    pe.wait_ge(s["val_ready"], n * 2)
                    mm(D0[0:C, 128:128 + TP], dcn[:, 4, :], val_cm[:, 4 * TP:5 * TP], False, True).then_inc(s["conv_done"], 1)
                if stage == 3:
                    pe.wait_ge(s["conv_ready"], n)
                    mm(D0[0:TP, 448:448 + C], dcn_cm[:, :], ident2[:, :]).then_inc(s["dcn_done"], 1)

            def sims(j, i0, u):
                for b in range(2):
                    i = i0 + (u % 2 * 2 + b) * IW
                    o = PS[u % 2][0:TP, b, 0:IW]
                    mm(o, xn_hh[:, bass.ds(j * TP, TP)], xn_hl[:, i:i + IW], True, False)
                    ins = mm(o, xn_ll[:, bass.ds(j * TP, TP)], xn_hl[:, i:i + IW], False, True)
                ins.then_inc(s["sim_done"], 1)

            def mix(u, par, body_no):
                if u in ACT_STEPS:
                    pe.wait_ge(s["sq_act"], body_no * ACT_N + ACT_STEPS.index(u) + 1)
                else:
                    pe.wait_ge(s["sq_dve"], body_no * DVE_N + DVE_STEPS.index(u) + 1)
                for b in range(2):
                    ins = mm((Y0, Y1)[u % 2][b * C:(b + 1) * C, 0:IW], xj[:, par, u // 2, :], sq[:, u % 2, b], False, False)
                ins.then_inc(s["mixed"], 1)

            def mixer_body(i0, j0, par, g, body_no, first, last, tile, plan):
                for u in range(SPB):
                    if not (last and u >= SPB - 2):
                        pe.wait_ge(s["relu_done"], g + u + 1)
                        sims(j0 + (u + 2) // 2, i0, u)
                    for stage in range(4):
                        if tile and plan["sample"][stage] == u:
                            sample(*tile, stage)
                    if u:
                        mix(u - 1, par, body_no)
                    elif not first:
                        mix(SPB - 1, 1 - par, body_no - 1)
                    if u == 0:
                        pe.wait_ge(s["xj_ready"], body_no + 1)
                if last:
                    mix(SPB - 1, par, body_no)

            def mixer(k, back):
                for half in range(2):
                    i0 = half * 4 * IW
                    hn = k * 2 + half
                    g0 = k * SPI + half * SPH
                    if half:
                        pe.wait_ge(s["x1_added"], k * 4 + 2)
                    else:
                        sims(0, i0, 0)
                        sims(0, i0, 1)
                    for y in (Y0, Y1):
                        mm(y[:, 0:IW], zero16[:, 0:128], zero16[:, 0:IW], True, False).then_inc(s["mixed"], 1)

                    def body(j, v, first, last):
                        t = j + half * BPH
                        mixer_body(i0, j * JB, v % 2, g0 + j * SPB, hn * BPH + j, first, last,
                                   (k - 1, t, (v + half * BPH) % 2) if back else None,
                                   MIX_FIRST if first and half == 0 else MIX)

                    for j in range(2):
                        body(j, j, j == 0, False)
                    with pe.Fori(1, BPH // 2) as bb:
                        for v in range(2):
                            body(bb * 2 + v, v, False, False)
                    body(BPH - 1, BPH - 1, False, True)
                    if not half:
                        pe.wait_ge(s["relu_done"], g0 + SPH)
                        sims(0, i0 + 4 * IW, 0)
                        sims(0, i0 + 4 * IW, 1)
                    pe.wait_ge(s["z_ready"], k * 2 + half + 1)
                    for m in range(2):
                        for t in range(7):
                            c0 = (m * 7 + t) * TP
                            ins = mm((D1, Y1)[m][0:TP, t * C:(t + 1) * C], z_cm[:, c0:c0 + TP], w_mix[:, :])
                        ins.then_inc(s["y_done"], 1)

            def experts_chunk(k, c, tiles, last):
                n0 = k * (NCH * E) + c * E
                p0 = k * (NCH * E // 2) + c * (E // 2)

                def up(e, c):
                    cols = bass.ds(c * CW, CW)
                    for h, l, o in ((w1h, w1l, S[e % 2]), (w2h, w2l, S[2 + e % 2])):
                        mm(o[:, 0:CW], h[:, e * HID:(e + 1) * HID], xn_hl[:, cols], True, False)
                        ins = mm(o[:, 0:CW], l[:, e * HID:(e + 1) * HID], xn_hl[:, cols], False, True)
                    ins.then_inc(s["up_done"], 1)

                def spread(p, c):
                    mm(Y1[:, 0:CW], pick[:, p * 128:(p + 1) * 128], dT[:, bass.ds(c * CW, CW)]).then_inc(s["share_done"], 1)

                def collect(p):
                    for t in range(CT):
                        ins = P.matmul(D1[0:TP, t * 128:(t + 1) * 128], scaled_y[:, p % 2, t * TP:(t + 1) * TP], ident[:, :],
                                       start=p == 0 and t == 0, stop=p == E // 2 - 1, is_transpose=True, skip_group_check=True)
                    return ins

                if tiles is UPS:
                    up(0, c)
                    up(1, c)
                    return
                if tiles is START:
                    spread(0, c)
                    return
                for e in range(E):
                    pe.wait_ge(s["hid_done"], n0 + e + 1)
                    if e + 2 < E:
                        up(e + 2, c)
                    if tiles and e % 8 in MOE_SAMPLE:
                        sample(*tiles[e // 8], MOE_SAMPLE.index(e % 8))
                    if e % 2:
                        p = e // 2
                        if p:
                            pe.wait_ge(s["scaled_done"], p0 + p)
                        for b in range(2):
                            f = e - 1 + b
                            ins = mm(Y0[b * C:(b + 1) * C, 0:CW], w3s[:, f, :], hid[:, f % 4, :], True, True)
                        ins.then_inc(s["down_done"], 1)
                        pe.wait_ge(s["share_ready"], p0 + p + 1)
                        if p + 1 < E // 2:
                            spread(p + 1, c)
                        if p:
                            if p == 1 and not (isinstance(k, int) and isinstance(c, int) and k * NCH + c == 0):
                                pe.wait_ge(s["x2_added"], k * NCH + c)
                            collect(p - 1)
                if not last:
                    spread(0, c + 1)
                    up(0, c + 1)
                pe.wait_ge(s["scaled_done"], p0 + E // 2)
                collect(E // 2 - 1).then_inc(s["ytm_done"], 1)
                if not last:
                    up(1, c + 1)

            def ffn(f):
                def up(c):
                    for m in range(2):
                        o = S[(2 * c + m) % 4][:, 0:CW]
                        src = xf[:, c * CW:(c + 1) * CW]
                        mm(o, f1h[:, m * 128:(m + 1) * 128], src, True, False)
                        mm(o, f1l[:, m * 128:(m + 1) * 128], src, False, True).then_inc(s["fup_done"], 1)

                up(0)
                for c in range(NCH):
                    if c >= 1 and c + 1 < NCH:
                        pe.wait_ge(s["gelu_done"], f * (2 * NCH) + 2 * c)
                    if c + 1 < NCH:
                        up(c + 1)
                    pe.wait_ge(s["gelu_done"], f * (2 * NCH) + 2 * c + 2)
                    if c == 4:
                        images = min(f + 2, B) if isinstance(f, int) else f + 2
                        pe.wait_ge(s["x2_added"], images * NCH)
                    for t in range(CT):
                        col = (c % 2 * CT + t) * C
                        for m in range(2):
                            ins = mm((Y0, Y1, D0, D1)[c // 2][0:TP, col:col + C], hid[:, (2 * c + m) % 4, t * TP:(t + 1) * TP],
                                     f2s[:, m, :], m == 0, m == 1)
                for t in range(T):
                    for w in (wrh, wrl):
                        ins = mm(D1[0:TP, 448 + t:449 + t], xf[:, t * TP:(t + 1) * TP], w[:, 0:1], w is wrh, w is wrl)
                ins.then_inc(s["fdown_done"], 1)

            def image(k, back, has_next):
                n0, tr0 = splits_before(k, back), chunks_before(k, back)
                bk = 1 if back else 0
                mixer(k, back)
                pe.wait_ge(s["split_done"], n0 + 1)

                def logits(c):
                    for t in range(c * CT, (c + 1) * CT):
                        for w in (gateh, gatel):
                            ins = mm(D0[0:TP, t * E:(t + 1) * E], xn_hl[:, t * TP:(t + 1) * TP], w[:, :], w is gateh, w is gatel)
                    if c == NCH - 1:
                        ins.then_inc(s["logits_done"], 1)

                transpose_all(tr0, use=logits)
                experts_chunk(k, 0, UPS, False)
                pe.wait_ge(s["disp_split"], k + 1)
                for c in range(NCH):
                    if c >= 3:
                        pe.wait_ge(s["disp_cm"], k * NCH + c - 2)
                    for i in range(CT):
                        ins = mm((D0, D1, Y0)[c % 3][0:2 * E, i * TP:(i + 1) * TP], dsplit[:, c * CT + i, :], ident16[:, :])
                    ins.then_inc(s["disp_tr"], 1)
                pe.wait_ge(s["disp_cm"], (k + 1) * NCH)
                experts_chunk(k, 0, START, False)

                def chunk(c, last):
                    experts_chunk(k, c, [(k - 1, c * 2 + 14 + q, q) for q in range(2)] if back else None, last)

                if back:
                    with pe.Fori(0, NCH - 1) as c:
                        chunk(c, False)
                else:
                    chunk(0, False)
                    with pe.Fori(1, NCH - 1) as c:
                        chunk(c, False)
                chunk(NCH - 1, True)
                if back:
                    ffn(k - 1)
                    pe.wait_ge(s["gelu_done"], k * 2 * NCH)
                pe.wait_ge(s["split_done"], n0 + 2)
                transpose_all(tr0 + NCH)
                pe.wait_ge(s["tr_cm"], tr0 + 2 * NCH)
                for g in range(2):
                    nt = 4 if g == 0 else NCH - 4
                    for tap in range(TAPS):
                        for w in (offh, offl):
                            for i in range(nt):
                                y = 8 * (4 * g + i) + tap // 3
                                ins = mm(S[g][i * OC:(i + 1) * OC, 0:CW].rearrange("p (y x) -> p y x", x=W), w[:, tap * OC:(tap + 1) * OC],
                                         pad_v[:, y:y + 8, tap % 3:tap % 3 + W], tap == 0 and w is offh, tap == TAPS - 1 and w is offl)
                    ins.then_inc(s["om_done"], 1)
                if back:
                    pe.wait_ge(s["fout_read"], k)
                for g in range(2):
                    rows = 128 if g == 0 else OC * (NCH - 4)
                    pe.wait_ge(s["om_ready"], k * 2 + g + 1)
                    for i in range(CT):
                        ins = P.transpose((Y0, Y1)[g][0:TP, i * 128:i * 128 + rows], om_c[g][0:rows, i * TP:(i + 1) * TP], ident[0:rows, 0:rows])
                    ins.then_inc(s["om_tr"], 1)
                if back:
                    pe.wait_ge(s["split_done"], n0 + 3)
                    transpose_all(tr0 + 2 * NCH, 1)
                    pe.wait_ge(s["tr_cm"], tr0 + 3 * NCH)
                if has_next:
                    stacks(tr0 + (2 + bk) * NCH, n0 + 2 + bk)
                pe.wait_ge(s["mask_out"], k * 2 + 2)

            stacks(0, 0)
            pe.wait_ge(s["w_loaded"], 16 * 17)
            pe.wait_ge(s["const_done"], 1)
            image(0, False, True)
            with pe.Fori(1, B - 1) as k:
                image(k, True, True)
            image(B - 1, True, False)
            def count(n, columns):
                pe.wait_ge(s["count_in"], n)
                mm(S[0][0:TP, 0:columns], ones16[:, :], cnt16[:, 0:columns]).then_inc(s["count_done"], 1)

            def ties(n, nb):
                pe.wait_ge(s["tie_in"], n)
                mm(S[0][0:TP, 0:nb * T], tri16[:, :], eq16[:, 0:nb * T])
                mm(S[1][0:TP, 0:nb * T], ones16[:, :], eq16[:, 0:nb * T]).then_inc(s["tie_done"], 1)

            ffn(B - 1)
            pe.wait_ge(s["fout_read"], B)
            pe.wait_ge(s["gelu_done"], B * 2 * NCH)
            count(1, B - 1)
            with pe.Fori(0, ROUNDS // 2) as u:
                for q in range(2):
                    for n in range(4):
                        sample(B - 1, u * 2 + q, q, n)
                    count(u * 2 + q + 2, 3 * (B - 1))
            for u in range(ROUNDS // 2, T // 2):
                for q in range(2):
                    for n in range(4):
                        sample(B - 1, u * 2 + q, q, n)
                    if u == ROUNDS // 2 and q == 0:
                        count(ROUNDS + 2, B - 1)
                        ties(1, B - 1)
            pe.wait_ge(s["split_done"], 4 * B)
            transpose_all(B * 6 * NCH - NCH)
            pe.wait_ge(s["tr_cm"], B * 6 * NCH)
            ffn(B)
            pe.wait_ge(s["gelu_done"], (B + 1) * 2 * NCH)
            count(ROUNDS + 3, 1)
            with pe.Fori(0, ROUNDS) as i:
                count(i + ROUNDS + 4, 3)
            count(2 * ROUNDS + 4, 1)
            ties(2, 1)


def kernel(**inputs):
    import numpy as _np
    import concourse.bacc as _bacc
    from concourse import mybir as _mybir
    from concourse.bass_utils import run_bass_kernel_spmd as _run

    a = {n: _np.ascontiguousarray(v) for n, v in inputs.items()}
    B, H, W, C = a["x"].shape
    T, TP, E = H // 2, 2 * W, a["L0_ffn_w1"].shape[0]
    p, t, tap = _np.arange(TP)[:, None, None], _np.arange(T)[None, :, None], _np.arange(9)[None, None, :]
    grid = _np.zeros((TP, T, 18), _np.float32)
    grid[:, :, 0::2] = 2 * t + p // W + tap // 3
    grid[:, :, 1::2] = p % W + tap % 3
    pick = _np.zeros((2 * E, E, C), _np.float32)
    for e in range(E):
        pick[e, e, :] = pick[E + e, e, :] = 1
    low = 2.0 ** _np.arange(30, -1, -2)[:, None]
    tries, adds = low * _np.array([1.0, 2.0, 3.0]), low * _np.ones(3)
    tries[0], adds[0] = low[0], low[0] * _np.array([1.0, 0.0, 0.0])
    arrays = {
        "x": a["x"], "conv_w": a["L0_conv_W"], "gate_w": a["L0_ffn_gate_w"], "gate_b": a["L0_ffn_gate_b"].reshape(1, -1),
        "w1": a["L0_ffn_w1"], "w2": a["L0_ffn_w2"], "w3": a["L0_ffn_w3"],
        "off_w": a["L1_conv_offset_w"].reshape(9 * C, 27), "off_b": a["L1_conv_offset_b"].reshape(27, 1),
        "dcn_w": _np.ascontiguousarray(a["L1_conv_dcn_weight"].transpose(2, 3, 1, 0)).reshape(9 * C, C),
        "wr": a["L1_ffn_wr"], "br": a["L1_ffn_br"].reshape(1, 1), "f1": a["L1_ffn_w1"], "fb1": a["L1_ffn_b1"].reshape(-1, 1),
        "f2": a["L1_ffn_w2"], "fb2": a["L1_ffn_b2"].reshape(1, -1),
        "ident_in": _np.eye(128, dtype=_np.float32), "grid_in": grid,
        "rank_in": _np.tile(_np.arange(E, 0, -1, dtype=_np.float32), (TP, 1)), "pick_in": pick.reshape(2 * E, E * C),
        "tri_in": _np.triu(_np.ones((TP, TP), _np.float32), 1),
        "bits_in": _np.tile(_np.concatenate([tries.ravel(), adds.ravel()]).astype(_np.float32), (TP, 1)),
    }
    nc = _bacc.Bacc("TRN2", target_bir_lowering=False, num_devices=1)
    args = {n: nc.dram_tensor(n, v.shape, _mybir.dt.from_np(v.dtype), kind="ExternalInput").ap() for n, v in arrays.items()}
    out = nc.dram_tensor("out", (B, H, W, C), _mybir.dt.float32, kind="ExternalOutput").ap()
    metaformer_kernel(nc, **args, out=out)
    r = _run(nc, [arrays], core_ids=[0])
    return r.results[0]["out"]
```
